# Optimizing a Trainium2 kernel written in Bass

```python
import numpy as np
import jax
import jax.numpy as jnp

def _softmax(x, axis=-1):
    return jax.nn.softmax(x, axis=axis)

def _gelu(x):
    return jax.nn.gelu(x, approximate=True)

def _silu(x):
    return jax.nn.silu(x)

def _sigmoid(x):
    return jax.nn.sigmoid(x)

def _layernorm(x, axis=-1, eps=1e-05):
    m = jnp.mean(x, axis=axis, keepdims=True)
    v = jnp.var(x, axis=axis, keepdims=True)
    return (x - m) / jnp.sqrt(v + eps)

def _scatter_add(tgt, idx, src, axis=0):
    return tgt.at[idx].add(src)

def _segment_sum(src, seg, n):
    return jax.ops.segment_sum(src, seg, n)
kernel_name = 'mk_prb_d2_jaxref_r8_fef1eb'

def setup_inputs(seed: int=0):
    np.random.seed(seed)
    _w = jnp.asarray

    def _L0_attn_setup():
        import jax, jax.numpy as jnp
        import numpy as np
        B, L, H, N = (4, 512, 128, 64)
        LN_EPS = 1e-05

        def _s4d_kernel(log_A_real, A_imag, C_re, C_im, log_dt, length):
            A = -jnp.exp(log_A_real) + 1j * A_imag
            dt = jnp.exp(log_dt)[:, None]
            dtA = dt * A
            C = C_re + 1j * C_im
            Ct = C * (jnp.exp(dtA) - 1.0) / A
            l = jnp.arange(length, dtype=jnp.float32)
            V = jnp.exp(dtA[:, :, None] * l[None, None, :])
            K = 2.0 * jnp.real(jnp.einsum('hn,hnl->hl', Ct, V))
            return K
        key = jax.random.key(seed)
        ks = jax.random.split(key, 6)
        x = jax.random.normal(ks[0], (B, L, H), dtype=jnp.float32)
        log_A_real = jnp.log(0.5 * jnp.ones((H, N), dtype=jnp.float32))
        A_imag = jnp.broadcast_to(jnp.pi * jnp.arange(N, dtype=jnp.float32), (H, N))
        C_re = jax.random.normal(ks[1], (H, N), dtype=jnp.float32) * 0.5
        C_im = jax.random.normal(ks[2], (H, N), dtype=jnp.float32) * 0.5
        u = jax.random.uniform(ks[3], (H,), dtype=jnp.float32)
        log_dt = u * (jnp.log(0.1) - jnp.log(0.001)) + jnp.log(0.001)
        D = jax.random.normal(ks[4], (H,), dtype=jnp.float32)
        ln_w = jnp.ones((H,), dtype=jnp.float32)
        ln_b = jnp.zeros((H,), dtype=jnp.float32)
        return {'x': x, 'log_A_real': log_A_real, 'A_imag': A_imag, 'C_re': C_re, 'C_im': C_im, 'log_dt': log_dt, 'D': D, 'ln_w': ln_w, 'ln_b': ln_b}
    _L0_attn_in = _L0_attn_setup()

    def _L0_ffn_setup():
        import jax, jax.numpy as jnp
        import numpy as np
        EMB_DIM = 128
        HIDDEN = int(2 / 3 * 4 * EMB_DIM)
        NUM_EXPERTS = 8
        TOP_K = 2
        B, S = (4, 128)
        key = jax.random.key(seed)
        ks = jax.random.split(key, 5)
        sc = 1.0 / np.sqrt(EMB_DIM)
        sh = 1.0 / np.sqrt(HIDDEN)
        return {'x': jax.random.normal(ks[0], (B, S, EMB_DIM), dtype=jnp.float32), 'Wg': jax.random.normal(ks[1], (NUM_EXPERTS, EMB_DIM), dtype=jnp.float32) * sc, 'W1': jax.random.normal(ks[2], (NUM_EXPERTS, HIDDEN, EMB_DIM), dtype=jnp.float32) * sc, 'W2': jax.random.normal(ks[3], (NUM_EXPERTS, HIDDEN, EMB_DIM), dtype=jnp.float32) * sc, 'W3': jax.random.normal(ks[4], (NUM_EXPERTS, EMB_DIM, HIDDEN), dtype=jnp.float32) * sh}
    _L0_ffn_in = _L0_ffn_setup()

    def _L1_attn_setup():
        import jax, jax.numpy as jnp
        import numpy as np
        OUT_DIM = 128
        key = jax.random.key(seed)
        k1, k2, k3, k4 = jax.random.split(key, 4)
        B, N, D = (4, 256, 128)
        s = 1.0 / np.sqrt(D)
        return {'x': jax.random.normal(k1, (B, N, D), dtype=jnp.float32), 'W_query': jax.random.normal(k2, (D, OUT_DIM), dtype=jnp.float32) * s, 'W_key': jax.random.normal(k3, (D, OUT_DIM), dtype=jnp.float32) * s, 'W_value': jax.random.normal(k4, (D, OUT_DIM), dtype=jnp.float32) * s}
    _L1_attn_in = _L1_attn_setup()

    def _L1_ffn_setup():
        import jax, jax.numpy as jnp
        import numpy as np
        MAX_THRESHOLD = 0.125
        key = jax.random.key(seed)
        ks = jax.random.split(key, 5)
        B, S, D, FF, E = (2, 256, 128, 512, 8)
        sd = 1.0 / np.sqrt(D)
        sf = 1.0 / np.sqrt(FF)
        return {'inputs': jax.random.normal(ks[0], (B, S, D), dtype=jnp.float32), 'Wg': jax.random.normal(ks[1], (D, E), dtype=jnp.float32) * sd, 'bg': jnp.zeros((E,), dtype=jnp.float32), 'Wt': jax.random.normal(ks[2], (D, 1), dtype=jnp.float32) * sd, 'bt': jnp.zeros((1,), dtype=jnp.float32), 'W1': jax.random.normal(ks[3], (E, D, FF), dtype=jnp.float32) * sd, 'b1': jnp.zeros((E, FF), dtype=jnp.float32), 'W2': jax.random.normal(ks[4], (E, FF, D), dtype=jnp.float32) * sf, 'b2': jnp.zeros((E, D), dtype=jnp.float32)}
    _L1_ffn_in = _L1_ffn_setup()
    _d = {'L0_attn_x': _L0_attn_in['x'], 'L0_attn_log_A_real': _L0_attn_in['log_A_real'], 'L0_attn_A_imag': _L0_attn_in['A_imag'], 'L0_attn_C_re': _L0_attn_in['C_re'], 'L0_attn_C_im': _L0_attn_in['C_im'], 'L0_attn_log_dt': _L0_attn_in['log_dt'], 'L0_attn_D': _L0_attn_in['D'], 'L0_attn_ln_w': _L0_attn_in['ln_w'], 'L0_attn_ln_b': _L0_attn_in['ln_b'], 'L0_ffn_Wg': _L0_ffn_in['Wg'], 'L0_ffn_W1': _L0_ffn_in['W1'], 'L0_ffn_W2': _L0_ffn_in['W2'], 'L0_ffn_W3': _L0_ffn_in['W3'], 'L1_attn_W_query': _L1_attn_in['W_query'], 'L1_attn_W_key': _L1_attn_in['W_key'], 'L1_attn_W_value': _L1_attn_in['W_value'], 'L1_ffn_Wg': _L1_ffn_in['Wg'], 'L1_ffn_bg': _L1_ffn_in['bg'], 'L1_ffn_Wt': _L1_ffn_in['Wt'], 'L1_ffn_bt': _L1_ffn_in['bt'], 'L1_ffn_W1': _L1_ffn_in['W1'], 'L1_ffn_b1': _L1_ffn_in['b1'], 'L1_ffn_W2': _L1_ffn_in['W2'], 'L1_ffn_b2': _L1_ffn_in['b2']}
    _x0 = _d['L0_attn_x']
    _d['L0_attn_x'] = jax.random.normal(jax.random.fold_in(jax.random.key(seed), 1), (4, 1024, 128), dtype=_x0.dtype)
    del _x0
    return _d

def reference(L0_attn_x, L0_attn_log_A_real, L0_attn_A_imag, L0_attn_C_re, L0_attn_C_im, L0_attn_log_dt, L0_attn_D, L0_attn_ln_w, L0_attn_ln_b, L0_ffn_Wg, L0_ffn_W1, L0_ffn_W2, L0_ffn_W3, L1_attn_W_query, L1_attn_W_key, L1_attn_W_value, L1_ffn_Wg, L1_ffn_bg, L1_ffn_Wt, L1_ffn_bt, L1_ffn_W1, L1_ffn_b1, L1_ffn_W2, L1_ffn_b2):

    def _L0_attn_ref(x, log_A_real, A_imag, C_re, C_im, log_dt, D, ln_w, ln_b):
        import jax, jax.numpy as jnp
        import numpy as np
        B, L, H, N = (4, 512, 128, 64)
        LN_EPS = 1e-05

        def _s4d_kernel(log_A_real, A_imag, C_re, C_im, log_dt, length):
            A = -jnp.exp(log_A_real) + 1j * A_imag
            dt = jnp.exp(log_dt)[:, None]
            dtA = dt * A
            C = C_re + 1j * C_im
            Ct = C * (jnp.exp(dtA) - 1.0) / A
            l = jnp.arange(length, dtype=jnp.float32)
            V = jnp.exp(dtA[:, :, None] * l[None, None, :])
            K = 2.0 * jnp.real(jnp.einsum('hn,hnl->hl', Ct, V))
            return K
        b, length, h = x.shape
        K = _s4d_kernel(log_A_real, A_imag, C_re, C_im, log_dt, length)
        n = 2 * length
        Xf = jnp.fft.rfft(x, n=n, axis=1)
        Kf = jnp.fft.rfft(K, n=n, axis=1)
        y = jnp.fft.irfft(Xf * Kf.T[None, :, :], n=n, axis=1)[:, :length, :]
        z = y + x * D[None, None, :]
        r = x + z
        mu = jnp.mean(r, axis=-1, keepdims=True)
        var = jnp.var(r, axis=-1, keepdims=True)
        out = (r - mu) * jax.lax.rsqrt(var + LN_EPS) * ln_w + ln_b
        return out

    def _L0_ffn_ref(x, Wg, W1, W2, W3):
        import jax, jax.numpy as jnp
        import numpy as np
        EMB_DIM = 128
        HIDDEN = int(2 / 3 * 4 * EMB_DIM)
        NUM_EXPERTS = 8
        TOP_K = 2
        B, S = (4, 128)
        gate_logits = jnp.einsum('bsd,ed->bse', x, Wg)
        top_v, top_i = jax.lax.top_k(gate_logits, TOP_K)
        mask = jnp.any(top_i[..., :, None] == jnp.arange(NUM_EXPERTS), axis=-2)
        sparse_logits = jnp.where(mask, gate_logits, -jnp.inf)
        gating = jax.nn.softmax(sparse_logits, axis=-1)
        h1 = jnp.einsum('bsd,ehd->bseh', x, W1)
        h2 = jnp.einsum('bsd,ehd->bseh', x, W2)
        hidden = jax.nn.silu(h1) * h2
        expert_out = jnp.einsum('bseh,edh->bsed', hidden, W3)
        return jnp.einsum('bsed,bse->bsd', expert_out, gating)

    def _L1_attn_ref(x, W_query, W_key, W_value):
        import jax, jax.numpy as jnp
        import numpy as np
        OUT_DIM = 128
        q = jnp.einsum('bnd,de->bne', x, W_query)
        k = jnp.einsum('bnd,de->bne', x, W_key)
        v = jnp.einsum('bnd,de->bne', x, W_value)
        sqrt_d = jnp.sqrt(jnp.asarray(OUT_DIM, dtype=jnp.float32))
        scores = jnp.einsum('bie,bje->bij', q, k) / sqrt_d
        attn = jax.nn.softmax(scores, axis=1)
        return jnp.einsum('bij,bie->bje', attn, v)

    def _L1_ffn_ref(inputs, Wg, bg, Wt, bt, W1, b1, W2, b2):
        import jax, jax.numpy as jnp
        import numpy as np
        MAX_THRESHOLD = 0.125
        x = inputs.reshape(-1, inputs.shape[-1])
        gate = jax.nn.softmax(x @ Wg + bg, axis=-1)
        thr = jax.nn.sigmoid(x @ Wt + bt) * MAX_THRESHOLD
        adapted = gate - thr
        mask = (adapted >= 0).astype(x.dtype)
        w = adapted * mask
        s = jnp.sum(w, axis=-1, keepdims=True)
        s = jnp.where(s == 0, jnp.ones_like(s), s)
        w = w / s
        h = jax.nn.gelu(jnp.einsum('td,edf->etf', x, W1) + b1[:, None, :])
        eo = jnp.einsum('etf,efd->etd', h, W2) + b2[:, None, :]
        out = jnp.einsum('te,etd->td', w, eo)
        return out.reshape(inputs.shape)
    x = L0_attn_x
    xn = _layernorm(x, axis=-1)
    x = x + _L0_attn_ref(xn, L0_attn_log_A_real, L0_attn_A_imag, L0_attn_C_re, L0_attn_C_im, L0_attn_log_dt, L0_attn_D, L0_attn_ln_w, L0_attn_ln_b) + _L0_ffn_ref(xn, L0_ffn_Wg, L0_ffn_W1, L0_ffn_W2, L0_ffn_W3)
    xn = _layernorm(x, axis=-1)
    x = x + _L1_attn_ref(xn, L1_attn_W_query, L1_attn_W_key, L1_attn_W_value) + _L1_ffn_ref(xn, L1_ffn_Wg, L1_ffn_bg, L1_ffn_Wt, L1_ffn_bt, L1_ffn_W1, L1_ffn_b1, L1_ffn_W2, L1_ffn_b2)
    return x

_drawn_inputs = setup_inputs


def setup_inputs(seed=0):
    import zlib

    import numpy as np

    out = dict(_drawn_inputs(seed))
    spreads = {'L0_attn_log_A_real': (-0.6931471824645996, 0.6),
     'L0_attn_ln_w': (1.0, 0.2),
     'L0_attn_ln_b': (0.0, 0.1),
     'L1_ffn_bg': (0.0, 0.365),
     'L1_ffn_b1': (0.0, 0.372),
     'L1_ffn_b2': (0.0, 0.1)}
    factors = {}
    for name, (base, spread) in spreads.items():
        noise = np.random.default_rng([zlib.crc32(name.encode()), seed]).standard_normal(out[name].shape)
        drawn = base * np.exp(spread * noise) if base else spread * noise
        out[name] = jnp.asarray(drawn.astype(out[name].dtype))
    for name, factor in factors.items():
        out[name] = (out[name] * factor).astype(out[name].dtype)
    return out
```

```python
import math
from contextlib import ExitStack

import numpy as np
import concourse.bass as bass
from concourse import mybir

F32 = mybir.dt.float32
F32R = mybir.dt.float32r
ALU = mybir.AluOpType
ACT = mybir.ActivationFunctionType
AX = mybir.AxisListType

B, L, H = 4, 1024, 128
N = 64
P = 128
G = L // P
W = B * P
E = 8
HID0 = 341
J0 = -(-HID0 // P)
HID1 = 512
J1 = HID1 // P
LN_EPS = 1e-5
THRESHOLD = 0.125
UN = E * J0
GW = 10
UN1 = E * J1
QKV, GATE1 = 2 * E * HID1, 2 * E * HID1 + 3 * P
SCALE = float(1.0 / np.sqrt(np.float32(H)))
CHUNK_STEPS = 13
LO = 32
LAGS = 2 * LO
HH = H // 2
CH = HH // G
C = 512
CT = C // P
M = C // P
MAGIC = 1.5 * 2.0 ** 23
MAGIC_13 = 1.5 * 2.0 ** 10
TWO_PI = 6.283185
INV_2PI = 1.0 / (2.0 * math.pi)
INV_2PI_HI = float(np.round(INV_2PI * 2 ** 14) / 2 ** 14)
INV_2PI_LO = INV_2PI - INV_2PI_HI
LN2_HI = 355.0 / 512.0
LN2_LO = math.log(2.0) - LN2_HI


class Tally:

    def __init__(self, sem):
        self.sem, self.base, self.n = sem, 0, 0

    def mark(self, instruction):
        instruction.then_inc(self.sem, 1)
        self.n += 1
        return self.base + self.n

    def enter(self, start, index, per_turn):
        self.base, self.n, self.per_turn, self.start = start + index * per_turn, 0, per_turn, start

    def leave(self, turns):
        assert self.n == self.per_turn, (self.n, self.per_turn)
        self.base, self.n = self.start + turns * self.per_turn, 0


def program(nc, x, state_params, log_dt, skip, ln_w, ln_b, wg0, w1_0, w2_0, w3_0, lag_row,
            dft_fwd, dft_inv, wqkv, wg1, gate_bias, w1_1, b1, w2_1, b2, out):
    ctx = ExitStack()
    with ctx:
        def sb(name, shape, dt=F32):
            return ctx.enter_context(nc.sbuf_tensor(name, shape, dt))

        def sem(name):
            return ctx.enter_context(nc.semaphore(name))

        kernel_dram = nc.dram_tensor("kernel_dram", (H, LO, LO), F32).ap()
        gates_dram = nc.dram_tensor("gates_dram", (2, G * B, E, P), F32).ap()

        WCOLS = 2 * E * HID1 + 3 * P + GW + 6
        w_hi = sb("w_hi", [P, WCOLS], F32R)
        w_lo = sb("w_lo", [P, WCOLS], F32R)
        xn = sb("xn", [P, G, W])
        acc = sb("acc", [P, G, W])
        ident = sb("ident", [P, P])
        stats = sb("stats", [P, 2 * B, 6])
        mv = sb("mv", [P, G * B, 2])
        rstd = sb("rstd", [P, G * B])
        newton = sb("newton", [P, G * B])
        eps = sb("eps", [P, 1])
        consts = sb("consts", [P, LAGS + E])
        lagv = consts[:, 0:LAGS]
        rev = consts[:, LAGS:LAGS + E]
        gates = sb("gates", [P, G * B, E])
        gates_t = sb("gates_t", [P, 2, P])

        vec_rows = sb("vec_rows", [P, 3, P])
        bias1 = sb("bias1", [P, GW])
        gl = sb("gl", [P, G * B, GW])
        gs = sb("gs", [P, 2, G * B])
        b1_sb = sb("b1_sb", [P, E * J1])
        b2_sb = sb("b2_sb", [P, E])
        mid = sb("mid", [P, 6, 2 * B])
        mid_mv = sb("mid_mv", [P, 2, B, 2])

        phase = ExitStack()

        def tmp(name, shape, dt=F32):
            return phase.enter_context(nc.sbuf_tensor(name, shape, dt))

        xt_hi = tmp("xt_hi", [P, G, W], F32R)
        xt_lo = tmp("xt_lo", [P, G, W], F32R)
        gate_row = tmp("gate_row", [P, 4, W])
        wst = tmp("wst", [P, 2, 2 * W])
        act, part = wst[:, 0].rearrange("p (a w) -> p a w", a=2), wst[:, 1].rearrange("p (a w) -> p a w", a=2)
        hid = tmp("hid", [P, 3, W])
        hid_hi = tmp("hid_hi", [P, 3, W], F32R)
        hid_lo = tmp("hid_lo", [P, 3, W], F32R)
        wg0_sb = tmp("wg0_sb", [P, E])
        wg0_hi = tmp("wg0_hi", [P, E], F32R)
        wg0_lo = tmp("wg0_lo", [P, E], F32R)
        small = tmp("small", [P, 4, HH])
        ks = tmp("ks", [P, 24, HH])
        exp2 = tmp("exp2", [P, 2 * HH], mybir.dt.int32)
        th_hi = tmp("th_hi", [P, HH], F32R)
        kc = tmp("kc", [P, 9, CH, LAGS])
        kg = tmp("kg", [P, 4, CH, LO])
        k_out = tmp("k_out", [LO, 2, CH, LO])
        tk = kc[:, 0:4].rearrange("p a b c -> p (a b c)")

        phase.close()

        phase = ExitStack()
        fwd = tmp("fwd", [P, CT, 2, C])
        prod = tmp("prod", [P, 8, W])
        inv = tmp("inv", [P, M, 2, C])
        z = tmp("z", [P, M, 2, 2, W])
        khat = tmp("khat", [P, M, 4, P])
        wst1 = tmp("wst1", [P, 2, 512])
        xs = tmp("xs", [P, 2, W])
        xn1 = tmp("xn1", [P, 2, W])
        k_nat = z[:, 3, 0].rearrange("p a b -> p (a b)")
        k_t = z[:, 2, 0].rearrange("p a b -> p (a b)").rearrange("p (t h) -> p t h", h=P)
        phase.close()

        phase = ExitStack()
        xt1_hi = tmp("xt1_hi", [P, G, W], F32R)
        xt1_lo = tmp("xt1_lo", [P, G, W], F32R)
        attention = phase
        phase = ExitStack()
        qk_hi = tmp("qk_hi", [P, 2, L], F32R)
        qk_lo = tmp("qk_lo", [P, 2, L], F32R)
        v_hi = tmp("v_hi", [P, G, P], F32R)
        v_lo = tmp("v_lo", [P, G, P], F32R)
        prob = tmp("prob", [P, 2, L])
        pt_hi = tmp("pt_hi", [P, G, C], F32R)
        pt_lo = tmp("pt_lo", [P, G, C], F32R)
        sm = tmp("sm", [P, 2, 4])
        phase.close()

        phase = ExitStack()
        hid1 = tmp("hid1", [P, 4, W])
        hid1_hi = tmp("hid1_hi", [P, 4, W], F32R)
        hid1_lo = tmp("hid1_lo", [P, 4, W], F32R)
        gate_row1 = tmp("gate_row1", [P, 4, W])
        part1 = tmp("part1", [P, 2, W])
        final = tmp("final", [P, 2, W])
        phase.close()
        attention.close()

        T = G * B
        lg, eq, k2, oh1, oh2 = (tk[:, i * T * E:(i + 1) * T * E].rearrange("p (t e) -> p t e", e=E) for i in range(5))
        m1, p1, m2, p2 = (tk[:, 5 * T * E + i * T:5 * T * E + (i + 1) * T] for i in range(4))
        ps = ctx.enter_context(nc.psum_tensor("ps", [P, 8, W], F32))

        x_in = sem("x_in")
        small_in = sem("small_in")
        wst_in = [sem(f"wst_in{i}") for i in range(2)]
        stats_done = sem("stats_done")
        wg0_done = sem("wg0_done")
        top2_done = sem("top2_done")
        gates_done = sem("gates_done")
        w_hi_done = sem("w_hi_done")
        w_lo_done = sem("w_lo_done")
        ident_done = sem("ident_done")
        pool_step = sem("pool_step")
        dve_step = sem("dve_step")
        trig_done = sem("trig_done")
        wg0_hi_done = sem("wg0_hi_done")
        root_done = sem("root_done")
        top2_exp_done = sem("top2_exp_done")
        xn_ready = sem("xn_ready")
        xt_done = sem("xt_done")
        xt_hi_done = sem("xt_hi_done")
        xt_lo_done = sem("xt_lo_done")
        logits_done = sem("logits_done")
        gates_turned = sem("gates_turned")
        gates_out = sem("gates_out")
        gate_in = [sem(f"gate_in{i}") for i in range(4)]
        up_done = sem("up_done")
        act_done = sem("act_done")
        hid_done = sem("hid_done")
        hid_lo_done = sem("hid_lo_done")
        expert_done = sem("expert_done")
        part_done = sem("part_done")
        acc_done = sem("acc_done")
        decay_done = sem("decay_done")
        phase_done = sem("phase_done")
        exp_done = sem("exp_done")
        sin_done = sem("sin_done")
        tables_done = sem("tables_done")
        k_mm_done = sem("k_mm_done")
        k_copied = sem("k_copied")
        k_stored = sem("k_stored")

        kernel_in = sem("kernel_in")
        fwd_in = sem("fwd_in")
        inv_in = sem("inv_in")
        rows_in = sem("rows_in")
        xs_in0 = sem("xs_in0")
        xs_in1 = sem("xs_in1")
        k_t_done = sem("k_t_done")
        k_t_copied = sem("k_t_copied")
        khat_mm = sem("khat_mm")
        khat_copied = sem("khat_copied")
        khat_ready = sem("khat_ready")
        x_hat_done = sem("x_hat_done")
        products_done = sem("products_done")
        z_ready = sem("z_ready")
        w1_free = sem("w1_free")
        wst1_in0 = sem("wst1_in0")
        wst1_in1 = sem("wst1_in1")
        w1_hi_done = sem("w1_hi_done")
        w1_lo_done = sem("w1_lo_done")
        skip_done = sem("skip_done")
        y_done = sem("y_done")
        r_done = sem("r_done")
        mid_stats = sem("mid_stats")
        root1_done = sem("root1_done")
        norm1_done = sem("norm1_done")
        scaled_done = sem("scaled_done")
        xb_done = sem("xb_done")
        ffn_turned = sem("ffn_turned")
        x1_done = sem("x1_done")
        mid_stats2 = sem("mid_stats2")
        root2_done = sem("root2_done")
        xn1_done = sem("xn1_done")
        xt1_done = sem("xt1_done")
        xt1_hi_done = sem("xt1_hi_done")
        xt1_lo_done = sem("xt1_lo_done")
        logits1_done = sem("logits1_done")
        logits1_read = sem("logits1_read")
        gate_exp_done = sem("gate_exp_done")
        gate_soft = sem("gate_soft")
        gates1_done = sem("gates1_done")
        gates1_turned = sem("gates1_turned")
        gates1_copied = sem("gates1_copied")
        qkv_mm = sem("qkv_mm")
        qkv_hi_done = sem("qkv_hi_done")
        qkv_lo_done = sem("qkv_lo_done")
        s_done = sem("s_done")
        max_done = sem("max_done")
        exp1_done = sem("exp1_done")
        prob_done = sem("prob_done")
        pt_done = sem("pt_done")
        pt_hi_done = sem("pt_hi_done")
        pt_lo_done = sem("pt_lo_done")
        pv_done = sem("pv_done")
        pv_copied = sem("pv_copied")
        up1_done = sem("up1_done")
        hid1_done = sem("hid1_done")
        hid1_lo_done = sem("hid1_lo_done")
        expert1_done = sem("expert1_done")
        part1_done = sem("part1_done")
        join1_done = sem("join1_done")
        gate1_in0 = sem("gate1_in0")
        gate1_in1 = sem("gate1_in1")
        gate1_in2 = sem("gate1_in2")
        gate1_in3 = sem("gate1_in3")
        final_done = sem("final_done")
        added_done = sem("added_done")
        stored = [sem(f"stored{n}") for n in range(2)]
        row_step = sem("row_step")
        gate1_in = [gate1_in0, gate1_in1, gate1_in2, gate1_in3]
        xs_in = [xs_in0, xs_in1]
        wst1_in = [wst1_in0, wst1_in1]

        block = ctx.enter_context(nc.Block())

        W2C, W3C = E * HID0, 2 * E * HID0
        HALF = 2 * HID0
        pieces0 = []
        for n in range(E // 2):
            pieces0.append((w1_0[:, n * HALF:(n + 1) * HALF], n * HALF, P, HALF))
            pieces0.append((w2_0[:, n * HALF:(n + 1) * HALF], W2C + n * HALF, P, HALF))
            if n == 0:
                for j in range(J0):
                    f = min(P, HID0 - j * P)
                    pieces0.append((w3_0[:, j * P:j * P + f, :].rearrange("e f d -> f e d"),
                                    W3C + j * E * P, f, E * P))

        pieces1 = [(wqkv, lambda a: a.rearrange("p (k e) -> p k e", k=3), QKV, 3 * P), (wg1, lambda a: a, GATE1, GW)]
        for e in range(E):
            pieces1.append((w1_1[e], lambda a: a, e * HID1, HID1))
            pieces1.append((w2_1[e].rearrange("(j f) d -> f j d", j=J1), lambda a: a.rearrange("p (j d) -> p j d", j=J1),
                            E * HID1 + e * HID1, HID1))

        def qkv_dst(qk, v, i):
            return qk[:, i // 2, (i % 2) * C:(i % 2 + 1) * C] if i < 4 else v[:, 4 * (i - 4):4 * (i - 3)]

        def turned_dst(pt, n, a):
            return pt[:, 4 * a:4 * a + 4, (n % 4) * P:(n % 4 + 1) * P]

        def turned_src(a):
            return ps[:, 4 + a].rearrange("p (t j) -> p t j", t=4)

        def qkv_src(n):
            bank = ps[:, 6 + n % 2]
            return bank if n % 6 < 4 else bank.rearrange("p (t e) -> p t e", t=4)

        def w3_col(e, j):
            return W3C + (j * E + e) * P

        @block.sync
        def _(sp):
            sp.sem_inc(k_stored, 32)
            sp.dma_start(small[:], state_params).then_inc(small_in, 16)
            for half in range(2):
                sp.dma_start(ks[half * N:(half + 1) * N, 0, :],
                             log_dt[half * HH:(half + 1) * HH].partition_broadcast(N)).then_inc(small_in, 16)
            sp.dma_start(consts[:], lag_row.partition_broadcast(P)).then_inc(small_in, 16)
            sp.dma_start(wg0_sb[:], wg0).then_inc(small_in, 16)
            for g in range(G):
                sp.dma_start(xn[:, g, :].rearrange("p (b h) -> p b h", b=B),
                             x[:, g * P:(g + 1) * P, :].rearrange("b p h -> p b h")).then_inc(x_in, 16)
            for n, (src, col, rows, cols) in enumerate(pieces0):
                if n >= 2:
                    sp.wait_ge(w_lo_done, n - 1)
                dst = wst[0:rows, n % 2, 0:cols]
                if len(src.shape) == 3:
                    dst = dst.rearrange("p (e d) -> p e d", e=E)
                sp.dma_start(dst, src).then_inc(wst_in[n % 2], 16)
            sp.wait_ge(gates_turned, 1)
            sp.dma_start(gates_dram[0].rearrange("(a t) e p -> (t e) a p", a=2), gates_t[:]).then_inc(gates_out, 16)
            sp.wait_ge(gates_out, 16)

            def gate_load(g, e):
                src = gates_dram[0, bass.ds(g * B, B), e, :].partition_broadcast(P)
                sp.dma_start(gate_row[:, e % 4, :].rearrange("p (b t) -> p b t", b=B), src).then_inc(gate_in[e % 4], 16)

            for e in range(4):
                gate_load(0, e)

            def expert_loads(g, last):
                for e in range(E):
                    if e == 4:
                        sp.wait_ge(k_copied, 2 * g + 2)
                        for half in range(2):
                            sp.dma_start(kernel_dram[bass.ds(half * HH + g * CH, CH)].rearrange("j m n -> m j n"),
                                         k_out[:, half]).then_inc(k_stored, 16)
                    sp.wait_ge(part_done, g * E + e + 1)
                    if not (last and e >= 4):
                        if e < 4:
                            gate_load(g, e + 4)
                        else:
                            gate_load(g + 1, e - 4)

            with sp.Fori(0, G - 1) as g:
                expert_loads(g, False)
            expert_loads(G - 1, True)
            sp.wait_ge(k_stored, 32 * G + 32)
            sp.wait_ge(acc_done, G * (E - 1))
            sp.dma_start(k_nat, kernel_dram.rearrange("h m n -> h (m n)")).then_inc(kernel_in, 16)
            sp.dma_start(fwd[:], dft_fwd).then_inc(fwd_in, 16)
            sp.dma_start(vec_rows[:, 0], skip.partition_broadcast(P)).then_inc(rows_in, 16)
            sp.dma_start(vec_rows[:, 1], ln_w.partition_broadcast(P)).then_inc(rows_in, 16)
            sp.dma_start(vec_rows[:, 2], ln_b.partition_broadcast(P)).then_inc(rows_in, 16)
            sp.dma_start(bias1[:], gate_bias.partition_broadcast(P)).then_inc(rows_in, 16)
            sp.dma_start(b1_sb[:], b1).then_inc(rows_in, 16)
            sp.dma_start(b2_sb[:], b2).then_inc(rows_in, 16)
            sp.dma_start(inv[:], dft_inv).then_inc(inv_in, 16)
            for n, (src, view, col, cols) in enumerate(pieces1):
                if n >= 2:
                    sp.wait_ge(w1_lo_done, n - 1)
                sp.dma_start(view(wst1[:, n % 2, 0:cols]), src).then_inc(wst1_in[n % 2], 16)
            for g in range(G):
                if g >= 2:
                    sp.wait_ge(x1_done, g - 1)
                sp.dma_start(xs[:, g % 2].rearrange("p (b h) -> p b h", b=B),
                             x[:, g * P:(g + 1) * P, :].rearrange("b p h -> p b h")).then_inc(xs_in[g % 2], 16)
            sp.wait_ge(gates1_copied, 1)
            sp.dma_start(gates_dram[1].rearrange("(a t) e p -> (t e) a p", a=2), gates_t[:]).then_inc(gates_out, 16)
            sp.wait_ge(gates_out, 32)
            sp.wait_ge(up1_done, 1)
            sp.wait_ge(pv_copied, 2 * B)

            def gate1_load(g, e):
                src = gates_dram[1, bass.ds(g * B, B), e, :].partition_broadcast(P)
                sp.dma_start(gate_row1[:, e % 4, :].rearrange("p (b t) -> p b t", b=B), src).then_inc(gate1_in[e % 4], 16)

            for e in range(4):
                gate1_load(0, e)

            def gate1_loads(g, last):
                for e in range(E):
                    sp.wait_ge(part1_done, g * E + e + 1)
                    if e < 4:
                        gate1_load(g, e + 4)
                    elif not last:
                        gate1_load(g + 1, e - 4)
                    if last and e < G - 1:
                        store(e)

            def store(g):
                sp.wait_ge(added_done, g + 1)
                sp.dma_start(out[:, g * P:(g + 1) * P, :].rearrange("b p h -> p b h"),
                             final[:, g % 2].rearrange("p (b h) -> p b h", b=B)).then_inc(stored[g % 2], 16)

            with sp.Fori(0, G - 1) as g:
                gate1_loads(g, False)
            gate1_loads(G - 1, True)
            store(G - 1)
            for n in range(2):
                sp.wait_ge(stored[n], 16 * G // 2)

        @block.gpsimd
        def _(pool):
            nc.gpsimd.memset(ident[:], 0.0).then_inc(pool_step, 1)
            pool.wait_ge(pool_step, 1)
            nc.gpsimd.affine_select(out=ident[:], in_=ident[:], compare_op=ALU.not_equal, fill=1.0, base=0,
                                    pattern=[[-1, P]], channel_multiplier=1).then_inc(ident_done, 1)
            for n, (_, col, rows, cols) in enumerate(pieces0):
                pool.wait_ge(w_hi_done, n + 1)
                nc.gpsimd.tensor_tensor(w_lo[0:rows, col:col + cols], wst[0:rows, n % 2, 0:cols],
                                        w_hi[0:rows, col:col + cols].bitcast(F32), ALU.subtract).then_inc(w_lo_done, 1)
            def low_parts(g, first=False):
                for u in range(UN):
                    e, j = divmod(u, J0)
                    f = min(P, HID0 - j * P)
                    joins = j == J0 - 1 and e != 1 and not (first and e == 0)
                    if joins:
                        to, ex = (g, e - 1) if e else (g - 1, E - 1)
                        if ex >= 2:
                            pool.wait_ge(acc_done, to * (E - 1) + ex - 1)
                        pool.wait_ge(part_done, g * E + e)
                    pool.wait_ge(hid_done, g * UN + u + 1)
                    nc.gpsimd.tensor_tensor(hid_lo[0:f, u % 3], hid[0:f, u % 3], hid_hi[0:f, u % 3].bitcast(F32),
                                            ALU.subtract).then_inc(hid_lo_done, 1)
                    if joins:
                        join(to, ex)

            def join(g, e):
                a = acc[:, bass.ds(g, 1), :].rearrange("p a w -> p (a w)")
                nc.gpsimd.tensor_tensor(a, a, part[:, e % 2], ALU.add).then_inc(acc_done, 1)

            low_parts(0, first=True)
            with pool.Fori(1, G) as g:
                low_parts(g)
            pool.wait_ge(acc_done, G * (E - 1) - 1)
            pool.wait_ge(part_done, G * E)
            join(G - 1, E - 1)

            pool.wait_ge(rows_in, 96)
            nc.gpsimd.tensor_scalar(vec_rows[:, 0], vec_rows[:, 0], 1.0, None, ALU.add).then_inc(row_step, 1)
            for n, (_, _, col, cols) in enumerate(pieces1):
                pool.wait_ge(w1_hi_done, n + 1)
                nc.gpsimd.tensor_tensor(w_lo[:, col:col + cols], wst1[:, n % 2, 0:cols],
                                        w_hi[:, col:col + cols].bitcast(F32), ALU.subtract).then_inc(w1_lo_done, 1)
            pool.wait_ge(x_hat_done, M)
            pool.wait_ge(row_step, 1)
            row = lambda i: vec_rows[:, i].unsqueeze(1).broadcast_to((P, B, P))
            for_batch = lambda a: a.rearrange("p (b h) -> p b h", b=B)

            def skip_term(g):
                nc.gpsimd.tensor_tensor(for_batch(xn[:, g]), for_batch(xn[:, g]), row(0), ALU.mult).then_inc(skip_done, 1)

            skip_term(0)
            for g in range(G):
                if g + 1 < G:
                    skip_term(g + 1)
                pool.wait_ge(xs_in[g % 2], 16 * (g // 2 + 1))
                nc.gpsimd.tensor_tensor(for_batch(xs[:, g % 2]), for_batch(xs[:, g % 2]), row(2), ALU.add).then_inc(xb_done, 1)
                pool.wait_ge(norm1_done, g + 1)
                nc.gpsimd.tensor_tensor(for_batch(xn[:, g]), for_batch(xn[:, g]), row(1), ALU.mult).then_inc(scaled_done, 1)

        @block.scalar
        def _(act_e):
            act_e.wait_ge(small_in, 80)
            act_e.wait_ge(decay_done, 1)
            nc.scalar.activation(ks[:, 5], ks[:, 4], ACT.Tanh, scale=0.5).then_inc(trig_done, 1)
            nc.scalar.activation(ks[:, 6], ks[:, 4], ACT.Exp).then_inc(trig_done, 1)
            nc.scalar.activation(wg0_hi[:], wg0_sb[:], ACT.Copy).then_inc(wg0_hi_done, 1)
            act_e.wait_ge(phase_done, 1)
            nc.scalar.activation(ks[:, 7], ks[:, 12], ACT.Sin, scale=TWO_PI).then_inc(trig_done, 1)
            nc.scalar.activation(ks[:, 8], ks[:, 12], ACT.Sin, scale=TWO_PI / 2).then_inc(trig_done, 1)
            act_e.wait_ge(stats_done, 1)
            nc.scalar.activation(rstd[:], mv[:, :, 1], ACT.Sqrt, bias=eps[:]).then_inc(root_done, 1)
            w_next = [0]

            def weights(count):
                for _ in range(count):
                    n = w_next[0]
                    if n == len(pieces0):
                        return
                    _, col, rows, cols = pieces0[n]
                    act_e.wait_ge(wst_in[n % 2], 16 * (n // 2 + 1))
                    nc.scalar.activation(w_hi[0:rows, col:col + cols], wst[0:rows, n % 2, 0:cols],
                                         ACT.Copy).then_inc(w_hi_done, 1)
                    w_next[0] += 1

            for g in range(G):
                weights(1)
                act_e.wait_ge(xt_done, g + 1)
                nc.scalar.activation(xt_hi[:, g], ps[:, g % 2], ACT.Copy).then_inc(xt_hi_done, 1)
            act_e.wait_ge(top2_done, 1)
            nc.scalar.activation(p2, m2, ACT.Exp).then_inc(top2_exp_done, 1)
            act_e.wait_ge(logits_done, G + 1)
            nc.scalar.activation(gates_t[:], ps[:, 3, 0:2 * P].rearrange("p (a t) -> p a t", a=2),
                                 ACT.Copy).then_inc(gates_turned, 1)
            weights(len(pieces0))

            def experts(g):
                for u in range(E * J0):
                    e, j = divmod(u, J0)
                    f = min(P, HID0 - j * P)
                    act_e.wait_ge(up_done, g * E * J0 + u + 1)
                    nc.scalar.activation(act[0:f, u % 2], ps[0:f, u % 2], ACT.Silu).then_inc(act_done, 1)
                    if u == 3:
                        act_e.wait_ge(decay_done, g + 2)
                        nc.scalar.activation(kc[:, 3], kc[:, 3], ACT.Exp).then_inc(exp_done, 1)
                    if u == 11:
                        act_e.wait_ge(phase_done, g + 2)
                        nc.scalar.activation(kc[:, 4], kc[:, 0], ACT.Sin, scale=TWO_PI).then_inc(sin_done, 1)
                        nc.scalar.activation(kc[:, 5], kc[:, 0], ACT.Sin, scale=TWO_PI / 2).then_inc(sin_done, 1)
                    if u == 12:
                        act_e.wait_ge(sin_done, 3 * g + 2)
                        nc.scalar.activation(kc[:, 5], kc[:, 5], ACT.Square).then_inc(sin_done, 1)
                for half in range(2):
                    act_e.wait_ge(k_mm_done, 2 * g + half + 1)
                    if half == 0:
                        act_e.wait_ge(k_stored, 32 * g + 32)
                    nc.scalar.activation(k_out[:, half], ps[0:LO, 6 + half, 0:CH * LO].rearrange("p (a b) -> p a b", a=CH),
                                         ACT.Copy).then_inc(k_copied, 1)

            with act_e.Fori(0, G) as g:
                experts(g)

            copy = lambda dst, src: nc.scalar.activation(dst, src, ACT.Copy)
            act_e.wait_ge(k_t_done, 1)
            for a in range(2):
                copy(k_t[:, 4 * a:4 * a + 4], ps[:, a].rearrange("p (t h) -> p t h", t=4)).then_inc(k_t_copied, 1)
            for m in range(M):
                act_e.wait_ge(khat_mm, m + 1)
                copy(khat[:, m].rearrange("p (c r) h -> p r c h", c=2),
                     ps[:, 4 + m].rearrange("p (r c h) -> p r c h", r=2, c=2)).then_inc(khat_copied, 1)
            act_e.wait_ge(expert_done, G * E)
            for n, (_, _, col, cols) in enumerate(pieces1):
                act_e.wait_ge(wst1_in[n % 2], 16 * (n // 2 + 1))
                copy(w_hi[:, col:col + cols], wst1[:, n % 2, 0:cols]).then_inc(w1_hi_done, 1)

            def root(i, signal, wait):
                act_e.wait_ge(*wait)
                nc.scalar.activation(mid[:, 2 * i, 0:B], mid_mv[:, i, :, 1], ACT.Sqrt, bias=eps[:]).then_inc(signal, 1)

            def high_part(g):
                act_e.wait_ge(xt1_done, g + 1)
                copy(xt1_hi[:, g], ps[:, 4 + g % 2]).then_inc(xt1_hi_done, 1)

            for g in range(G):
                root(0, root1_done, (mid_stats, g + 1))
                if g >= 1:
                    high_part(g - 1)
                root(1, root2_done, (mid_stats2, g + 1))
            high_part(G - 1)

            def qkv_high(n):
                b, i = divmod(n, 6)
                act_e.wait_ge(qkv_mm, n + 1)
                copy(qkv_dst(qk_hi, v_hi, i), qkv_src(n)).then_inc(qkv_hi_done, 1)

            def turned_high(n):
                for a in range(2):
                    act_e.wait_ge(pt_done, 2 * n + a + 1)
                    copy(turned_dst(pt_hi, n, a), turned_src(a)).then_inc(pt_hi_done, 1)

            def softmax_exp(n):
                act_e.wait_ge(max_done, n + 1)
                nc.scalar.activation(prob[:, n % 2], ps[:, 2 * (n % 2):2 * (n % 2) + 2].rearrange("p a w -> p (a w)"), ACT.Exp,
                                     bias=sm[:, n % 2, 1:2], scale=SCALE, accum_out=sm[:, n % 2, 2:3]).then_inc(exp1_done, 1)

            for i in range(6):
                qkv_high(i)
            softmax_exp(0)
            for n in range(B * G):
                if n == 2:
                    act_e.wait_ge(gate_soft, 1)
                    nc.scalar.activation(gl[:, :, 0:E], gl[:, :, 0:E], ACT.Exp).then_inc(gate_exp_done, 1)
                    nc.scalar.activation(gl[:, :, E:E + 1], gl[:, :, E:E + 1], ACT.Tanh, scale=0.5).then_inc(gate_exp_done, 1)
                if n == 5:
                    act_e.wait_ge(gates1_turned, 1)
                    copy(gates_t[:], ps[:, 7, 0:2 * P].rearrange("p (a t) -> p a t", a=2)).then_inc(gates1_copied, 1)
                b, jt = divmod(n, G)
                turned_high(n)
                if n + 1 < B * G:
                    softmax_exp(n + 1)
                if jt == G - 2 and b + 1 < B:
                    for i in range(4):
                        qkv_high(6 * (b + 1) + i)
                if jt % 4 == 3:
                    jb = jt // 4
                    act_e.wait_ge(pv_done, 2 * b + jb + 1)
                    copy(acc[:, 4 * jb:4 * jb + 4, b * P:(b + 1) * P],
                         ps[:, 6].rearrange("p (t j) -> p t j", t=4)).then_inc(pv_copied, 1)
                    if jb == 1 and b + 1 < B:
                        for i in range(4, 6):
                            qkv_high(6 * (b + 1) + i)

            def hidden1(g):
                for u in range(UN1):
                    act_e.wait_ge(up1_done, g * UN1 + u + 1)
                    nc.scalar.activation(hid1[:, u % 4], ps[:, u % 4], ACT.Gelu_apprx_tanh, bias=b1_sb[:, u:u + 1])
                    nc.scalar.activation(hid1_hi[:, u % 4], ps[:, u % 4], ACT.Gelu_apprx_tanh,
                                         bias=b1_sb[:, u:u + 1]).then_inc(hid1_done, 1)

            with act_e.Fori(0, G) as g:
                hidden1(g)

        @block.vector
        def _(dve):
            step = Tally(dve_step)
            need = lambda v: dve.wait_ge(dve_step, v)
            tt, ts, stt = nc.vector.tensor_tensor, nc.vector.tensor_scalar, nc.vector.scalar_tensor_tensor
            mul, add, sub = ALU.mult, ALU.add, ALU.subtract
            K = lambda i: ks[:, i]
            a_im, c_re, c_im = small[:, 1], small[:, 2], small[:, 3]
            step.mark(nc.vector.memset(eps[:], LN_EPS))

            def inverse_root(r, var, t):
                v = step.mark(nc.vector.reciprocal(r, r))
                need(v)
                v = step.mark(tt(t, r, r, mul))
                need(v)
                v = step.mark(stt(t, var, LN_EPS, t, add, mul))
                need(v)
                v = step.mark(ts(t, t, -0.5, 1.5, mul, add))
                need(v)
                v = step.mark(tt(r, r, t, mul))
                need(v)

            dve.wait_ge(small_in, 80)
            step.mark(nc.vector.tensor_copy(ks[:, 1], ks[:, 0]))
            v = step.mark(nc.vector.tensor_copy(ks[:, 2], small[:, 0]))
            pair = lambda i: ks[:, i:i + 2]
            X, NN, R, PP = pair(1), pair(5), pair(7), pair(9)
            need(v)
            v = step.mark(ts(X, X, 88.0, -87.0, ALU.min, ALU.max))
            need(v)
            v = step.mark(ts(NN, X, 1.0 / math.log(2.0), None, mul))
            need(v)
            v = step.mark(ts(NN, NN, MAGIC, MAGIC, add, sub))
            need(v)
            v = step.mark(stt(R, NN, -LN2_HI, X, mul, add))
            need(v)
            v = step.mark(stt(R, NN, -LN2_LO, R, mul, add))
            need(v)
            v = step.mark(ts(PP, R, 1.0 / math.factorial(7), None, mul))
            for k in range(6, 0, -1):
                need(v)
                v = step.mark(stt(PP, PP, 1.0 / math.factorial(k), R, add, mul))
            power = exp2[:].rearrange("p (a h) -> p a h", a=2)
            v = step.mark(ts(power, NN, 127.0, 2.0 ** 23, add, mul))
            need(v)
            v = step.mark(stt(X, PP, 1.0, power.bitcast(F32), add, mul))
            need(v)
            s_th = step.mark(tt(K(9), K(1), a_im, mul))
            step.mark(ts(K(3), K(2), -1.0, None, mul))
            nc.vector.scalar_tensor_tensor(K(4), K(2), -1.0, K(1), mul, mul).then_inc(decay_done, 1)
            need(s_th)
            v = step.mark(nc.vector.tensor_copy(th_hi[:], K(9)))
            need(v)
            step.mark(tt(K(10), K(9), th_hi[:].bitcast(F32), sub))
            v = step.mark(ts(K(11), th_hi[:].bitcast(F32), INV_2PI_HI, None, mul))
            need(v)
            v = step.mark(ts(K(12), K(11), MAGIC, MAGIC, add, sub))
            need(v)
            step.mark(tt(K(11), K(11), K(12), sub))
            v = step.mark(ts(K(13), K(10), INV_2PI_HI, None, mul))
            need(v)
            v = step.mark(stt(K(13), K(9), INV_2PI_LO, K(13), mul, add))
            need(v)
            v = step.mark(tt(K(14), K(11), K(13), add))
            need(v)
            v = step.mark(ts(K(15), K(14), MAGIC_13, MAGIC_13, add, sub))
            need(v)
            v = step.mark(tt(K(11), K(11), K(15), sub))
            need(v)
            v = step.mark(tt(K(16), K(11), K(13), add))
            step.mark(ts(K(12), K(14), MAGIC, MAGIC, add, sub))
            need(step.base + step.n)
            nc.vector.tensor_tensor(K(12), K(14), K(12), sub).then_inc(phase_done, 1)
            step.mark(tt(K(17), K(3), K(3), mul))
            v = step.mark(tt(K(18), a_im, a_im, mul))
            need(v)
            v = step.mark(tt(K(17), K(17), K(18), add))
            need(v)
            v = step.mark(nc.vector.reciprocal(K(17), K(17)))
            need(v)
            v = step.mark(ts(K(17), K(17), 2.0 / C, None, mul))
            dve.wait_ge(trig_done, 4)
            step.mark(tt(K(8), K(8), K(8), mul))
            step.mark(tt(K(7), K(7), K(6), mul))
            v = step.mark(stt(K(5), K(6), 1.0, K(5), add, mul))
            need(v)
            v = step.mark(tt(K(8), K(8), K(6), mul))
            need(v)
            v = step.mark(stt(K(8), K(8), -2.0, K(5), mul, add))
            need(v)
            step.mark(tt(K(18), K(8), K(3), mul))
            step.mark(tt(K(19), K(7), a_im, mul))
            step.mark(tt(K(20), K(7), K(3), mul))
            v = step.mark(tt(K(21), K(8), a_im, mul))
            need(v)
            step.mark(tt(K(18), K(18), K(19), add))
            v = step.mark(tt(K(20), K(20), K(21), sub))
            need(v)
            step.mark(tt(K(18), K(18), K(17), mul))
            v = step.mark(tt(K(20), K(20), K(17), mul))
            need(v)
            step.mark(tt(K(19), c_re, K(18), mul))
            step.mark(tt(K(21), c_im, K(20), mul))
            step.mark(tt(K(22), c_re, K(20), mul))
            v = step.mark(tt(K(23), c_im, K(18), mul))
            need(v)
            step.mark(tt(K(19), K(19), K(21), sub))
            v = step.mark(tt(K(22), K(22), K(23), add))
            need(v)
            v = step.mark(ts(K(21), K(19), -1.0, None, mul))
            FH, FL, AR, CTR, CTI, NCTR = K(15), K(16), K(4), K(19), K(22), K(21)

            dve.wait_ge(x_in, 16 * G)
            for g in range(G):
                for b in range(B):
                    st = (g % 2) * B + b
                    v = step.mark(nc.vector.bn_stats(stats[:, st], xn[:, g, b * P:(b + 1) * P]))
                need(v)
                for b in range(B):
                    last = nc.vector.bn_aggr(mv[:, g * B + b], stats[:, (g % 2) * B + b])
            last.then_inc(stats_done, 1)
            dve.wait_ge(root_done, 1)
            dve.wait_ge(wg0_hi_done, 1)
            inverse_root(rstd[:], mv[:, :, 1], newton[:])

            def low_part(g):
                dve.wait_ge(xt_hi_done, g + 1)
                nc.vector.tensor_tensor(xt_lo[:, g], ps[:, g % 2], xt_hi[:, g].bitcast(F32), sub).then_inc(xt_lo_done, 1)

            tt(wg0_lo[:], wg0_sb[:], wg0_hi[:].bitcast(F32), sub).then_inc(wg0_done, 1)
            for g in range(G):
                for b in range(B):
                    t = g * B + b
                    v = nc.vector.tensor_scalar(xn[:, g, b * P:(b + 1) * P], xn[:, g, b * P:(b + 1) * P],
                                                mv[:, t, 0:1], rstd[:, t:t + 1], sub, mul)
                v.then_inc(xn_ready, 1)
                if g >= 1:
                    low_part(g - 1)
            low_part(G - 1)

            wide = lambda a: a.unsqueeze(2).broadcast_to((P, T, E))
            revb = rev.unsqueeze(1).broadcast_to((P, T, E))
            dve.wait_ge(logits_done, G)
            v = step.mark(nc.vector.tensor_copy(lg, ps[:, 2, 0:T * E].rearrange("p (t e) -> p t e", e=E)))
            need(v)
            for m, p, oh, low in ((m1, p1, oh1, False), (m2, p2, oh2, True)):
                v = step.mark(nc.vector.reduce_max(m, lg, AX.X))
                need(v)
                v = step.mark(tt(eq, lg, wide(m), ALU.is_equal))
                need(v)
                v = step.mark(tt(k2, eq, revb, mul))
                need(v)
                v = step.mark(nc.vector.reduce_max(p, k2, AX.X))
                need(v)
                v = step.mark(tt(oh, k2, wide(p), ALU.is_equal))
                need(v)
                if not low:
                    v = step.mark(stt(lg, oh, -3.0e38, lg, mul, add))
                    need(v)
            tt(m2, m2, m1, sub).then_inc(top2_done, 1)
            dve.wait_ge(top2_exp_done, 1)
            v = step.mark(ts(p1, p2, 1.0, None, add))
            need(v)
            v = step.mark(nc.vector.reciprocal(p1, p1))
            need(v)
            step.mark(tt(p2, p2, p1, mul))
            v = step.mark(tt(oh1, oh1, wide(p1), mul))
            need(v)
            v = step.mark(tt(oh2, oh2, wide(p2), mul))
            need(v)
            tt(gates[:], oh1, oh2, add).then_inc(gates_done, 1)

            def chunk(g):
                col = lambda a, n: a[:, bass.ds(g * CH, CH)].unsqueeze(2).broadcast_to((P, CH, n))
                lag = lagv.unsqueeze(1).broadcast_to((P, CH, LAGS))
                lo, hi = slice(0, LO), slice(LO, LAGS)
                v1 = step.mark(tt(kc[:, 0], col(FH, LAGS), lag, mul))
                yield
                nc.vector.tensor_tensor(kc[:, 3], col(AR, LAGS), lag, mul).then_inc(decay_done, 1)
                yield
                need(v1)
                v1 = step.mark(ts(kc[:, 1], kc[:, 0], MAGIC, MAGIC, add, sub))
                yield
                v2 = step.mark(tt(kc[:, 2], col(FL, LAGS), lag, mul))
                yield
                need(v1)
                v1 = step.mark(tt(kc[:, 0], kc[:, 0], kc[:, 1], sub))
                yield
                need(v1)
                v1 = step.mark(tt(kc[:, 0], kc[:, 0], kc[:, 2], add))
                yield
                need(v1)
                v1 = step.mark(ts(kc[:, 1], kc[:, 0], MAGIC, MAGIC, add, sub))
                yield
                need(v1)
                nc.vector.tensor_tensor(kc[:, 0], kc[:, 0], kc[:, 1], sub).then_inc(phase_done, 1)
                yield
                yield
                yield
                yield
                yield
                dve.wait_ge(sin_done, 3 * g + 3)
                v1 = step.mark(ts(kc[:, 6], kc[:, 5], -2.0, 1.0, mul, add))
                yield
                dve.wait_ge(exp_done, g + 1)
                need(v1)
                v1 = step.mark(tt(kc[:, 7], kc[:, 3], kc[:, 6], mul))
                v2 = step.mark(tt(kc[:, 8], kc[:, 3], kc[:, 4], mul))
                yield
                need(v2)
                step.mark(tt(kg[:, 0], col(CTR, LO), kc[:, 7, :, hi], mul))
                v3 = step.mark(tt(kg[:, 2], col(CTI, LO), kc[:, 8, :, hi], mul))
                yield
                step.mark(tt(kg[:, 1], col(NCTR, LO), kc[:, 8, :, hi], mul))
                v4 = step.mark(tt(kg[:, 3], col(CTI, LO), kc[:, 7, :, hi], mul))
                yield
                need(v4)
                nc.vector.tensor_tensor(kg[:, 0], kg[:, 0], kg[:, 2], sub).then_inc(tables_done, 1)
                nc.vector.tensor_tensor(kg[:, 1], kg[:, 1], kg[:, 3], sub).then_inc(tables_done, 1)
                yield

            def weigh(g, e):
                dve.wait_ge(expert_done, g * E + e + 1)
                dve.wait_ge(gate_in[e % 4], 16 * (2 * g + e // 4 + 1))
                dst = part[:, e % 2] if e else acc[:, bass.ds(g, 1), :].rearrange("p a w -> p (a w)")
                nc.vector.tensor_tensor(dst, ps[:, 4 + e % 2], gate_row[:, e % 4], mul).then_inc(part_done, 1)

            def hidden(g, first=False):
                chunk_steps = chunk(g)
                for u in range(UN):
                    e, j = divmod(u, J0)
                    s, f = u % 2, min(P, HID0 - j * P)
                    dve.wait_ge(act_done, g * UN + u + 1)
                    tt(hid[0:f, u % 3], act[0:f, s], ps[0:f, 2 + s], mul)
                    tt(hid_hi[0:f, u % 3], act[0:f, s], ps[0:f, 2 + s], mul).then_inc(hid_done, 1)
                    next(chunk_steps, None)
                    if j == 1 and not (first and e == 0):
                        weigh(g if e else g - 1, (e - 1) % E)
                assert next(chunk_steps, 1) == 1

            start = step.base + step.n
            step.enter(start, 0, CHUNK_STEPS)
            hidden(0, first=True)
            with dve.Fori(1, G) as g:
                step.enter(start, g, CHUNK_STEPS)
                hidden(g)
            step.leave(G)
            weigh(G - 1, E - 1)

            dve.wait_ge(khat_copied, M)
            for half, (o_re, o_im) in enumerate(((sub, add), (add, sub))):
                m = slice(2 * half, 2 * half + 2)
                tt(khat[:, m, 2], khat[:, m, 2], khat[:, m, 1], o_re).then_inc(khat_ready, 1)
                tt(khat[:, m, 3], khat[:, m, 3], khat[:, m, 0], o_im).then_inc(khat_ready, 1)
            dve.wait_ge(khat_ready, 4)
            for m in range(M):
                X = lambda c, ri: ps[:, 4 * (m % 2) + 2 * c + ri].rearrange("p (b h) -> p b h", b=B)
                KH = lambda kind: khat[:, m, kind].unsqueeze(1).broadcast_to((P, B, P))
                wide3 = lambda a: a.rearrange("p (b h) -> p b h", b=B)
                Z = lambda c, ri: z[:, m, c, ri]
                T_ = lambda i: prod[:, i]
                dve.wait_ge(x_hat_done, m + 1)
                if m:
                    dve.wait_ge(z_ready, m)
                for dst, c, ri, kind in ((Z(0, 0), 0, 0, 0), (T_(0), 0, 1, 1), (Z(0, 1), 0, 0, 1), (T_(1), 0, 1, 0),
                                           (Z(1, 0), 0, 0, 2), (T_(2), 0, 1, 3), (Z(1, 1), 0, 0, 3), (T_(3), 0, 1, 2),
                                           (T_(4), 1, 0, 0), (T_(5), 1, 1, 1), (T_(6), 1, 0, 1), (T_(7), 1, 1, 0)):
                    v = tt(wide3(dst), X(c, ri), KH(kind), mul)
                v.then_inc(products_done, 1)
                dve.wait_ge(products_done, m + 1)
                tt(Z(0, 0), Z(0, 0), T_(0), sub)
                tt(Z(0, 1), Z(0, 1), T_(1), add)
                step.mark(tt(Z(1, 0), Z(1, 0), T_(2), sub))
                step.mark(tt(Z(1, 1), Z(1, 1), T_(3), add))
                step.mark(tt(T_(4), T_(4), T_(5), sub))
                v = step.mark(tt(T_(6), T_(6), T_(7), add))
                need(v)
                tt(Z(1, 0), Z(1, 0), T_(4), add)
                tt(Z(1, 1), Z(1, 1), T_(6), add).then_inc(z_ready, 1)

            def moments(src, i, signal):
                for b in range(B):
                    v = step.mark(nc.vector.bn_stats(stats[:, b], src[:, b * P:(b + 1) * P]))
                need(v)
                for b in range(B):
                    last = nc.vector.bn_aggr(mid_mv[:, i, b], stats[:, b])
                last.then_inc(signal, 1)

            def normalise(dst, src, i, signal):
                inverse_root(mid[:, 2 * i, 0:B], mid_mv[:, i, :, 1], mid[:, 2 * i + 1, 0:B])
                for b in range(B):
                    c = slice(b * P, (b + 1) * P)
                    last = ts(dst[:, c], src[:, c], mid_mv[:, i, b, 0:1], mid[:, 2 * i, b:b + 1], sub, mul)
                last.then_inc(signal, 1)

            def residual(g):
                dve.wait_ge(skip_done, g + 1)
                dve.wait_ge(y_done, g + 1)
                tt(xn[:, g], ps[:, g % 2], xn[:, g], add).then_inc(r_done, 1)
                dve.wait_ge(r_done, g + 1)
                moments(xn[:, g], 0, mid_stats)

            def first_norm(g):
                dve.wait_ge(root1_done, g + 1)
                normalise(xn[:, g], xn[:, g], 0, norm1_done)

            def layer0_sum(g):
                dve.wait_ge(xb_done, g + 1)
                dve.wait_ge(ffn_turned, g + 1)
                v = step.mark(tt(xs[:, g % 2], ps[:, 2 + g % 2], xs[:, g % 2], add))
                dve.wait_ge(scaled_done, g + 1)
                need(v)
                tt(xn[:, g], xn[:, g], xs[:, g % 2], add).then_inc(x1_done, 1)
                dve.wait_ge(x1_done, g + 1)
                moments(xn[:, g], 1, mid_stats2)

            def second_norm(g):
                dve.wait_ge(root2_done, g + 1)
                normalise(xn1[:, g % 2], xn[:, g], 1, xn1_done)

            def low1(g):
                dve.wait_ge(xt1_hi_done, g + 1)
                tt(xt1_lo[:, g], ps[:, 4 + g % 2], xt1_hi[:, g].bitcast(F32), sub).then_inc(xt1_lo_done, 1)

            for g in range(G):
                residual(g)
                if g >= 1:
                    second_norm(g - 1)
                first_norm(g)
                if g >= 1:
                    low1(g - 1)
                layer0_sum(g)
            second_norm(G - 1)
            low1(G - 1)

            def qkv_low(n):
                i = n % 6
                dve.wait_ge(qkv_hi_done, n + 1)
                tt(qkv_dst(qk_lo, v_lo, i), qkv_src(n), qkv_dst(qk_hi, v_hi, i).bitcast(F32), sub).then_inc(qkv_lo_done, 1)

            def row_max(n):
                s = n % 2
                dve.wait_ge(s_done, n + 1)
                v = step.mark(nc.vector.reduce_max(sm[:, s, 0:1], ps[:, 2 * s:2 * s + 2].rearrange("p a w -> p (a w)"), AX.X))
                need(v)
                ts(sm[:, s, 1:2], sm[:, s, 0:1], -SCALE, None, mul).then_inc(max_done, 1)

            def probabilities(n):
                s = n % 2
                dve.wait_ge(exp1_done, n + 1)
                v = step.mark(nc.vector.reciprocal(sm[:, s, 3:4], sm[:, s, 2:3]))
                need(v)
                ts(prob[:, s], prob[:, s], sm[:, s, 3:4], None, mul).then_inc(prob_done, 1)

            def turned_low(n):
                for a in range(2):
                    dve.wait_ge(pt_hi_done, 2 * n + a + 1)
                    tt(turned_dst(pt_lo, n, a), turned_src(a), turned_dst(pt_hi, n, a).bitcast(F32), sub).then_inc(pt_lo_done, 1)

            gw, thr = gl[:, :, 0:E], gl[:, :, E:E + 1]
            per_token = lambda i: gs[:, i].unsqueeze(2).broadcast_to((P, T, E))

            def gate_logits():
                dve.wait_ge(logits1_done, G)
                v = step.mark(tt(gl[:], ps[:, 6, 0:T * GW].rearrange("p (t e) -> p t e", e=GW),
                                 bias1[:].unsqueeze(1).broadcast_to((P, T, GW)), add))
                need(v)
                v = step.mark(nc.vector.reduce_max(gs[:, 0], gw, AX.X))
                need(v)
                tt(gw, gw, per_token(0), sub).then_inc(gate_soft, 1)

            def gate_weights():
                dve.wait_ge(gate_exp_done, 2)
                step.mark(nc.vector.reduce_sum(gs[:, 0], gw, AX.X))
                v = step.mark(ts(thr, thr, THRESHOLD / 2, THRESHOLD / 2, mul, add))
                need(v)
                v = step.mark(nc.vector.reciprocal(gs[:, 0], gs[:, 0]))
                need(v)
                v = step.mark(tt(gw, gw, per_token(0), mul))
                need(v)
                v = step.mark(tt(gw, gw, thr.broadcast_to((P, T, E)), sub))
                need(v)
                v = step.mark(ts(gw, gw, 0.0, None, ALU.max))
                need(v)
                v = step.mark(nc.vector.reduce_sum(gs[:, 0], gw, AX.X))
                need(v)
                v = step.mark(ts(gs[:, 1], gs[:, 0], 0.0, None, ALU.is_equal))
                need(v)
                v = step.mark(tt(gs[:, 0], gs[:, 0], gs[:, 1], add))
                need(v)
                v = step.mark(nc.vector.reciprocal(gs[:, 0], gs[:, 0]))
                need(v)
                tt(gates[:], gw, per_token(0), mul).then_inc(gates1_done, 1)

            gate_logits()
            for i in range(6):
                qkv_low(i)
            row_max(0)
            for n in range(B * G):
                if n == 3:
                    gate_weights()
                b, jt = divmod(n, G)
                probabilities(n)
                if n + 1 < B * G:
                    row_max(n + 1)
                turned_low(n)
                if jt == G - 2 and b + 1 < B:
                    for i in range(4):
                        qkv_low(6 * (b + 1) + i)
                if jt == G - 1 and b + 1 < B:
                    for i in range(4, 6):
                        qkv_low(6 * (b + 1) + i)

            def weigh1(g, e):
                dve.wait_ge(gate1_in[e % 4], 16 * (2 * g + e // 4 + 1))
                dve.wait_ge(expert1_done, g * E + e + 1)
                stt(part1[:, e % 2], ps[:, 4 + e % 2], b2_sb[:, e:e + 1], gate_row1[:, e % 4], add, mul).then_inc(part1_done, 1)

            def join1(g, e):
                a = acc[:, bass.ds(g, 1), :].rearrange("p a w -> p (a w)")
                dve.wait_ge(part1_done, g * E + e + 1)
                if e:
                    dve.wait_ge(join1_done, g * E + e)
                tt(a, a, part1[:, e % 2], add).then_inc(join1_done, 1)

            def add_final(g):
                if g >= 2:
                    dve.wait_ge(stored[g % 2], 16 * (g // 2))
                dve.wait_ge(final_done, g + 1)
                tt(final[:, g % 2], ps[:, 6 + g % 2], xn[:, g], add).then_inc(added_done, 1)

            def hidden1(g, first=False, last=False):
                for u in range(UN1):
                    e, j = divmod(u, J1)
                    dve.wait_ge(hid1_done, g * UN1 + u + 1)
                    tt(hid1_lo[:, u % 4], hid1[:, u % 4], hid1_hi[:, u % 4].bitcast(F32), sub).then_inc(hid1_lo_done, 1)
                    if not (first and e == 0):
                        to, ex = (g, e - 1) if e else (g - 1, E - 1)
                        if j == 2:
                            weigh1(to, ex)
                        if j == 3:
                            join1(to, ex)
                    if last and j == 1 and e >= 1:
                        add_final(e - 1)

            dve.wait_ge(pv_copied, 2 * B)
            hidden1(0, first=True)
            with dve.Fori(1, G - 1) as g:
                hidden1(g)
            hidden1(G - 1, last=True)
            weigh1(G - 1, E - 1)
            join1(G - 1, E - 1)
            add_final(G - 1)

        @block.tensor
        def _(pe):
            mm = nc.tensor.matmul

            def three(dst, a_hi, a_lo, b_hi, b_lo, first=True, last=True):
                mm(dst, a_lo, b_hi, start=first, stop=False)
                mm(dst, a_hi, b_lo, start=False, stop=False)
                return mm(dst, a_hi, b_hi, start=False, stop=last)

            pe.wait_ge(ident_done, 1)
            pe.wait_ge(wg0_done, 1)

            def logits(g):
                pe.wait_ge(xt_lo_done, g + 1)
                for b in range(B):
                    c = slice(b * P, (b + 1) * P)
                    o = ps[:, 2, (g * B + b) * E:(g * B + b + 1) * E]
                    last = three(o, xt_hi[:, g, c], xt_lo[:, g, c], wg0_hi[:], wg0_lo[:])
                last.then_inc(logits_done, 1)

            for g in range(G):
                pe.wait_ge(xn_ready, g + 1)
                for b in range(B):
                    last = nc.tensor.transpose(ps[:, g % 2, b * P:(b + 1) * P], xn[:, g, b * P:(b + 1) * P], ident[:])
                last.then_inc(xt_done, 1)
                if g >= 1:
                    logits(g - 1)
            logits(G - 1)
            pe.wait_ge(gates_done, 1)
            flat = gates[:].rearrange("p t e -> p (t e)")
            for a in range(2):
                last = nc.tensor.transpose(ps[:, 3, a * P:(a + 1) * P], flat[:, a * P:(a + 1) * P], ident[:])
            last.then_inc(logits_done, 1)

            def up(g, u):
                e, j = divmod(u, J0)
                f = min(P, HID0 - j * P)
                xh, xl = (t[:, bass.ds(g, 1), :].rearrange("p a w -> p (a w)") for t in (xt_hi, xt_lo))
                for bank, base in ((u % 2, 0), (2 + u % 2, W2C)):
                    c = base + e * HID0 + j * P
                    last = three(ps[0:f, bank], w_hi[:, c:c + f], w_lo[:, c:c + f], xh, xl)
                last.then_inc(up_done, 1)

            def down(g, u):
                e, j = divmod(u, J0)
                s, f = u % 3, min(P, HID0 - j * P)
                pe.wait_ge(hid_lo_done, g * UN + u + 1)
                c = w3_col(e, j)
                last = three(ps[:, 4 + e % 2], w_hi[0:f, c:c + P], w_lo[0:f, c:c + P], hid_hi[0:f, s], hid_lo[0:f, s],
                             first=(j == 0), last=(j == J0 - 1))
                if j == J0 - 1:
                    last.then_inc(expert_done, 1)

            def kernel_chunk(g):
                for half in range(2):
                    rows = slice(half * N, (half + 1) * N)
                    for h in range(CH):
                        o = ps[0:LO, 6 + half, h * LO:(h + 1) * LO]
                        mm(o, kg[rows, 0, h, :], kc[rows, 7, h, 0:LO], start=True, stop=False)
                        last = mm(o, kg[rows, 1, h, :], kc[rows, 8, h, 0:LO], start=False, stop=True)
                    last.then_inc(k_mm_done, 1)

            pe.wait_ge(w_lo_done, len(pieces0))
            pe.wait_ge(gates_turned, 1)
            for u in range(2):
                up(0, u)

            def experts(g, last):
                for u in range(UN):
                    if u + 2 < UN or not last:
                        pe.wait_ge(hid_done, g * UN + u + 1)
                        up(g + (u + 2) // UN, (u + 2) % UN)
                    if u == UN - 4:
                        pe.wait_ge(tables_done, 2 * g + 2)
                    down(g, u)
                    if u == UN - 4:
                        kernel_chunk(g)

            with pe.Fori(0, G - 1) as g:
                experts(g, False)
            experts(G - 1, True)

            pe.wait_ge(kernel_in, 16)
            for t in range(G):
                last = nc.tensor.transpose(ps[:, t // 4, (t % 4) * P:(t % 4 + 1) * P], k_nat[:, t * P:(t + 1) * P], ident[:])
            last.then_inc(k_t_done, 1)
            pe.wait_ge(k_t_copied, 2)
            pe.wait_ge(fwd_in, 16)
            pe.wait_ge(part_done, G * E)
            pe.wait_ge(k_copied, 2 * G)
            halves = k_t.rearrange("p (c t) h -> p t c h", c=2)
            for m in range(M):
                for part_ in range(2):
                    for t in range(CT):
                        last = mm(ps[:, 4 + m, part_ * 2 * P:(part_ + 1) * 2 * P], fwd[:, t, part_, m * P:(m + 1) * P],
                                  halves[:, t], start=(t == 0), stop=(t == CT - 1))
                last.then_inc(khat_mm, 1)

            for m in range(M):
                if m == 1:
                    pe.wait_ge(khat_copied, M)
                if m >= 2:
                    pe.wait_ge(products_done, m - 1)
                for c in range(2):
                    for part_ in range(2):
                        for t in range(CT):
                            last = mm(ps[:, 4 * (m % 2) + 2 * c + part_], fwd[:, t, part_, m * P:(m + 1) * P],
                                      xn[:, c * CT + t], start=(t == 0), stop=(t == CT - 1))
                last.then_inc(x_hat_done, 1)

            def logits1(g):
                pe.wait_ge(xt1_lo_done, g + 1)
                for b in range(B):
                    c = slice(b * P, (b + 1) * P)
                    o = ps[:, 6, (g * B + b) * GW:(g * B + b + 1) * GW]
                    w = slice(GATE1, GATE1 + GW)
                    last = three(o, xt1_hi[:, g, c], xt1_lo[:, g, c], w_hi[:, w], w_lo[:, w])
                last.then_inc(logits1_done, 1)

            def turn1(g):
                pe.wait_ge(xn1_done, g + 1)
                for b in range(B):
                    last = nc.tensor.transpose(ps[:, 4 + g % 2, b * P:(b + 1) * P], xn1[:, g % 2, b * P:(b + 1) * P], ident[:])
                last.then_inc(xt1_done, 1)

            pe.wait_ge(z_ready, M)
            pe.wait_ge(inv_in, 16)
            pe.wait_ge(w1_lo_done, 2)
            for g in range(G):
                c, t = divmod(g, CT)
                if g >= 2:
                    pe.wait_ge(r_done, g - 1)
                for m in range(M):
                    for part_ in range(2):
                        last = mm(ps[:, g % 2], inv[:, m, part_, t * P:(t + 1) * P], z[:, m, c, part_],
                                  start=(m == 0 and part_ == 0), stop=(m == M - 1 and part_ == 1))
                last.then_inc(y_done, 1)
                if g >= 2:
                    pe.wait_ge(x1_done, g - 1)
                for b in range(B):
                    last = nc.tensor.transpose(ps[:, 2 + g % 2, b * P:(b + 1) * P], acc[:, g, b * P:(b + 1) * P], ident[:])
                last.then_inc(ffn_turned, 1)
                if g >= 1:
                    if g >= 2:
                        logits1(g - 2)
                    turn1(g - 1)
            logits1(G - 2)
            turn1(G - 1)
            logits1(G - 1)

            def qkv(n):
                b, i = divmod(n, 6)
                if n >= 2:
                    pe.wait_ge(qkv_lo_done, n - 1)
                bank = ps[:, 6 + n % 2]
                cols = slice(b * P, (b + 1) * P)
                if i < 4:
                    w = slice(QKV + (i // 2) * P, QKV + (i // 2 + 1) * P)
                    gr = slice(4 * (i % 2), 4 * (i % 2) + 4)
                    last = three(bank.rearrange("p (t j) -> p t j", t=4), w_hi[:, w], w_lo[:, w],
                                 xt1_hi[:, gr, cols], xt1_lo[:, gr, cols])
                else:
                    w = slice(QKV + 2 * P, QKV + 3 * P)
                    for t in range(4):
                        gr = 4 * (i - 4) + t
                        last = three(bank[:, t * P:(t + 1) * P], xt1_hi[:, gr, cols], xt1_lo[:, gr, cols], w_hi[:, w], w_lo[:, w])
                last.then_inc(qkv_mm, 1)

            def scores(n):
                jt = n % G
                pe.wait_ge(qkv_lo_done, 6 * (n // G) + 4)
                if n >= 2:
                    pe.wait_ge(exp1_done, n - 1)
                j = slice(jt * P, (jt + 1) * P)
                for a in range(2):
                    i = slice(a * C, (a + 1) * C)
                    last = three(ps[:, 2 * (n % 2) + a], qk_hi[:, 1, j], qk_lo[:, 1, j], qk_hi[:, 0, i], qk_lo[:, 0, i])
                last.then_inc(s_done, 1)

            pe.wait_ge(gate_soft, 1)
            for i in range(6):
                qkv(i)
            scores(0)
            scores(1)
            for n in range(B * G):
                if n == 4:
                    pe.wait_ge(gates1_done, 1)
                    for a in range(2):
                        last = nc.tensor.transpose(ps[:, 7, a * P:(a + 1) * P], flat[:, a * P:(a + 1) * P], ident[:])
                    last.then_inc(gates1_turned, 1)
                b, jt = divmod(n, G)
                pe.wait_ge(prob_done, n + 1)
                for a in range(2):
                    if n >= 1:
                        pe.wait_ge(pt_lo_done, 2 * n - 1 + a)
                    for t in range(4):
                        last = nc.tensor.transpose(ps[:, 4 + a, t * P:(t + 1) * P],
                                                   prob[:, n % 2, (4 * a + t) * P:(4 * a + t + 1) * P], ident[:])
                    last.then_inc(pt_done, 1)
                if jt == G - 2 and b + 1 < B:
                    pe.wait_ge(pv_copied, 2 * b + 1)
                    pe.wait_ge(gates1_copied, 1)
                    for i in range(4):
                        qkv(6 * (b + 1) + i)
                if n + 2 < B * G:
                    scores(n + 2)
                if jt % 4 == 3:
                    pe.wait_ge(pt_lo_done, 2 * n + 2)
                    pe.wait_ge(qkv_lo_done, 6 * (b + 1) + (4 if jt == G - 1 and b + 1 < B else 0))
                    for t in range(G):
                        last = three(ps[:, 6], v_hi[:, t], v_lo[:, t], pt_hi[:, t], pt_lo[:, t],
                                     first=(t == 0), last=(t == G - 1))
                    last.then_inc(pv_done, 1)
                    if jt == G - 1 and b + 1 < B:
                        pe.wait_ge(pv_copied, 2 * b + 2)
                        for i in range(4, 6):
                            qkv(6 * (b + 1) + i)

            def up1(g, u):
                xh, xl = (t[:, bass.ds(g, 1), :].rearrange("p a w -> p (a w)") for t in (xt1_hi, xt1_lo))
                w = slice(u * P, (u + 1) * P)
                three(ps[:, u % 4], w_hi[:, w], w_lo[:, w], xh, xl).then_inc(up1_done, 1)

            def down1(g, u):
                e, j = divmod(u, J1)
                pe.wait_ge(hid1_lo_done, g * UN1 + u + 1)
                w = slice(E * HID1 + u * P, E * HID1 + (u + 1) * P)
                last = three(ps[:, 4 + e % 2], w_hi[:, w], w_lo[:, w], hid1_hi[:, u % 4], hid1_lo[:, u % 4],
                             first=(j == 0), last=(j == J1 - 1))
                if j == J1 - 1:
                    last.then_inc(expert1_done, 1)

            def turn_out(g):
                if g >= 2:
                    pe.wait_ge(added_done, g - 1)
                for b in range(B):
                    last = nc.tensor.transpose(ps[:, 6 + g % 2, b * P:(b + 1) * P], acc[:, g, b * P:(b + 1) * P], ident[:])
                last.then_inc(final_done, 1)

            def experts1(g, last):
                for u in range(UN1):
                    if u + 3 < UN1 or not last:
                        up1(g + (u + 3) // UN1, (u + 3) % UN1)
                    down1(g, u)
                    if last and u % J1 == 0 and u // J1 >= 1:
                        pe.wait_ge(join1_done, (u // J1) * E)
                        turn_out(u // J1 - 1)

            pe.wait_ge(w1_lo_done, len(pieces1))
            pe.wait_ge(exp1_done, B * G)
            pe.wait_ge(pv_copied, 2 * B)
            for u in range(3):
                up1(0, u)
            with pe.Fori(0, G - 1) as g:
                experts1(g, False)
            experts1(G - 1, True)
            pe.wait_ge(join1_done, G * E)
            turn_out(G - 1)


def kernel(**inputs):
    from concourse import bacc
    from concourse.bass_utils import run_bass_kernel_spmd

    nc = bacc.Bacc("TRN2", target_bir_lowering=False, num_devices=1)
    arrays = layout({k: np.asarray(v) for k, v in inputs.items()})
    aps = {n: nc.dram_tensor(n, a.shape, F32, kind="ExternalInput").ap() for n, a in arrays.items()}
    out = nc.dram_tensor("out", (B, L, H), F32, kind="ExternalOutput").ap()
    program(nc, out=out, **aps)
    return run_bass_kernel_spmd(nc, [arrays], core_ids=[0]).results[0]["out"]


def layout(a):
    def by_state(p):
        return p.reshape(2, HH, N).transpose(0, 2, 1).reshape(P, HH)

    freq = np.concatenate([np.arange(0, C, 2), np.arange(1, C, 2)]) + 0.5
    angle = 2 * np.pi * np.outer(np.arange(C), freq) / (2 * C)
    dft = np.stack([np.cos(angle), -np.sin(angle)]).astype(np.float32)
    fwd = dft.reshape(2, CT, P, C).transpose(2, 1, 0, 3)
    inv = dft.transpose(0, 2, 1).reshape(2, M, P, C).transpose(2, 1, 0, 3)
    d = dict(
        x=a["L0_attn_x"],
        state_params=np.stack([by_state(a["L0_attn_" + n]) for n in ("log_A_real", "A_imag", "C_re", "C_im")], 1),
        log_dt=a["L0_attn_log_dt"], skip=a["L0_attn_D"], ln_w=a["L0_attn_ln_w"], ln_b=a["L0_attn_ln_b"],
        wg0=a["L0_ffn_Wg"].T,
        w1_0=a["L0_ffn_W1"].transpose(2, 0, 1).reshape(P, E * HID0),
        w2_0=a["L0_ffn_W2"].transpose(2, 0, 1).reshape(P, E * HID0),
        w3_0=a["L0_ffn_W3"].transpose(0, 2, 1),
        lag_row=np.concatenate([np.arange(LO), LO * np.arange(LO), E - np.arange(E)]).astype(np.float32),
        dft_fwd=fwd, dft_inv=inv,
        wqkv=np.stack([a["L1_attn_W_query"], a["L1_attn_W_key"], a["L1_attn_W_value"]], 1),
        wg1=np.pad(np.concatenate([a["L1_ffn_Wg"], a["L1_ffn_Wt"]], 1), ((0, 0), (0, GW - E - 1))),
        gate_bias=np.pad(np.concatenate([a["L1_ffn_bg"], a["L1_ffn_bt"]]), (0, GW - E - 1)),
        w1_1=a["L1_ffn_W1"],
        b1=a["L1_ffn_b1"].reshape(E * J1, P).T,
        w2_1=a["L1_ffn_W2"],
        b2=a["L1_ffn_b2"].T,
    )
    return {n: np.ascontiguousarray(v) for n, v in d.items()}
```

```python
import math
from contextlib import ExitStack

import numpy as np
import concourse.bass as bass
from concourse import mybir

F32 = mybir.dt.float32
F32R = mybir.dt.float32r
ALU = mybir.AluOpType
ACT = mybir.ActivationFunctionType
AX = mybir.AxisListType

B, L, H = 4, 1024, 128
N = 64
P = 128
G = L // P
W = B * P
E = 8
HID0 = 341
J0 = -(-HID0 // P)
HID1 = 512
J1 = HID1 // P
LN_EPS = 1e-5
THRESHOLD = 0.125
T = G * B
NC = (2 * B * L - E) // W + E
WA, WC = 2 * HID0, 2 * HID0 + J0 * P
assert NC % 2 == 1
GW = 10
UN1 = E * J1
QKV, GATE1 = 2 * E * HID1, 2 * E * HID1 + 3 * P
SCALE = float(1.0 / np.sqrt(np.float32(H)))
LO = 32
LAGS = 2 * LO
HH = H // 2
CH = 16
KC = HH // CH
C = 512
CT = C // P
M = C // P
MAGIC = 1.5 * 2.0 ** 23
MAGIC_13 = 1.5 * 2.0 ** 10
TWO_PI = 6.283185
INV_2PI = 1.0 / (2.0 * math.pi)
INV_2PI_HI = float(np.round(INV_2PI * 2 ** 14) / 2 ** 14)
INV_2PI_LO = INV_2PI - INV_2PI_HI
LN2_HI = 355.0 / 512.0
LN2_LO = math.log(2.0) - LN2_HI


class Tally:

    def __init__(self, sem):
        self.sem, self.n = sem, 0

    def mark(self, instruction):
        instruction.then_inc(self.sem, 1)
        self.n += 1
        return self.n



def program(nc, x, state_params, log_dt, skip, ln_w, ln_b, wg0, w0, lag_row,
            dft_fwd, dft_inv, wqkv, wg1, gate_bias, w1_1, b1, w2_1, b2, out):
    ctx = ExitStack()
    with ctx:
        def sb(name, shape, dt=F32):
            return ctx.enter_context(nc.sbuf_tensor(name, shape, dt))

        def sem(name):
            return ctx.enter_context(nc.semaphore(name))

        kernel_dram = nc.dram_tensor("kernel_dram", (H, LO, LO), F32).ap()
        gates_dram = nc.dram_tensor("gates_dram", (T, E, P), F32).ap()
        x_slots = nc.dram_tensor("x_slots", (NC * W, H), F32).ap()
        y_slots = nc.dram_tensor("y_slots", (NC * W, H), F32).ap()

        WCOLS = 2 * E * HID1 + 3 * P + GW + 6
        w_hi = sb("w_hi", [P, WCOLS], F32R)
        w_lo = sb("w_lo", [P, WCOLS], F32R)
        xn = sb("xn", [P, G, W])
        acc = sb("acc", [P, G, W])
        gate2 = sb("gate2", [P, 2, T])
        slot = sb("slot", [P, 2, T], mybir.dt.int32)
        expert_of = sb("expert_of", [P, NC], mybir.dt.int32)
        ident = sb("ident", [P, P])
        stats = sb("stats", [P, 2 * B, 6])
        mv = sb("mv", [P, G * B, 2])
        rstd = sb("rstd", [P, G * B])
        newton = sb("newton", [P, G * B])
        eps = sb("eps", [P, 1])
        consts = sb("consts", [P, LAGS + E])
        lagv = consts[:, 0:LAGS]
        rev = consts[:, LAGS:LAGS + E]
        gates = sb("gates", [P, G * B, E])
        gates_t = sb("gates_t", [P, 2, P])

        vec_rows = sb("vec_rows", [P, 3, P])
        bias1 = sb("bias1", [P, GW])
        gl = sb("gl", [P, G * B, GW])
        gs = sb("gs", [P, 2, G * B])
        b1_sb = sb("b1_sb", [P, E * J1])
        b2_sb = sb("b2_sb", [P, E])
        mid = sb("mid", [P, 6, 2 * B])
        mid_mv = sb("mid_mv", [P, 2, B, 2])

        phase = ExitStack()

        def tmp(name, shape, dt=F32):
            return phase.enter_context(nc.sbuf_tensor(name, shape, dt))

        xt = tmp("xt", [P, 2, W])
        wst1 = tmp("wst1", [P, 2, 512])
        wg0_sb = tmp("wg0_sb", [P, E])
        zeros = tmp("zeros", [P, W])
        before = tmp("before", [P, P])
        ones = tmp("ones", [P, P])
        small = tmp("small", [P, 4, HH])
        ks = tmp("ks", [P, 24, HH])
        exp2 = tmp("exp2", [P, 2 * HH], mybir.dt.int32)
        th_hi = tmp("th_hi", [P, HH], F32R)
        route = tmp("route", [P, 8, E])
        slot_f = tmp("slot_f", [P, 2, T])
        expert_f = tmp("expert_f", [P, NC])
        kc = tmp("kc", [P, 2, 7, CH, LAGS])
        kg = tmp("kg", [P, 2, 4, CH, LO])
        k_out = tmp("k_out", [LO, 2, 2, CH, LO])
        tk = kc[:, 0].rearrange("p a b c -> p (a b c)")
        phase.close()

        phase = ExitStack()
        xc = tmp("xc", [P, 2, 4, P])
        xct_hi = tmp("xct_hi", [P, 2, W], F32R)
        xct_lo = tmp("xct_lo", [P, 2, W], F32R)
        wraw = tmp("wraw", [P, 2, WC])
        wc = tmp("wc", [P, 2, 2, WC], F32R)
        act = tmp("act", [P, 2, W])
        hid = tmp("hid", [P, J0, W])
        hid_hi = tmp("hid_hi", [P, J0, W], F32R)
        hid_lo = tmp("hid_lo", [P, J0, W], F32R)
        yo = tmp("yo", [P, 2, 4, P])
        phase.close()

        phase = ExitStack()
        fwd = tmp("fwd", [P, CT, 2, C])
        prod = tmp("prod", [P, 8, W])
        inv = tmp("inv", [P, M, 2, C])
        z = tmp("z", [P, M, 2, 2, W])
        khat = tmp("khat", [P, M, 4, P])
        xs = tmp("xs", [P, 2, W])
        xn1 = tmp("xn1", [P, 2, W])
        k_nat = z[:, 3, 0].rearrange("p a b -> p (a b)")
        k_t = z[:, 2, 0].rearrange("p a b -> p (a b)").rearrange("p (t h) -> p t h", h=P)
        phase.close()

        phase = ExitStack()
        xt1_hi = tmp("xt1_hi", [P, G, W], F32R)
        xt1_lo = tmp("xt1_lo", [P, G, W], F32R)
        attention = phase
        phase = ExitStack()
        qk_hi = tmp("qk_hi", [P, 2, L], F32R)
        qk_lo = tmp("qk_lo", [P, 2, L], F32R)
        v_hi = tmp("v_hi", [P, G, P], F32R)
        v_lo = tmp("v_lo", [P, G, P], F32R)
        prob = tmp("prob", [P, 2, L])
        pt_hi = tmp("pt_hi", [P, G, C], F32R)
        pt_lo = tmp("pt_lo", [P, G, C], F32R)
        sm = tmp("sm", [P, 2, 4])
        phase.close()

        phase = ExitStack()
        hid1 = tmp("hid1", [P, 4, W])
        hid1_hi = tmp("hid1_hi", [P, 4, W], F32R)
        hid1_lo = tmp("hid1_lo", [P, 4, W], F32R)
        gate_row1 = tmp("gate_row1", [P, 4, W])
        part1 = tmp("part1", [P, 2, W])
        final = tmp("final", [P, 2, W])
        phase.close()
        attention.close()

        lg, eq, k2, oh1, oh2, member, rank, count_a, count_b = (
            tk[:, i * T * E:(i + 1) * T * E].rearrange("p (t e) -> p t e", e=E) for i in range(9))
        m1, p1, m2, p2 = (tk[:, 9 * T * E + i * T:9 * T * E + (i + 1) * T] for i in range(4))
        ps = ctx.enter_context(nc.psum_tensor("ps", [P, 8, W], F32))

        x_in = [sem(f"x_in{g}") for g in range(G)]
        small_in = sem("small_in")
        stats_done = sem("stats_done")
        top2_done = sem("top2_done")
        gate2_done = sem("gate2_done")
        zeros_done = sem("zeros_done")
        zeros_out = sem("zeros_out")
        member_done = sem("member_done")
        counted = sem("counted")
        slots_done = sem("slots_done")
        scattered = sem("scattered")
        ident_done = sem("ident_done")
        pool_step = sem("pool_step")
        dve_step = sem("dve_step")
        trig_done = sem("trig_done")
        root_done = sem("root_done")
        top2_exp_done = sem("top2_exp_done")
        xn_ready = sem("xn_ready")
        xt_done = sem("xt_done")
        xt_copied = sem("xt_copied")
        logits_done = sem("logits_done")
        decay_done = sem("decay_done")
        phase_done = sem("phase_done")
        exp_done = sem("exp_done")
        sin_done = sem("sin_done")
        tables_done = sem("tables_done")
        k_mm_done = sem("k_mm_done")
        k_copied = sem("k_copied")
        k_stored = [sem(f"k_stored{i}") for i in range(2)]
        xc_in = [sem(f"xc_in{i}") for i in range(2)]
        wraw_in = [sem(f"wraw_in{i}") for i in range(2)]
        xct_done = sem("xct_done")
        xct_hi_done = sem("xct_hi_done")
        xct_lo_done = sem("xct_lo_done")
        up_hi_done = sem("up_hi_done")
        up_lo_done = sem("up_lo_done")
        down_hi_done = sem("down_hi_done")
        down_lo_done = sem("down_lo_done")
        up_done = sem("up_done")
        act_done = sem("act_done")
        hid_done = sem("hid_done")
        hid_lo_done = sem("hid_lo_done")
        chunk_done = sem("chunk_done")
        y_half_copied = sem("y_half_copied")
        y_copied = sem("y_copied")
        y_stored = [sem(f"y_stored{i}") for i in range(2)]
        first_in = sem("first_in")
        second_in = [sem(f"second_in{g}") for g in range(G)]

        kernel_in = sem("kernel_in")
        fwd_in = sem("fwd_in")
        inv_in = sem("inv_in")
        rows_in = sem("rows_in")
        xs_in0 = sem("xs_in0")
        xs_in1 = sem("xs_in1")
        k_t_done = sem("k_t_done")
        k_t_copied = sem("k_t_copied")
        khat_mm = sem("khat_mm")
        khat_copied = sem("khat_copied")
        khat_ready = sem("khat_ready")
        x_hat_done = sem("x_hat_done")
        products_done = sem("products_done")
        z_ready = sem("z_ready")
        wst1_in0 = sem("wst1_in0")
        wst1_in1 = sem("wst1_in1")
        w1_hi_done = sem("w1_hi_done")
        w1_lo_done = sem("w1_lo_done")
        skip_done = sem("skip_done")
        y_done = sem("y_done")
        r_done = sem("r_done")
        mid_stats = sem("mid_stats")
        root1_done = sem("root1_done")
        norm1_done = sem("norm1_done")
        scaled_done = sem("scaled_done")
        xb_done = sem("xb_done")
        x1_done = sem("x1_done")
        mid_stats2 = sem("mid_stats2")
        root2_done = sem("root2_done")
        xn1_done = sem("xn1_done")
        xt1_done = sem("xt1_done")
        xt1_hi_done = sem("xt1_hi_done")
        xt1_lo_done = sem("xt1_lo_done")
        logits1_done = sem("logits1_done")
        logits1_read = sem("logits1_read")
        gates_out = sem("gates_out")
        gate_exp_done = sem("gate_exp_done")
        gate_soft = sem("gate_soft")
        gates1_done = sem("gates1_done")
        gates1_turned = sem("gates1_turned")
        gates1_copied = sem("gates1_copied")
        qkv_mm = sem("qkv_mm")
        qkv_hi_done = sem("qkv_hi_done")
        qkv_lo_done = sem("qkv_lo_done")
        s_done = sem("s_done")
        max_done = sem("max_done")
        exp1_done = sem("exp1_done")
        prob_done = sem("prob_done")
        pt_done = sem("pt_done")
        pt_hi_done = sem("pt_hi_done")
        pt_lo_done = sem("pt_lo_done")
        pv_done = sem("pv_done")
        pv_copied = sem("pv_copied")
        up1_done = sem("up1_done")
        hid1_done = sem("hid1_done")
        hid1_lo_done = sem("hid1_lo_done")
        expert1_done = sem("expert1_done")
        part1_done = sem("part1_done")
        join1_done = sem("join1_done")
        gate1_in0 = sem("gate1_in0")
        gate1_in1 = sem("gate1_in1")
        gate1_in2 = sem("gate1_in2")
        gate1_in3 = sem("gate1_in3")
        final_done = sem("final_done")
        added_done = sem("added_done")
        stored = [sem(f"stored{n}") for n in range(2)]
        row_step = sem("row_step")
        gate1_in = [gate1_in0, gate1_in1, gate1_in2, gate1_in3]
        xs_in = [xs_in0, xs_in1]
        wst1_in = [wst1_in0, wst1_in1]

        block = ctx.enter_context(nc.Block())

        def all_chunks(engine, body):
            body(0, 0, 0)
            with engine.Fori(0, (NC - 3) // 2) as i:
                body(i * 2 + 1, i, 1)
                body(i * 2 + 2, i + 1, 0)
            body(NC - 2, (NC - 2) // 2, 1)
            body(NC - 1, (NC - 1) // 2, 0)

        is_first = lambda q: isinstance(q, int) and q == 0
        is_last = lambda q: isinstance(q, int) and q == NC - 1
        y_parts = ps[:, 4:6].rearrange("p a (t i c) -> p (a t) i c", t=2, i=2)
        width0 = lambda j: min(P, HID0 - j * P)

        pieces1 = [(wqkv, lambda a: a.rearrange("p (k e) -> p k e", k=3), QKV, 3 * P), (wg1, lambda a: a, GATE1, GW)]
        for e in range(E):
            pieces1.append((w1_1[e], lambda a: a, e * HID1, HID1))
            pieces1.append((w2_1[e].rearrange("(j f) d -> f j d", j=J1), lambda a: a.rearrange("p (j d) -> p j d", j=J1),
                            E * HID1 + e * HID1, HID1))

        def qkv_dst(qk, v, i):
            return qk[:, i // 2, (i % 2) * C:(i % 2 + 1) * C] if i < 4 else v[:, 4 * (i - 4):4 * (i - 3)]

        def turned_dst(pt, n, a):
            return pt[:, 4 * a:4 * a + 4, (n % 4) * P:(n % 4 + 1) * P]

        def turned_src(a):
            return ps[:, 4 + a].rearrange("p (t j) -> p t j", t=4)

        def qkv_src(n):
            bank = ps[:, 6 + n % 2]
            return bank if n % 6 < 4 else bank.rearrange("p (t e) -> p t e", t=4)

        @block.sync
        def _(sp):
            for g in range(G):
                sp.dma_start(xn[:, g, :].rearrange("p (b h) -> p b h", b=B),
                             x[:, g * P:(g + 1) * P, :].rearrange("b p h -> p b h")).then_inc(x_in[g], 16)
            sp.dma_start(small[:], state_params).then_inc(small_in, 16)
            for half in range(2):
                sp.dma_start(ks[half * N:(half + 1) * N, 0, :],
                             log_dt[half * HH:(half + 1) * HH].partition_broadcast(N)).then_inc(small_in, 16)
            sp.dma_start(consts[:], lag_row.partition_broadcast(P)).then_inc(small_in, 16)
            sp.dma_start(wg0_sb[:], wg0).then_inc(small_in, 16)
            sp.wait_ge(zeros_done, 1)
            sp.dma_start(x_slots.rearrange("(p r) h -> p (r h)", p=P).rearrange("p (a w) -> p a w", w=W),
                         zeros[:].unsqueeze(1).broadcast_to((P, NC, W))).then_inc(zeros_out, 16)
            for n, (src, view, col, cols) in enumerate(pieces1):
                if n >= 2:
                    sp.wait_ge(w1_lo_done, n - 1)
                sp.dma_start(view(wst1[:, n % 2, 0:cols]), src).then_inc(wst1_in[n % 2], 16)
            sp.dma_start(vec_rows[:, 0], skip.partition_broadcast(P)).then_inc(rows_in, 16)
            sp.dma_start(vec_rows[:, 1], ln_w.partition_broadcast(P)).then_inc(rows_in, 16)
            sp.dma_start(vec_rows[:, 2], ln_b.partition_broadcast(P)).then_inc(rows_in, 16)
            sp.dma_start(bias1[:], gate_bias.partition_broadcast(P)).then_inc(rows_in, 16)
            sp.dma_start(b1_sb[:], b1).then_inc(rows_in, 16)
            sp.dma_start(b2_sb[:], b2).then_inc(rows_in, 16)
            for c in range(KC):
                sp.wait_ge(k_copied, 2 * c + 2)
                for half in range(2):
                    heads = half * HH + c * CH
                    sp.dma_start(kernel_dram[heads:heads + CH].rearrange("j m n -> m j n"),
                                 k_out[:, c % 2, half]).then_inc(k_stored[c % 2], 16)
            for n in range(2):
                sp.wait_ge(k_stored[n], 16 * KC)

            rows_of = lambda a, q: a[bass.ds(q * W, W)].rearrange("(p t) h -> p t h", t=4)

            def x_load(q, s):
                sp.dma_start(xc[:, s], rows_of(x_slots, q)).then_inc(xc_in[s], 16)

            def w_load(q, s):
                e = sp.value_load(expert_of[0:1, bass.ds(q, 1)], min_val=0, max_val=E - 1)
                sp.dma_start(wraw[:, s], w0[bass.ds(e, 1)].rearrange("a p w -> p (a w)")).then_inc(wraw_in[s], 16)

            sp.wait_ge(slots_done, 3)
            sp.wait_ge(tables_done, 2 * KC)
            sp.wait_ge(w1_lo_done, len(pieces1))
            for q in range(2):
                w_load(q, q)
            sp.wait_ge(scattered, 16 * 2 * T)
            for q in range(2):
                x_load(q, q)
                sp.sem_inc(y_stored[q], 16)

            def y_store(q, s):
                sp.wait_ge(y_copied, q + 1)
                sp.dma_start(rows_of(y_slots, q), yo[:, s]).then_inc(y_stored[s], 16)

            def chunk_loads(q, k, s):
                if not (isinstance(q, int) and q + 2 >= NC):
                    sp.wait_ge(xct_done, q + 1)
                    x_load(q + 2, s)
                    sp.wait_ge(up_lo_done, q + 1)
                    sp.wait_ge(down_lo_done, q + 1)
                    w_load(q + 2, s)
                if not is_first(q):
                    y_store(q - 1, 1 - s)

            all_chunks(sp, chunk_loads)
            y_store(NC - 1, 0)

            sp.wait_ge(chunk_done, NC)
            sp.dma_start(k_nat, kernel_dram.rearrange("h m n -> h (m n)")).then_inc(kernel_in, 16)
            sp.dma_start(fwd[:], dft_fwd).then_inc(fwd_in, 16)
            sp.dma_start(inv[:], dft_inv).then_inc(inv_in, 16)
            for g in range(G):
                if g >= 2:
                    sp.wait_ge(x1_done, g - 1)
                sp.dma_start(xs[:, g % 2].rearrange("p (b h) -> p b h", b=B),
                             x[:, g * P:(g + 1) * P, :].rearrange("b p h -> p b h")).then_inc(xs_in[g % 2], 16)
            sp.wait_ge(gates1_copied, 1)
            sp.dma_start(gates_dram.rearrange("(a t) e p -> (t e) a p", a=2), gates_t[:]).then_inc(gates_out, 16)
            sp.wait_ge(gates_out, 16)
            sp.wait_ge(up1_done, 1)
            sp.wait_ge(pv_copied, 2 * B)

            def gate1_load(g, e):
                src = gates_dram[bass.ds(g * B, B), e, :].partition_broadcast(P)
                sp.dma_start(gate_row1[:, e % 4, :].rearrange("p (b t) -> p b t", b=B), src).then_inc(gate1_in[e % 4], 16)

            for e in range(4):
                gate1_load(0, e)

            def gate1_loads(g, last):
                for e in range(E):
                    sp.wait_ge(part1_done, g * E + e + 1)
                    if e < 4:
                        gate1_load(g, e + 4)
                    elif not last:
                        gate1_load(g + 1, e - 4)
                    if last and e < G - 1:
                        store(e)

            def store(g):
                sp.wait_ge(added_done, g + 1)
                sp.dma_start(out[:, g * P:(g + 1) * P, :].rearrange("b p h -> p b h"),
                             final[:, g % 2].rearrange("p (b h) -> p b h", b=B)).then_inc(stored[g % 2], 16)

            with sp.Fori(0, G - 1) as g:
                gate1_loads(g, False)
            gate1_loads(G - 1, True)
            store(G - 1)
            for n in range(2):
                sp.wait_ge(stored[n], 16 * G // 2)

        @block.gpsimd
        def _(pool):
            nc.gpsimd.memset(zeros[:], 0.0).then_inc(zeros_done, 1)
            nc.gpsimd.memset(ident[:], 0.0).then_inc(pool_step, 1)
            nc.gpsimd.memset(before[:], 1.0).then_inc(pool_step, 1)
            nc.gpsimd.memset(ones[:], 1.0).then_inc(pool_step, 1)
            pool.wait_ge(pool_step, 3)
            nc.gpsimd.affine_select(out=ident[:], in_=ident[:], compare_op=ALU.not_equal, fill=1.0, base=0,
                                    pattern=[[-1, P]], channel_multiplier=1).then_inc(ident_done, 1)
            nc.gpsimd.affine_select(out=before[:], in_=before[:], compare_op=ALU.is_gt, fill=0.0, base=0,
                                    pattern=[[1, P]], channel_multiplier=-1).then_inc(ident_done, 1)
            for n, (_, _, col, cols) in enumerate(pieces1):
                pool.wait_ge(w1_hi_done, n + 1)
                nc.gpsimd.tensor_tensor(w_lo[:, col:col + cols], wst1[:, n % 2, 0:cols],
                                        w_hi[:, col:col + cols].bitcast(F32), ALU.subtract).then_inc(w1_lo_done, 1)
            pool.wait_ge(rows_in, 96)
            nc.gpsimd.tensor_scalar(vec_rows[:, 0], vec_rows[:, 0], 1.0, None, ALU.add).then_inc(row_step, 1)

            of_slots = lambda k, t: bass.IndirectOffsetOnAxis(ap=slot[:, k, t:t + 1], axis=0)
            rows = lambda a, t: a[:, t // B, (t % B) * P:(t % B + 1) * P]
            pool.wait_ge(zeros_out, 16)
            pool.wait_ge(slots_done, 3)
            for t in range(T):
                for k in range(2):
                    nc.gpsimd.indirect_dma_start(x_slots, of_slots(k, t), rows(xn, t), None).then_inc(scattered, 16)

            def hidden_low(q, j):
                pool.wait_ge(hid_done, q * J0 + j + 1)
                f = width0(j)
                nc.gpsimd.tensor_tensor(hid_lo[0:f, j], hid[0:f, j], hid_hi[0:f, j].bitcast(F32),
                                        ALU.subtract).then_inc(hid_lo_done, 1)

            def up_low(q, s):
                pool.wait_ge(up_hi_done, q + 1)
                nc.gpsimd.tensor_tensor(wc[:, s, 1, 0:WA], wraw[:, s, 0:WA], wc[:, s, 0, 0:WA].bitcast(F32),
                                        ALU.subtract).then_inc(up_lo_done, 1)

            def chunk_low(q, k, s):
                hidden_low(q, 0)
                if not is_last(q):
                    up_low(q + 1, 1 - s)
                hidden_low(q, 1)
                hidden_low(q, 2)

            up_low(0, 0)
            all_chunks(pool, chunk_low)

            for n in range(2):
                pool.wait_ge(y_stored[n], 16 * (1 + (NC + 1 - n) // 2))
            for t in range(T):
                nc.gpsimd.indirect_dma_start(rows(acc, t), None, y_slots, of_slots(0, t)).then_inc(first_in, 16)
            pool.wait_ge(z_ready, M)

            def second_outputs(g):
                for t in range(g * B, (g + 1) * B):
                    nc.gpsimd.indirect_dma_start(rows(prod, t), None, y_slots, of_slots(1, t)).then_inc(second_in[g], 16)

            second_outputs(0)
            pool.wait_ge(x_hat_done, M)
            pool.wait_ge(row_step, 1)
            row = lambda i: vec_rows[:, i].unsqueeze(1).broadcast_to((P, B, P))
            for_batch = lambda a: a.rearrange("p (b h) -> p b h", b=B)

            def skip_term(g):
                nc.gpsimd.tensor_tensor(for_batch(xn[:, g]), for_batch(xn[:, g]), row(0), ALU.mult).then_inc(skip_done, 1)

            skip_term(0)
            for g in range(G):
                if g + 1 < G:
                    skip_term(g + 1)
                pool.wait_ge(xs_in[g % 2], 16 * (g // 2 + 1))
                nc.gpsimd.tensor_tensor(for_batch(xs[:, g % 2]), for_batch(xs[:, g % 2]), row(2), ALU.add).then_inc(xb_done, 1)
                if g + 1 < G:
                    second_outputs(g + 1)
                pool.wait_ge(norm1_done, g + 1)
                nc.gpsimd.tensor_tensor(for_batch(xn[:, g]), for_batch(xn[:, g]), row(1), ALU.mult).then_inc(scaled_done, 1)

        @block.scalar
        def _(act_e):
            copy = lambda dst, src: nc.scalar.activation(dst, src, ACT.Copy)
            w_next = [0]

            def weights(count):
                for n in range(w_next[0], min(w_next[0] + count, len(pieces1))):
                    _, _, col, cols = pieces1[n]
                    act_e.wait_ge(wst1_in[n % 2], 16 * (n // 2 + 1))
                    copy(w_hi[:, col:col + cols], wst1[:, n % 2, 0:cols]).then_inc(w1_hi_done, 1)
                    w_next[0] = n + 1

            act_e.wait_ge(stats_done, 1)
            nc.scalar.activation(rstd[:], mv[:, :, 1], ACT.Sqrt, bias=eps[:]).then_inc(root_done, 1)
            for g in range(G):
                act_e.wait_ge(xt_done, g + 1)
                copy(xt[:, g % 2], ps[:, g % 2]).then_inc(xt_copied, 1)
                weights(1)
            act_e.wait_ge(decay_done, 1)
            nc.scalar.activation(ks[:, 5], ks[:, 4], ACT.Tanh, scale=0.5).then_inc(trig_done, 1)
            nc.scalar.activation(ks[:, 6], ks[:, 4], ACT.Exp).then_inc(trig_done, 1)
            act_e.wait_ge(top2_done, 1)
            nc.scalar.activation(p2, m2, ACT.Exp).then_inc(top2_exp_done, 1)
            act_e.wait_ge(phase_done, 1)
            nc.scalar.activation(ks[:, 7], ks[:, 12], ACT.Sin, scale=TWO_PI).then_inc(trig_done, 1)
            nc.scalar.activation(ks[:, 8], ks[:, 12], ACT.Sin, scale=TWO_PI / 2).then_inc(trig_done, 1)
            weights(len(pieces1))

            def k_copy(c):
                for half in range(2):
                    act_e.wait_ge(k_mm_done, 2 * c + half + 1)
                    if c >= 2 and half == 0:
                        act_e.wait_ge(k_stored[c % 2], 32 * (c // 2))
                    copy(k_out[:, c % 2, half], ps[0:LO, 4 + 2 * (c % 2) + half].rearrange("p (a b) -> p a b", a=CH)).then_inc(k_copied, 1)

            for c in range(KC):
                s = c % 2
                act_e.wait_ge(decay_done, c + 2)
                nc.scalar.activation(kc[:, s, 3], kc[:, s, 3], ACT.Exp).then_inc(exp_done, 1)
                act_e.wait_ge(phase_done, c + 2)
                nc.scalar.activation(kc[:, s, 4], kc[:, s, 0], ACT.Sin, scale=TWO_PI).then_inc(sin_done, 1)
                nc.scalar.activation(kc[:, s, 5], kc[:, s, 0], ACT.Sin, scale=TWO_PI / 2).then_inc(sin_done, 1)
                act_e.wait_ge(sin_done, 3 * c + 2)
                nc.scalar.activation(kc[:, s, 5], kc[:, s, 5], ACT.Square).then_inc(sin_done, 1)
                if c >= 1:
                    k_copy(c - 1)
            k_copy(KC - 1)

            def up_high(q, k, s):
                act_e.wait_ge(wraw_in[s], (k + 1) * 16)
                copy(wc[:, s, 0, 0:WA], wraw[:, s, 0:WA]).then_inc(up_hi_done, 1)

            def down_high(q, s):
                if not (isinstance(q, int) and q < 2):
                    act_e.wait_ge(chunk_done, q - 1)
                copy(wc[:, s, 0, WA:WC], wraw[:, s, WA:WC]).then_inc(down_hi_done, 1)

            def input_high(q, s):
                act_e.wait_ge(xct_done, q + 1)
                copy(xct_hi[:, s], ps[:, 6]).then_inc(xct_hi_done, 1)

            def output_half(q, k, s):
                act_e.wait_ge(chunk_done, q + 1)
                act_e.wait_ge(y_stored[s], (k + 1) * 16)
                copy(yo[:, s], y_parts[:, :, 1]).then_inc(y_half_copied, 1)

            def chunk_act(q, k, s):
                for j in range(J0):
                    f, r = width0(j), (s + j) % 2
                    act_e.wait_ge(up_done, q * J0 + j + 1)
                    nc.scalar.activation(act[0:f, r], ps[0:f, r], ACT.Silu).then_inc(act_done, 1)
                    if j == 1 and not is_first(q):
                        output_half(q - 1, k - (1 - s), 1 - s)
                    if is_last(q):
                        continue
                    if j == 0:
                        up_high(q + 1, k + s, 1 - s)
                    elif j == 1:
                        input_high(q + 1, 1 - s)
                    else:
                        down_high(q + 1, 1 - s)

            act_e.wait_ge(tables_done, 2 * KC)
            act_e.wait_ge(w1_lo_done, len(pieces1))
            up_high(0, 0, 0)
            down_high(0, 0)
            input_high(0, 0)
            all_chunks(act_e, chunk_act)
            output_half(NC - 1, (NC - 1) // 2, 0)

            act_e.wait_ge(k_t_done, 1)
            for a in range(2):
                copy(k_t[:, 4 * a:4 * a + 4], ps[:, a].rearrange("p (t h) -> p t h", t=4)).then_inc(k_t_copied, 1)
            for m in range(M):
                act_e.wait_ge(khat_mm, m + 1)
                copy(khat[:, m].rearrange("p (c r) h -> p r c h", c=2),
                     ps[:, 4 + m].rearrange("p (r c h) -> p r c h", r=2, c=2)).then_inc(khat_copied, 1)

            def root(i, signal, wait):
                act_e.wait_ge(*wait)
                nc.scalar.activation(mid[:, 2 * i, 0:B], mid_mv[:, i, :, 1], ACT.Sqrt, bias=eps[:]).then_inc(signal, 1)

            def high_part(g):
                act_e.wait_ge(xt1_done, g + 1)
                copy(xt1_hi[:, g], ps[:, 4 + g % 2]).then_inc(xt1_hi_done, 1)

            for g in range(G):
                root(0, root1_done, (mid_stats, g + 1))
                if g >= 1:
                    high_part(g - 1)
                root(1, root2_done, (mid_stats2, g + 1))
            high_part(G - 1)

            def qkv_high(n):
                b, i = divmod(n, 6)
                act_e.wait_ge(qkv_mm, n + 1)
                copy(qkv_dst(qk_hi, v_hi, i), qkv_src(n)).then_inc(qkv_hi_done, 1)

            def turned_high(n):
                for a in range(2):
                    act_e.wait_ge(pt_done, 2 * n + a + 1)
                    copy(turned_dst(pt_hi, n, a), turned_src(a)).then_inc(pt_hi_done, 1)

            def softmax_exp(n):
                act_e.wait_ge(max_done, n + 1)
                nc.scalar.activation(prob[:, n % 2], ps[:, 2 * (n % 2):2 * (n % 2) + 2].rearrange("p a w -> p (a w)"), ACT.Exp,
                                     bias=sm[:, n % 2, 1:2], scale=SCALE, accum_out=sm[:, n % 2, 2:3]).then_inc(exp1_done, 1)

            for i in range(6):
                qkv_high(i)
            softmax_exp(0)
            for n in range(B * G):
                if n == 2:
                    act_e.wait_ge(gate_soft, 1)
                    nc.scalar.activation(gl[:, :, 0:E], gl[:, :, 0:E], ACT.Exp).then_inc(gate_exp_done, 1)
                    nc.scalar.activation(gl[:, :, E:E + 1], gl[:, :, E:E + 1], ACT.Tanh, scale=0.5).then_inc(gate_exp_done, 1)
                if n == 5:
                    act_e.wait_ge(gates1_turned, 1)
                    copy(gates_t[:], ps[:, 7, 0:2 * P].rearrange("p (a t) -> p a t", a=2)).then_inc(gates1_copied, 1)
                b, jt = divmod(n, G)
                turned_high(n)
                if n + 1 < B * G:
                    softmax_exp(n + 1)
                if jt == G - 2 and b + 1 < B:
                    for i in range(4):
                        qkv_high(6 * (b + 1) + i)
                if jt % 4 == 3:
                    jb = jt // 4
                    act_e.wait_ge(pv_done, 2 * b + jb + 1)
                    copy(acc[:, 4 * jb:4 * jb + 4, b * P:(b + 1) * P],
                         ps[:, 6].rearrange("p (t j) -> p t j", t=4)).then_inc(pv_copied, 1)
                    if jb == 1 and b + 1 < B:
                        for i in range(4, 6):
                            qkv_high(6 * (b + 1) + i)

            def hidden1(g):
                for u in range(UN1):
                    act_e.wait_ge(up1_done, g * UN1 + u + 1)
                    nc.scalar.activation(hid1[:, u % 4], ps[:, u % 4], ACT.Gelu_apprx_tanh, bias=b1_sb[:, u:u + 1])
                    nc.scalar.activation(hid1_hi[:, u % 4], ps[:, u % 4], ACT.Gelu_apprx_tanh,
                                         bias=b1_sb[:, u:u + 1]).then_inc(hid1_done, 1)

            with act_e.Fori(0, G) as g:
                hidden1(g)

        @block.vector
        def _(dve):
            step = Tally(dve_step)
            need = lambda v: dve.wait_ge(dve_step, v)
            tt, ts, stt = nc.vector.tensor_tensor, nc.vector.tensor_scalar, nc.vector.scalar_tensor_tensor
            mul, add, sub = ALU.mult, ALU.add, ALU.subtract
            K = lambda i: ks[:, i]
            a_im, c_re, c_im = small[:, 1], small[:, 2], small[:, 3]
            step.mark(nc.vector.memset(eps[:], LN_EPS))

            def inverse_root(r, var, t):
                v = step.mark(nc.vector.reciprocal(r, r))
                need(v)
                v = step.mark(tt(t, r, r, mul))
                need(v)
                v = step.mark(stt(t, var, LN_EPS, t, add, mul))
                need(v)
                v = step.mark(ts(t, t, -0.5, 1.5, mul, add))
                need(v)
                v = step.mark(tt(r, r, t, mul))
                need(v)

            for g in range(G):
                dve.wait_ge(x_in[g], 16)
                for b in range(B):
                    st = (g % 2) * B + b
                    v = step.mark(nc.vector.bn_stats(stats[:, st], xn[:, g, b * P:(b + 1) * P]))
                need(v)
                for b in range(B):
                    last = nc.vector.bn_aggr(mv[:, g * B + b], stats[:, (g % 2) * B + b])
            last.then_inc(stats_done, 1)
            dve.wait_ge(root_done, 1)
            inverse_root(rstd[:], mv[:, :, 1], newton[:])
            for g in range(G):
                for b in range(B):
                    t = g * B + b
                    v = nc.vector.tensor_scalar(xn[:, g, b * P:(b + 1) * P], xn[:, g, b * P:(b + 1) * P],
                                                mv[:, t, 0:1], rstd[:, t:t + 1], sub, mul)
                v.then_inc(xn_ready, 1)

            dve.wait_ge(small_in, 80)
            step.mark(nc.vector.tensor_copy(ks[:, 1], ks[:, 0]))
            v = step.mark(nc.vector.tensor_copy(ks[:, 2], small[:, 0]))
            pair = lambda i: ks[:, i:i + 2]
            X, NN, R, PP = pair(1), pair(5), pair(7), pair(9)
            need(v)
            v = step.mark(ts(X, X, 88.0, -87.0, ALU.min, ALU.max))
            need(v)
            v = step.mark(ts(NN, X, 1.0 / math.log(2.0), None, mul))
            need(v)
            v = step.mark(ts(NN, NN, MAGIC, MAGIC, add, sub))
            need(v)
            v = step.mark(stt(R, NN, -LN2_HI, X, mul, add))
            need(v)
            v = step.mark(stt(R, NN, -LN2_LO, R, mul, add))
            need(v)
            v = step.mark(ts(PP, R, 1.0 / math.factorial(7), None, mul))
            for k in range(6, 0, -1):
                need(v)
                v = step.mark(stt(PP, PP, 1.0 / math.factorial(k), R, add, mul))
            power = exp2[:].rearrange("p (a h) -> p a h", a=2)
            v = step.mark(ts(power, NN, 127.0, 2.0 ** 23, add, mul))
            need(v)
            v = step.mark(stt(X, PP, 1.0, power.bitcast(F32), add, mul))
            need(v)
            s_th = step.mark(tt(K(9), K(1), a_im, mul))
            step.mark(ts(K(3), K(2), -1.0, None, mul))
            nc.vector.scalar_tensor_tensor(K(4), K(2), -1.0, K(1), mul, mul).then_inc(decay_done, 1)
            need(s_th)
            v = step.mark(nc.vector.tensor_copy(th_hi[:], K(9)))
            need(v)
            step.mark(tt(K(10), K(9), th_hi[:].bitcast(F32), sub))
            v = step.mark(ts(K(11), th_hi[:].bitcast(F32), INV_2PI_HI, None, mul))
            need(v)
            v = step.mark(ts(K(12), K(11), MAGIC, MAGIC, add, sub))
            need(v)
            step.mark(tt(K(11), K(11), K(12), sub))
            v = step.mark(ts(K(13), K(10), INV_2PI_HI, None, mul))
            need(v)
            v = step.mark(stt(K(13), K(9), INV_2PI_LO, K(13), mul, add))
            need(v)
            v = step.mark(tt(K(14), K(11), K(13), add))
            need(v)
            v = step.mark(ts(K(15), K(14), MAGIC_13, MAGIC_13, add, sub))
            need(v)
            v = step.mark(tt(K(11), K(11), K(15), sub))
            need(v)
            v = step.mark(tt(K(16), K(11), K(13), add))
            step.mark(ts(K(12), K(14), MAGIC, MAGIC, add, sub))
            need(step.n)
            nc.vector.tensor_tensor(K(12), K(14), K(12), sub).then_inc(phase_done, 1)
            wide = lambda a: a.unsqueeze(2).broadcast_to((P, T, E))
            revb = rev.unsqueeze(1).broadcast_to((P, T, E))
            dve.wait_ge(logits_done, G)
            v = step.mark(nc.vector.tensor_copy(lg, ps[:, 2, 0:T * E].rearrange("p (t e) -> p t e", e=E)))
            need(v)
            for m, p, oh, low in ((m1, p1, oh1, False), (m2, p2, oh2, True)):
                v = step.mark(nc.vector.reduce_max(m, lg, AX.X))
                need(v)
                v = step.mark(tt(eq, lg, wide(m), ALU.is_equal))
                need(v)
                v = step.mark(tt(k2, eq, revb, mul))
                need(v)
                v = step.mark(nc.vector.reduce_max(p, k2, AX.X))
                need(v)
                v = step.mark(tt(oh, k2, wide(p), ALU.is_equal))
                need(v)
                if not low:
                    v = step.mark(stt(lg, oh, -3.0e38, lg, mul, add))
                    need(v)
            tt(m2, m2, m1, sub).then_inc(top2_done, 1)
            tt(member, oh1, oh2, add).then_inc(member_done, 1)
            dve.wait_ge(top2_exp_done, 1)
            v = step.mark(ts(p1, p2, 1.0, None, add))
            need(v)
            v = step.mark(nc.vector.reciprocal(p1, p1))
            need(v)
            tt(p2, p2, p1, mul).then_inc(gate2_done, 1)
            step.mark(nc.vector.tensor_copy(gate2[:, 0], p1))
            dve.wait_ge(gate2_done, 1)
            step.mark(nc.vector.tensor_copy(gate2[:, 1], p2))

            dve.wait_ge(counted, 1)
            before_in_tile = ps[:, 3, 0:T * E].rearrange("p (t e) -> p t e", e=E)
            in_tile = ps[:, 3, T * E:2 * T * E].rearrange("p (t e) -> p t e", e=E)
            v = step.mark(nc.vector.tensor_copy(count_a, in_tile))
            step.mark(nc.vector.tensor_copy(rank, before_in_tile))
            src, dst, d = count_a, count_b, 1
            while d < T:
                need(step.n)
                step.mark(nc.vector.tensor_copy(dst[:, 0:d], src[:, 0:d]))
                step.mark(tt(dst[:, d:], src[:, d:], src[:, :T - d], add))
                src, dst, d = dst, src, 2 * d
            need(step.n)
            v = step.mark(tt(dst, src, in_tile, sub))
            R_ = lambda i: route[:, i]
            step.mark(ts(R_(0), src[:, T - 1], 1.0 / W, (W - 1) / 2.0 / W, mul, add))
            need(step.n)
            step.mark(tt(rank, rank, dst, add))
            v = step.mark(ts(R_(0), R_(0), MAGIC, MAGIC, add, sub))
            need(v)
            a, b_, d = 0, 1, 1
            while d < E:
                need(step.n)
                step.mark(nc.vector.tensor_copy(R_(b_)[:, 0:d], R_(a)[:, 0:d]))
                step.mark(tt(R_(b_)[:, d:], R_(a)[:, d:], R_(a)[:, :E - d], add))
                a, b_, d = b_, b_ + 1, 2 * d
            need(step.n)
            v = step.mark(tt(R_(5), R_(a), R_(0), sub))
            need(v)
            v = step.mark(ts(R_(5), R_(5), float(W), None, mul))
            need(v)
            v = step.mark(tt(rank, rank, R_(5).unsqueeze(1).broadcast_to((P, T, E)), add))
            need(v)
            step.mark(tt(oh1, oh1, rank, mul))
            v = step.mark(tt(oh2, oh2, rank, mul))
            need(v)
            step.mark(nc.vector.reduce_sum(slot_f[:, 0], oh1, AX.X))
            v = step.mark(nc.vector.reduce_sum(slot_f[:, 1], oh2, AX.X))
            done = eq.rearrange("p t e -> p (t e)")[:, 0:NC * E].rearrange("p (q e) -> p q e", e=E)
            v2 = step.mark(tt(done, lagv[:, 0:NC].unsqueeze(2).broadcast_to((P, NC, E)),
                              R_(a).unsqueeze(1).broadcast_to((P, NC, E)), ALU.is_ge))
            need(v2)
            nc.vector.tensor_copy(slot[:, 0], slot_f[:, 0]).then_inc(slots_done, 1)
            nc.vector.tensor_copy(slot[:, 1], slot_f[:, 1]).then_inc(slots_done, 1)
            v = step.mark(nc.vector.reduce_sum(expert_f[:], done, AX.X))
            need(v)
            ts(expert_of[:], expert_f[:], float(E - 1), None, ALU.min).then_inc(slots_done, 1)

            step.mark(tt(K(17), K(3), K(3), mul))
            v = step.mark(tt(K(18), a_im, a_im, mul))
            need(v)
            v = step.mark(tt(K(17), K(17), K(18), add))
            need(v)
            v = step.mark(nc.vector.reciprocal(K(17), K(17)))
            need(v)
            v = step.mark(ts(K(17), K(17), 2.0 / C, None, mul))
            dve.wait_ge(trig_done, 4)
            step.mark(tt(K(8), K(8), K(8), mul))
            step.mark(tt(K(7), K(7), K(6), mul))
            v = step.mark(stt(K(5), K(6), 1.0, K(5), add, mul))
            need(v)
            v = step.mark(tt(K(8), K(8), K(6), mul))
            need(v)
            v = step.mark(stt(K(8), K(8), -2.0, K(5), mul, add))
            need(v)
            step.mark(tt(K(18), K(8), K(3), mul))
            step.mark(tt(K(19), K(7), a_im, mul))
            step.mark(tt(K(20), K(7), K(3), mul))
            v = step.mark(tt(K(21), K(8), a_im, mul))
            need(v)
            step.mark(tt(K(18), K(18), K(19), add))
            v = step.mark(tt(K(20), K(20), K(21), sub))
            need(v)
            step.mark(tt(K(18), K(18), K(17), mul))
            v = step.mark(tt(K(20), K(20), K(17), mul))
            need(v)
            step.mark(tt(K(19), c_re, K(18), mul))
            step.mark(tt(K(21), c_im, K(20), mul))
            step.mark(tt(K(22), c_re, K(20), mul))
            v = step.mark(tt(K(23), c_im, K(18), mul))
            need(v)
            step.mark(tt(K(19), K(19), K(21), sub))
            v = step.mark(tt(K(22), K(22), K(23), add))
            need(v)
            v = step.mark(ts(K(21), K(19), -1.0, None, mul))
            FH, FL, AR, CTR, CTI, NCTR = K(15), K(16), K(4), K(19), K(22), K(21)

            lag = lagv.unsqueeze(1).broadcast_to((P, CH, LAGS))
            lo, hi = slice(0, LO), slice(LO, LAGS)

            def angles(c):
                k = lambda i: kc[:, c % 2, i]
                col = lambda a: a[:, c * CH:(c + 1) * CH].unsqueeze(2).broadcast_to((P, CH, LAGS))
                if c >= 2:
                    dve.wait_ge(k_mm_done, 2 * c - 2)
                v1 = step.mark(tt(k(0), col(FH), lag, mul))
                v2 = step.mark(tt(k(2), col(FL), lag, mul))
                tt(k(3), col(AR), lag, mul).then_inc(decay_done, 1)
                need(v1)
                v1 = step.mark(ts(k(1), k(0), MAGIC, MAGIC, add, sub))
                need(v1)
                v1 = step.mark(tt(k(0), k(0), k(1), sub))
                need(v1)
                v1 = step.mark(tt(k(0), k(0), k(2), add))
                need(v1)
                v1 = step.mark(ts(k(1), k(0), MAGIC, MAGIC, add, sub))
                need(v1)
                tt(k(0), k(0), k(1), sub).then_inc(phase_done, 1)

            def powers(c):
                k = lambda i: kc[:, c % 2, i]
                g_ = lambda i: kg[:, c % 2, i]
                col = lambda a: a[:, c * CH:(c + 1) * CH].unsqueeze(2).broadcast_to((P, CH, LO))
                dve.wait_ge(sin_done, 3 * c + 3)
                v1 = step.mark(ts(k(1), k(5), -2.0, 1.0, mul, add))
                dve.wait_ge(exp_done, c + 1)
                step.mark(tt(k(6), k(3), k(4), mul))
                need(v1)
                v2 = step.mark(tt(k(2), k(3), k(1), mul))
                need(v2)
                step.mark(tt(g_(0), col(CTR), k(2)[:, :, hi], mul))
                step.mark(tt(g_(2), col(CTI), k(6)[:, :, hi], mul))
                step.mark(tt(g_(1), col(NCTR), k(6)[:, :, hi], mul))
                v4 = step.mark(tt(g_(3), col(CTI), k(2)[:, :, hi], mul))
                need(v4)
                tt(g_(0), g_(0), g_(2), sub).then_inc(tables_done, 1)
                tt(g_(1), g_(1), g_(3), sub).then_inc(tables_done, 1)

            angles(0)
            for c in range(KC):
                if c + 1 < KC:
                    angles(c + 1)
                powers(c)

            def input_low(q, s):
                dve.wait_ge(xct_hi_done, q + 1)
                tt(xct_lo[:, s], ps[:, 6], xct_hi[:, s].bitcast(F32), sub).then_inc(xct_lo_done, 1)

            def down_low(q, s):
                dve.wait_ge(down_hi_done, q + 1)
                tt(wc[:, s, 1, WA:WC], wraw[:, s, WA:WC], wc[:, s, 0, WA:WC].bitcast(F32), sub).then_inc(down_lo_done, 1)

            def output(q, s):
                dve.wait_ge(y_half_copied, q + 1)
                tt(yo[:, s], yo[:, s], y_parts[:, :, 0], add).then_inc(y_copied, 1)

            def chunk_hidden(q, k, s):
                for j in range(J0):
                    f, r = width0(j), (s + j) % 2
                    dve.wait_ge(act_done, q * J0 + j + 1)
                    tt(hid[0:f, j], act[0:f, r], ps[0:f, 2 + r], mul)
                    tt(hid_hi[0:f, j], act[0:f, r], ps[0:f, 2 + r], mul).then_inc(hid_done, 1)
                    if j == 1:
                        if not is_first(q):
                            output(q - 1, 1 - s)
                        if not is_last(q):
                            input_low(q + 1, 1 - s)
                    if j == 2 and not is_last(q):
                        down_low(q + 1, 1 - s)

            dve.wait_ge(scattered, 16 * 2 * T)
            dve.wait_ge(k_copied, 2 * KC)
            down_low(0, 0)
            input_low(0, 0)
            all_chunks(dve, chunk_hidden)
            output(NC - 1, 0)

            dve.wait_ge(khat_copied, M)
            for half, (o_re, o_im) in enumerate(((sub, add), (add, sub))):
                m = slice(2 * half, 2 * half + 2)
                tt(khat[:, m, 2], khat[:, m, 2], khat[:, m, 1], o_re).then_inc(khat_ready, 1)
                tt(khat[:, m, 3], khat[:, m, 3], khat[:, m, 0], o_im).then_inc(khat_ready, 1)
            dve.wait_ge(khat_ready, 4)
            for m in range(M):
                X = lambda c, ri: ps[:, 4 * (m % 2) + 2 * c + ri].rearrange("p (b h) -> p b h", b=B)
                KH = lambda kind: khat[:, m, kind].unsqueeze(1).broadcast_to((P, B, P))
                wide3 = lambda a: a.rearrange("p (b h) -> p b h", b=B)
                Z = lambda c, ri: z[:, m, c, ri]
                T_ = lambda i: prod[:, i]
                dve.wait_ge(x_hat_done, m + 1)
                if m:
                    dve.wait_ge(z_ready, m)
                for dst, c, ri, kind in ((Z(0, 0), 0, 0, 0), (T_(0), 0, 1, 1), (Z(0, 1), 0, 0, 1), (T_(1), 0, 1, 0),
                                           (Z(1, 0), 0, 0, 2), (T_(2), 0, 1, 3), (Z(1, 1), 0, 0, 3), (T_(3), 0, 1, 2),
                                           (T_(4), 1, 0, 0), (T_(5), 1, 1, 1), (T_(6), 1, 0, 1), (T_(7), 1, 1, 0)):
                    v = tt(wide3(dst), X(c, ri), KH(kind), mul)
                v.then_inc(products_done, 1)
                dve.wait_ge(products_done, m + 1)
                tt(Z(0, 0), Z(0, 0), T_(0), sub)
                tt(Z(0, 1), Z(0, 1), T_(1), add)
                step.mark(tt(Z(1, 0), Z(1, 0), T_(2), sub))
                step.mark(tt(Z(1, 1), Z(1, 1), T_(3), add))
                step.mark(tt(T_(4), T_(4), T_(5), sub))
                v = step.mark(tt(T_(6), T_(6), T_(7), add))
                need(v)
                tt(Z(1, 0), Z(1, 0), T_(4), add)
                tt(Z(1, 1), Z(1, 1), T_(6), add).then_inc(z_ready, 1)

            def moments(src, i, signal):
                for b in range(B):
                    v = step.mark(nc.vector.bn_stats(stats[:, b], src[:, b * P:(b + 1) * P]))
                need(v)
                for b in range(B):
                    last = nc.vector.bn_aggr(mid_mv[:, i, b], stats[:, b])
                last.then_inc(signal, 1)

            def normalise(dst, src, i, signal):
                inverse_root(mid[:, 2 * i, 0:B], mid_mv[:, i, :, 1], mid[:, 2 * i + 1, 0:B])
                for b in range(B):
                    c = slice(b * P, (b + 1) * P)
                    last = ts(dst[:, c], src[:, c], mid_mv[:, i, b, 0:1], mid[:, 2 * i, b:b + 1], sub, mul)
                last.then_inc(signal, 1)

            def residual(g):
                dve.wait_ge(skip_done, g + 1)
                dve.wait_ge(y_done, g + 1)
                tt(xn[:, g], ps[:, g % 2], xn[:, g], add).then_inc(r_done, 1)
                dve.wait_ge(r_done, g + 1)
                moments(xn[:, g], 0, mid_stats)

            def first_norm(g):
                dve.wait_ge(root1_done, g + 1)
                normalise(xn[:, g], xn[:, g], 0, norm1_done)

            def layer0_sum(g):
                dve.wait_ge(xb_done, g + 1)
                if g == 0:
                    dve.wait_ge(first_in, 16 * T)
                dve.wait_ge(second_in[g], 16 * B)
                for k, y in enumerate((acc, prod)):
                    if k:
                        need(v)
                    for b in range(B):
                        c = slice(b * P, (b + 1) * P)
                        v = step.mark(stt(xs[:, g % 2, c], y[:, g, c], gate2[:, k, g * B + b:g * B + b + 1], xs[:, g % 2, c], mul, add))
                dve.wait_ge(scaled_done, g + 1)
                need(v)
                tt(xn[:, g], xn[:, g], xs[:, g % 2], add).then_inc(x1_done, 1)
                dve.wait_ge(x1_done, g + 1)
                moments(xn[:, g], 1, mid_stats2)

            def second_norm(g):
                dve.wait_ge(root2_done, g + 1)
                normalise(xn1[:, g % 2], xn[:, g], 1, xn1_done)

            def low1(g):
                dve.wait_ge(xt1_hi_done, g + 1)
                tt(xt1_lo[:, g], ps[:, 4 + g % 2], xt1_hi[:, g].bitcast(F32), sub).then_inc(xt1_lo_done, 1)

            for g in range(G):
                residual(g)
                if g >= 1:
                    second_norm(g - 1)
                first_norm(g)
                if g >= 1:
                    low1(g - 1)
                layer0_sum(g)
            second_norm(G - 1)
            low1(G - 1)

            def qkv_low(n):
                i = n % 6
                dve.wait_ge(qkv_hi_done, n + 1)
                tt(qkv_dst(qk_lo, v_lo, i), qkv_src(n), qkv_dst(qk_hi, v_hi, i).bitcast(F32), sub).then_inc(qkv_lo_done, 1)

            def row_max(n):
                s = n % 2
                dve.wait_ge(s_done, n + 1)
                v = step.mark(nc.vector.reduce_max(sm[:, s, 0:1], ps[:, 2 * s:2 * s + 2].rearrange("p a w -> p (a w)"), AX.X))
                need(v)
                ts(sm[:, s, 1:2], sm[:, s, 0:1], -SCALE, None, mul).then_inc(max_done, 1)

            def probabilities(n):
                s = n % 2
                dve.wait_ge(exp1_done, n + 1)
                v = step.mark(nc.vector.reciprocal(sm[:, s, 3:4], sm[:, s, 2:3]))
                need(v)
                ts(prob[:, s], prob[:, s], sm[:, s, 3:4], None, mul).then_inc(prob_done, 1)

            def turned_low(n):
                for a in range(2):
                    dve.wait_ge(pt_hi_done, 2 * n + a + 1)
                    tt(turned_dst(pt_lo, n, a), turned_src(a), turned_dst(pt_hi, n, a).bitcast(F32), sub).then_inc(pt_lo_done, 1)

            gw, thr = gl[:, :, 0:E], gl[:, :, E:E + 1]
            per_token = lambda i: gs[:, i].unsqueeze(2).broadcast_to((P, T, E))

            def gate_logits():
                dve.wait_ge(logits1_done, G)
                v = step.mark(tt(gl[:], ps[:, 6, 0:T * GW].rearrange("p (t e) -> p t e", e=GW),
                                 bias1[:].unsqueeze(1).broadcast_to((P, T, GW)), add))
                need(v)
                v = step.mark(nc.vector.reduce_max(gs[:, 0], gw, AX.X))
                need(v)
                tt(gw, gw, per_token(0), sub).then_inc(gate_soft, 1)

            def gate_weights():
                dve.wait_ge(gate_exp_done, 2)
                step.mark(nc.vector.reduce_sum(gs[:, 0], gw, AX.X))
                v = step.mark(ts(thr, thr, THRESHOLD / 2, THRESHOLD / 2, mul, add))
                need(v)
                v = step.mark(nc.vector.reciprocal(gs[:, 0], gs[:, 0]))
                need(v)
                v = step.mark(tt(gw, gw, per_token(0), mul))
                need(v)
                v = step.mark(tt(gw, gw, thr.broadcast_to((P, T, E)), sub))
                need(v)
                v = step.mark(ts(gw, gw, 0.0, None, ALU.max))
                need(v)
                v = step.mark(nc.vector.reduce_sum(gs[:, 0], gw, AX.X))
                need(v)
                v = step.mark(ts(gs[:, 1], gs[:, 0], 0.0, None, ALU.is_equal))
                need(v)
                v = step.mark(tt(gs[:, 0], gs[:, 0], gs[:, 1], add))
                need(v)
                v = step.mark(nc.vector.reciprocal(gs[:, 0], gs[:, 0]))
                need(v)
                tt(gates[:], gw, per_token(0), mul).then_inc(gates1_done, 1)

            gate_logits()
            for i in range(6):
                qkv_low(i)
            row_max(0)
            for n in range(B * G):
                if n == 3:
                    gate_weights()
                b, jt = divmod(n, G)
                probabilities(n)
                if n + 1 < B * G:
                    row_max(n + 1)
                turned_low(n)
                if jt == G - 2 and b + 1 < B:
                    for i in range(4):
                        qkv_low(6 * (b + 1) + i)
                if jt == G - 1 and b + 1 < B:
                    for i in range(4, 6):
                        qkv_low(6 * (b + 1) + i)

            def weigh1(g, e):
                dve.wait_ge(gate1_in[e % 4], 16 * (2 * g + e // 4 + 1))
                dve.wait_ge(expert1_done, g * E + e + 1)
                stt(part1[:, e % 2], ps[:, 4 + e % 2], b2_sb[:, e:e + 1], gate_row1[:, e % 4], add, mul).then_inc(part1_done, 1)

            def join1(g, e):
                a = acc[:, bass.ds(g, 1), :].rearrange("p a w -> p (a w)")
                dve.wait_ge(part1_done, g * E + e + 1)
                if e:
                    dve.wait_ge(join1_done, g * E + e)
                tt(a, a, part1[:, e % 2], add).then_inc(join1_done, 1)

            def add_final(g):
                if g >= 2:
                    dve.wait_ge(stored[g % 2], 16 * (g // 2))
                dve.wait_ge(final_done, g + 1)
                tt(final[:, g % 2], ps[:, 6 + g % 2], xn[:, g], add).then_inc(added_done, 1)

            def hidden1(g, first=False, last=False):
                for u in range(UN1):
                    e, j = divmod(u, J1)
                    dve.wait_ge(hid1_done, g * UN1 + u + 1)
                    tt(hid1_lo[:, u % 4], hid1[:, u % 4], hid1_hi[:, u % 4].bitcast(F32), sub).then_inc(hid1_lo_done, 1)
                    if not (first and e == 0):
                        to, ex = (g, e - 1) if e else (g - 1, E - 1)
                        if j == 2:
                            weigh1(to, ex)
                        if j == 3:
                            join1(to, ex)
                    if last and j == 1 and e >= 1:
                        add_final(e - 1)

            dve.wait_ge(pv_copied, 2 * B)
            hidden1(0, first=True)
            with dve.Fori(1, G - 1) as g:
                hidden1(g)
            hidden1(G - 1, last=True)
            weigh1(G - 1, E - 1)
            join1(G - 1, E - 1)
            add_final(G - 1)

        @block.tensor
        def _(pe):
            mm = nc.tensor.matmul

            def three(dst, a_hi, a_lo, b_hi, b_lo, first=True, last=True):
                mm(dst, a_lo, b_hi, start=first, stop=False)
                mm(dst, a_hi, b_lo, start=False, stop=False)
                return mm(dst, a_hi, b_hi, start=False, stop=last)

            pe.wait_ge(ident_done, 1)
            pe.wait_ge(small_in, 80)

            def logits(g):
                pe.wait_ge(xt_copied, g + 1)
                for b in range(B):
                    o = ps[:, 2, (g * B + b) * E:(g * B + b + 1) * E]
                    last = mm(o, xt[:, g % 2, b * P:(b + 1) * P], wg0_sb[:], start=True, stop=True)
                last.then_inc(logits_done, 1)

            for g in range(G):
                pe.wait_ge(xn_ready, g + 1)
                for b in range(B):
                    last = nc.tensor.transpose(ps[:, g % 2, b * P:(b + 1) * P], xn[:, g, b * P:(b + 1) * P], ident[:])
                last.then_inc(xt_done, 1)
                if g >= 1:
                    logits(g - 1)
            logits(G - 1)
            pe.wait_ge(member_done, 1)
            pe.wait_ge(ident_done, 2)
            chosen = member.rearrange("p t e -> p (t e)")
            mm(ps[:, 3, 0:T * E], before[:], chosen, start=True, stop=True)
            mm(ps[:, 3, T * E:2 * T * E], ones[:], chosen, start=True, stop=True).then_inc(counted, 1)

            for c in range(KC):
                pe.wait_ge(tables_done, 2 * c + 2)
                if c >= 2:
                    pe.wait_ge(k_copied, 2 * c - 2)
                for half in range(2):
                    states = slice(half * N, (half + 1) * N)
                    for h in range(CH):
                        o = ps[0:LO, 4 + 2 * (c % 2) + half, h * LO:(h + 1) * LO]
                        mm(o, kg[states, c % 2, 0, h, :], kc[states, c % 2, 2, h, 0:LO], start=True, stop=False)
                        last = mm(o, kg[states, c % 2, 1, h, :], kc[states, c % 2, 6, h, 0:LO], start=False, stop=True)
                    last.then_inc(k_mm_done, 1)

            def turn_inputs(q, k, s):
                pe.wait_ge(xc_in[s], (k + 1) * 16)
                for t in range(4):
                    last = nc.tensor.transpose(ps[:, 6, t * P:(t + 1) * P], xc[:, s, t], ident[:])
                last.then_inc(xct_done, 1)

            def up(s, j):
                f, r = width0(j), (s + j) % 2
                for bank, col in ((r, 0), (2 + r, HID0)):
                    w = slice(col + j * P, col + j * P + f)
                    last = three(ps[0:f, bank], wc[:, s, 0, w], wc[:, s, 1, w], xct_hi[:, s], xct_lo[:, s])
                last.then_inc(up_done, 1)

            def down(q, s, j):
                f = width0(j)
                pe.wait_ge(hid_lo_done, q * J0 + j + 1)
                if j == 0:
                    pe.wait_ge(down_lo_done, q + 1)
                    if not is_first(q):
                        pe.wait_ge(y_copied, q)
                w = wc[0:f, s, :, WA + j * P:WA + (j + 1) * P]
                for t in range(4):
                    o = ps[:, 4 + t // 2, (t % 2) * 2 * P:(t % 2 + 1) * 2 * P].rearrange("p (i c) -> p i c", i=2)
                    mm(o, hid_lo[0:f, j, t * P:(t + 1) * P], w, start=(j == 0 and t % 2 == 0), stop=False)
                    last = mm(o, hid_hi[0:f, j, t * P:(t + 1) * P], w, start=False, stop=(j == J0 - 1 and t % 2 == 1))
                if j == J0 - 1:
                    last.then_inc(chunk_done, 1)

            def chunk_products(q, k, s):
                for j in range(J0):
                    if j == 0 and not is_last(q):
                        turn_inputs(q + 1, k + s, 1 - s)
                    if j == 0 or not is_last(q):
                        pe.wait_ge(hid_done, q * J0 + j + 1)
                    if j == 0:
                        up(s, 2)
                    elif not is_last(q):
                        if j == 1:
                            pe.wait_ge(xct_lo_done, q + 2)
                            pe.wait_ge(up_lo_done, q + 2)
                        up(1 - s, j - 1)
                    down(q, s, j)

            pe.wait_ge(k_copied, 2 * KC)
            turn_inputs(0, 0, 0)
            pe.wait_ge(xct_lo_done, 1)
            pe.wait_ge(up_lo_done, 1)
            up(0, 0)
            up(0, 1)
            all_chunks(pe, chunk_products)

            pe.wait_ge(kernel_in, 16)
            for t in range(G):
                last = nc.tensor.transpose(ps[:, t // 4, (t % 4) * P:(t % 4 + 1) * P], k_nat[:, t * P:(t + 1) * P], ident[:])
            last.then_inc(k_t_done, 1)
            pe.wait_ge(k_t_copied, 2)
            pe.wait_ge(fwd_in, 16)
            pe.wait_ge(y_copied, NC)
            halves = k_t.rearrange("p (c t) h -> p t c h", c=2)
            for m in range(M):
                for part_ in range(2):
                    for t in range(CT):
                        last = mm(ps[:, 4 + m, part_ * 2 * P:(part_ + 1) * 2 * P], fwd[:, t, part_, m * P:(m + 1) * P],
                                  halves[:, t], start=(t == 0), stop=(t == CT - 1))
                last.then_inc(khat_mm, 1)

            for m in range(M):
                if m == 1:
                    pe.wait_ge(khat_copied, M)
                if m >= 2:
                    pe.wait_ge(products_done, m - 1)
                for c in range(2):
                    for part_ in range(2):
                        for t in range(CT):
                            last = mm(ps[:, 4 * (m % 2) + 2 * c + part_], fwd[:, t, part_, m * P:(m + 1) * P],
                                      xn[:, c * CT + t], start=(t == 0), stop=(t == CT - 1))
                last.then_inc(x_hat_done, 1)

            def logits1(g):
                pe.wait_ge(xt1_lo_done, g + 1)
                for b in range(B):
                    c = slice(b * P, (b + 1) * P)
                    o = ps[:, 6, (g * B + b) * GW:(g * B + b + 1) * GW]
                    w = slice(GATE1, GATE1 + GW)
                    last = three(o, xt1_hi[:, g, c], xt1_lo[:, g, c], w_hi[:, w], w_lo[:, w])
                last.then_inc(logits1_done, 1)

            def turn1(g):
                pe.wait_ge(xn1_done, g + 1)
                for b in range(B):
                    last = nc.tensor.transpose(ps[:, 4 + g % 2, b * P:(b + 1) * P], xn1[:, g % 2, b * P:(b + 1) * P], ident[:])
                last.then_inc(xt1_done, 1)

            pe.wait_ge(z_ready, M)
            pe.wait_ge(inv_in, 16)
            for g in range(G):
                c, t = divmod(g, CT)
                if g >= 2:
                    pe.wait_ge(r_done, g - 1)
                for m in range(M):
                    for part_ in range(2):
                        last = mm(ps[:, g % 2], inv[:, m, part_, t * P:(t + 1) * P], z[:, m, c, part_],
                                  start=(m == 0 and part_ == 0), stop=(m == M - 1 and part_ == 1))
                last.then_inc(y_done, 1)
                if g >= 1:
                    if g >= 2:
                        logits1(g - 2)
                    turn1(g - 1)
            logits1(G - 2)
            turn1(G - 1)
            logits1(G - 1)

            def qkv(n):
                b, i = divmod(n, 6)
                if n >= 2:
                    pe.wait_ge(qkv_lo_done, n - 1)
                bank = ps[:, 6 + n % 2]
                cols = slice(b * P, (b + 1) * P)
                if i < 4:
                    w = slice(QKV + (i // 2) * P, QKV + (i // 2 + 1) * P)
                    gr = slice(4 * (i % 2), 4 * (i % 2) + 4)
                    last = three(bank.rearrange("p (t j) -> p t j", t=4), w_hi[:, w], w_lo[:, w],
                                 xt1_hi[:, gr, cols], xt1_lo[:, gr, cols])
                else:
                    w = slice(QKV + 2 * P, QKV + 3 * P)
                    for t in range(4):
                        gr = 4 * (i - 4) + t
                        last = three(bank[:, t * P:(t + 1) * P], xt1_hi[:, gr, cols], xt1_lo[:, gr, cols], w_hi[:, w], w_lo[:, w])
                last.then_inc(qkv_mm, 1)

            def scores(n):
                jt = n % G
                pe.wait_ge(qkv_lo_done, 6 * (n // G) + 4)
                if n >= 2:
                    pe.wait_ge(exp1_done, n - 1)
                j = slice(jt * P, (jt + 1) * P)
                for a in range(2):
                    i = slice(a * C, (a + 1) * C)
                    last = three(ps[:, 2 * (n % 2) + a], qk_hi[:, 1, j], qk_lo[:, 1, j], qk_hi[:, 0, i], qk_lo[:, 0, i])
                last.then_inc(s_done, 1)

            pe.wait_ge(gate_soft, 1)
            for i in range(6):
                qkv(i)
            scores(0)
            scores(1)
            for n in range(B * G):
                if n == 4:
                    pe.wait_ge(gates1_done, 1)
                    flat = gates[:].rearrange("p t e -> p (t e)")
                    for a in range(2):
                        last = nc.tensor.transpose(ps[:, 7, a * P:(a + 1) * P], flat[:, a * P:(a + 1) * P], ident[:])
                    last.then_inc(gates1_turned, 1)
                b, jt = divmod(n, G)
                pe.wait_ge(prob_done, n + 1)
                for a in range(2):
                    if n >= 1:
                        pe.wait_ge(pt_lo_done, 2 * n - 1 + a)
                    for t in range(4):
                        last = nc.tensor.transpose(ps[:, 4 + a, t * P:(t + 1) * P],
                                                   prob[:, n % 2, (4 * a + t) * P:(4 * a + t + 1) * P], ident[:])
                    last.then_inc(pt_done, 1)
                if jt == G - 2 and b + 1 < B:
                    pe.wait_ge(pv_copied, 2 * b + 1)
                    pe.wait_ge(gates1_copied, 1)
                    for i in range(4):
                        qkv(6 * (b + 1) + i)
                if n + 2 < B * G:
                    scores(n + 2)
                if jt % 4 == 3:
                    pe.wait_ge(pt_lo_done, 2 * n + 2)
                    pe.wait_ge(qkv_lo_done, 6 * (b + 1) + (4 if jt == G - 1 and b + 1 < B else 0))
                    for t in range(G):
                        last = three(ps[:, 6], v_hi[:, t], v_lo[:, t], pt_hi[:, t], pt_lo[:, t],
                                     first=(t == 0), last=(t == G - 1))
                    last.then_inc(pv_done, 1)
                    if jt == G - 1 and b + 1 < B:
                        pe.wait_ge(pv_copied, 2 * b + 2)
                        for i in range(4, 6):
                            qkv(6 * (b + 1) + i)

            def up1(g, u):
                xh, xl = (t[:, bass.ds(g, 1), :].rearrange("p a w -> p (a w)") for t in (xt1_hi, xt1_lo))
                w = slice(u * P, (u + 1) * P)
                three(ps[:, u % 4], w_hi[:, w], w_lo[:, w], xh, xl).then_inc(up1_done, 1)

            def down1(g, u):
                e, j = divmod(u, J1)
                pe.wait_ge(hid1_lo_done, g * UN1 + u + 1)
                w = slice(E * HID1 + u * P, E * HID1 + (u + 1) * P)
                last = three(ps[:, 4 + e % 2], w_hi[:, w], w_lo[:, w], hid1_hi[:, u % 4], hid1_lo[:, u % 4],
                             first=(j == 0), last=(j == J1 - 1))
                if j == J1 - 1:
                    last.then_inc(expert1_done, 1)

            def turn_out(g):
                if g >= 2:
                    pe.wait_ge(added_done, g - 1)
                for b in range(B):
                    last = nc.tensor.transpose(ps[:, 6 + g % 2, b * P:(b + 1) * P], acc[:, g, b * P:(b + 1) * P], ident[:])
                last.then_inc(final_done, 1)

            def experts1(g, last):
                for u in range(UN1):
                    if u + 3 < UN1 or not last:
                        up1(g + (u + 3) // UN1, (u + 3) % UN1)
                    down1(g, u)
                    if last and u % J1 == 0 and u // J1 >= 1:
                        pe.wait_ge(join1_done, (u // J1) * E)
                        turn_out(u // J1 - 1)

            pe.wait_ge(w1_lo_done, len(pieces1))
            pe.wait_ge(exp1_done, B * G)
            pe.wait_ge(pv_copied, 2 * B)
            for u in range(3):
                up1(0, u)
            with pe.Fori(0, G - 1) as g:
                experts1(g, False)
            experts1(G - 1, True)
            pe.wait_ge(join1_done, G * E)
            turn_out(G - 1)


def kernel(**inputs):
    from concourse import bacc
    from concourse.bass_utils import run_bass_kernel_spmd

    nc = bacc.Bacc("TRN2", target_bir_lowering=False, num_devices=1)
    arrays = layout({k: np.asarray(v) for k, v in inputs.items()})
    aps = {n: nc.dram_tensor(n, a.shape, F32, kind="ExternalInput").ap() for n, a in arrays.items()}
    out = nc.dram_tensor("out", (B, L, H), F32, kind="ExternalOutput").ap()
    program(nc, out=out, **aps)
    return run_bass_kernel_spmd(nc, [arrays], core_ids=[0]).results[0]["out"]


def layout(a):
    def by_state(p):
        return p.reshape(2, HH, N).transpose(0, 2, 1).reshape(P, HH)

    freq = np.concatenate([np.arange(0, C, 2), np.arange(1, C, 2)]) + 0.5
    angle = 2 * np.pi * np.outer(np.arange(C), freq) / (2 * C)
    dft = np.stack([np.cos(angle), -np.sin(angle)]).astype(np.float32)
    fwd = dft.reshape(2, CT, P, C).transpose(2, 1, 0, 3)
    inv = dft.transpose(0, 2, 1).reshape(2, M, P, C).transpose(2, 1, 0, 3)
    d = dict(
        x=a["L0_attn_x"],
        state_params=np.stack([by_state(a["L0_attn_" + n]) for n in ("log_A_real", "A_imag", "C_re", "C_im")], 1),
        log_dt=a["L0_attn_log_dt"], skip=a["L0_attn_D"], ln_w=a["L0_attn_ln_w"], ln_b=a["L0_attn_ln_b"],
        wg0=a["L0_ffn_Wg"].T,
        w0=np.concatenate([
            a["L0_ffn_W1"].transpose(0, 2, 1), a["L0_ffn_W2"].transpose(0, 2, 1),
            np.pad(a["L0_ffn_W3"].transpose(0, 2, 1), ((0, 0), (0, J0 * P - HID0), (0, 0)))
            .reshape(E, J0, P, P).transpose(0, 2, 1, 3).reshape(E, P, J0 * P)], 2),
        lag_row=np.concatenate([np.arange(LO), LO * np.arange(LO), E - np.arange(E)]).astype(np.float32),
        dft_fwd=fwd, dft_inv=inv,
        wqkv=np.stack([a["L1_attn_W_query"], a["L1_attn_W_key"], a["L1_attn_W_value"]], 1),
        wg1=np.pad(np.concatenate([a["L1_ffn_Wg"], a["L1_ffn_Wt"]], 1), ((0, 0), (0, GW - E - 1))),
        gate_bias=np.pad(np.concatenate([a["L1_ffn_bg"], a["L1_ffn_bt"]]), (0, GW - E - 1)),
        w1_1=a["L1_ffn_W1"],
        b1=a["L1_ffn_b1"].reshape(E * J1, P).T,
        w2_1=a["L1_ffn_W2"],
        b2=a["L1_ffn_b2"].T,
    )
    return {n: np.ascontiguousarray(v) for n, v in d.items()}
```

```python
import math
from contextlib import ExitStack

import numpy as np
import concourse.bass as bass
from concourse import mybir

F32 = mybir.dt.float32
F32R = mybir.dt.float32r
ALU = mybir.AluOpType
ACT = mybir.ActivationFunctionType
AX = mybir.AxisListType

B, L, H = 4, 1024, 128
N = 64
P = 128
G = L // P
W = B * P
E = 8
HID0 = 341
J0 = -(-HID0 // P)
HID1 = 512
J1 = HID1 // P
LN_EPS = 1e-5
THRESHOLD = 0.125
T = G * B
NC = (2 * B * L - E) // W + E
WA, WC = 2 * HID0, 2 * HID0 + J0 * P
MIN_PAIRS, MAX_PAIRS = (2 * B * L // W - 2) // 2, (NC - 3) // 2
SURE = 3 + 2 * MIN_PAIRS
assert NC % 2 == 1
GW = 10
UN1 = E * J1
QKV, GATE1 = 2 * E * HID1, 2 * E * HID1 + 3 * P
STAGES = 4
SCALE = float(1.0 / np.sqrt(np.float32(H)))
LO = 32
LAGS = 2 * LO
HH = H // 2
CH = 16
KC = HH // CH
C = 512
CT = C // P
M = C // P
ME = M - 1
MAGIC = 1.5 * 2.0 ** 23
MAGIC_13 = 1.5 * 2.0 ** 10
TWO_PI = 6.283185
INV_2PI = 1.0 / (2.0 * math.pi)
INV_2PI_HI = float(np.round(INV_2PI * 2 ** 14) / 2 ** 14)
INV_2PI_LO = INV_2PI - INV_2PI_HI
LN2_HI = 355.0 / 512.0
LN2_LO = math.log(2.0) - LN2_HI


class Tally:

    def __init__(self, sem):
        self.sem, self.n = sem, 0

    def mark(self, instruction):
        instruction.then_inc(self.sem, 1)
        self.n += 1
        return self.n



def program(nc, x, state_params, log_dt, skip, ln_w, ln_b, wg0, w0, lag_row,
            dft_fwd, dft_inv, wqkv, wg1, gate_bias, w1_1, b1, w2_1, b2, out):
    ctx = ExitStack()
    with ctx:
        def sb(name, shape, dt=F32):
            return ctx.enter_context(nc.sbuf_tensor(name, shape, dt))

        def sem(name):
            return ctx.enter_context(nc.semaphore(name))

        kernel_dram = nc.dram_tensor("kernel_dram", (H, LO, LO), F32).ap()
        gates_dram = nc.dram_tensor("gates_dram", (T, E, P), F32).ap()
        x_slots = nc.dram_tensor("x_slots", (NC * W, H), F32).ap()
        y_slots = nc.dram_tensor("y_slots", (NC * W, H), F32).ap()

        x_hat_dram = nc.dram_tensor("x_hat_dram", (ME, 4, P, W), F32).ap()

        WCOLS = 2 * E * HID1 + 3 * P + GW + 6
        w_hi = sb("w_hi", [P, WCOLS], F32R)
        w_lo = sb("w_lo", [P, WCOLS], F32R)
        xn = sb("xn", [P, G, W])
        acc = sb("acc", [P, G, W])
        gate2 = sb("gate2", [P, 2, T])
        slot = sb("slot", [P, 2, T], mybir.dt.int32)
        pairs = sb("pairs", [P, 1], mybir.dt.int32)
        expert_of = sb("expert_of", [P, NC], mybir.dt.int32)
        ident = sb("ident", [P, P])
        stats = sb("stats", [P, 2 * B, 6])
        eps = sb("eps", [P, 1])
        gates = sb("gates", [P, G * B, E])
        gates_t = gates[:].rearrange("p (a t) e -> p a (t e)", a=2)
        bias1 = sb("bias1", [P, GW])
        gl = sb("gl", [P, G * B, GW])
        gs = sb("gs", [P, 2, G * B])
        b1_sb = sb("b1_sb", [P, E * J1])
        b2_sb = sb("b2_sb", [P, E])
        mid = sb("mid", [P, 2, 2, 3, B])
        mid_mv = sb("mid_mv", [P, 2, 2, B, 2])

        phase = ExitStack()

        def tmp(name, shape, dt=F32):
            return phase.enter_context(nc.sbuf_tensor(name, shape, dt))

        xt = tmp("xt", [P, 2, W])
        wst1 = tmp("wst1", [P, STAGES, 512])
        zeros = tmp("zeros", [P, W])
        mv = tmp("mv", [P, G * B, 2])
        rstd = tmp("rstd", [P, G * B])
        newton = tmp("newton", [P, G * B])
        consts = tmp("consts", [P, LAGS + E])
        lagv = consts[:, 0:LAGS]
        rev = consts[:, LAGS:LAGS + E]
        wg0_sb = tmp("wg0_sb", [P, E])
        before = tmp("before", [P, P])
        ones = tmp("ones", [P, P])
        small = tmp("small", [P, 4, HH])
        ks = tmp("ks", [P, 24, HH])
        exp2 = tmp("exp2", [P, 2 * HH], mybir.dt.int32)
        th_hi = tmp("th_hi", [P, HH], F32R)
        route = tmp("route", [P, 8, E])
        slot_f = tmp("slot_f", [P, 2, T])
        expert_f = tmp("expert_f", [P, NC])
        kc = tmp("kc", [P, 2, 7, CH, LAGS])
        kg = tmp("kg", [P, 2, 4, CH, LO])
        k_out = tmp("k_out", [LO, 2, 2, CH, LO])
        fwd0 = acc[:].rearrange("p (t r) w -> p t r w", r=2)
        tk = kc[:, 0].rearrange("p a b c -> p (a b c)")
        phase.close()

        phase = ExitStack()
        wraw = tmp("wraw", [P, 2, WC])
        xc = tmp("xc", [P, 2, 4, P])
        xct_hi = tmp("xct_hi", [P, 2, W], F32R)
        xct_lo = tmp("xct_lo", [P, 2, W], F32R)
        wc = tmp("wc", [P, 2, 2, WC], F32R)
        act = tmp("act", [P, 2, W])
        hid = tmp("hid", [P, J0, W])
        hid_hi = tmp("hid_hi", [P, J0, W], F32R)
        hid_lo = tmp("hid_lo", [P, J0, W], F32R)
        yo = tmp("yo", [P, 2, 4, P])
        phase.close()

        phase = ExitStack()
        inv = tmp("inv", [P, M, 2, C])
        khat = tmp("khat", [P, M, 4, P])
        xs = tmp("xs", [P, 2, W])
        xn1 = tmp("xn1", [P, 2, W])
        z = tmp("z", [P, M, 2, 2, W])
        fwd = tmp("fwd", [P, CT, 2, C])
        prod = tmp("prod", [P, 8, W])
        vec_rows = tmp("vec_rows", [P, 3, P])
        k_nat = prod[:, 0:2].rearrange("p a b -> p (a b)")
        k_t = xn1[:].rearrange("p a b -> p (a b)").rearrange("p (t h) -> p t h", h=P)
        phase.close()

        phase = ExitStack()
        pt_hi = tmp("pt_hi", [P, 2, G, 2 * P], F32R)
        pt_lo = tmp("pt_lo", [P, 2, G, 2 * P], F32R)
        q_hi = tmp("q_hi", [P, 2, L], F32R)
        q_lo = tmp("q_lo", [P, 2, L], F32R)
        k_hi = tmp("k_hi", [P, L], F32R)
        k_lo = tmp("k_lo", [P, L], F32R)
        v_hi = tmp("v_hi", [P, G, P], F32R)
        v_lo = tmp("v_lo", [P, G, P], F32R)
        xt1_hi = tmp("xt1_hi", [P, G, W], F32R)
        xt1_lo = tmp("xt1_lo", [P, G, W], F32R)
        prob = tmp("prob", [P, 2, L])
        sm = tmp("sm", [P, 2, 4])
        phase.close()

        phase = ExitStack()
        hid1 = tmp("hid1", [P, 4, W])
        hid1_hi = tmp("hid1_hi", [P, 4, W], F32R)
        hid1_lo = tmp("hid1_lo", [P, 4, W], F32R)
        gate_row1 = tmp("gate_row1", [P, 4, W])
        part1 = tmp("part1", [P, 2, W])
        final = tmp("final", [P, 2, W])
        phase.close()

        lg, eq, k2, oh1, oh2, member, rank, count_a, count_b = (
            tk[:, i * T * E:(i + 1) * T * E].rearrange("p (t e) -> p t e", e=E) for i in range(9))
        m1, p1, m2, p2 = (tk[:, 9 * T * E + i * T:9 * T * E + (i + 1) * T] for i in range(4))
        ps = ctx.enter_context(nc.psum_tensor("ps", [P, 8, W], F32))

        x_in = [sem(f"x_in{g}") for g in range(G)]
        small_in = sem("small_in")
        stats_done = sem("stats_done")
        top2_done = sem("top2_done")
        gate2_done = sem("gate2_done")
        zeros_done = sem("zeros_done")
        zeros_out = sem("zeros_out")
        member_done = sem("member_done")
        counted = sem("counted")
        slots_done = sem("slots_done")
        scattered = sem("scattered")
        ident_done = sem("ident_done")
        pool_step = sem("pool_step")
        dve_step = sem("dve_step")
        trig_done = sem("trig_done")
        root_done = sem("root_done")
        top2_exp_done = sem("top2_exp_done")
        xn_ready = sem("xn_ready")
        xt_done = sem("xt_done")
        xt_copied = sem("xt_copied")
        logits_done = sem("logits_done")
        decay_done = sem("decay_done")
        phase_done = sem("phase_done")
        exp_done = sem("exp_done")
        sin_done = sem("sin_done")
        tables_done = sem("tables_done")
        k_mm_done = sem("k_mm_done")
        k_copied = sem("k_copied")
        k_stored = [sem(f"k_stored{i}") for i in range(2)]
        xc_in = [sem(f"xc_in{i}") for i in range(2)]
        wraw_in = [sem(f"wraw_in{i}") for i in range(2)]
        xct_done = sem("xct_done")
        xct_hi_done = sem("xct_hi_done")
        xct_lo_done = sem("xct_lo_done")
        up_hi_done = sem("up_hi_done")
        up_lo_done = sem("up_lo_done")
        down_hi_done = sem("down_hi_done")
        down_lo_done = sem("down_lo_done")
        up_done = sem("up_done")
        act_done = sem("act_done")
        hid_done = sem("hid_done")
        hid_lo_done = sem("hid_lo_done")
        chunk_done = sem("chunk_done")
        y_half_copied = sem("y_half_copied")
        y_copied = sem("y_copied")
        y_stored = [sem(f"y_stored{i}") for i in range(2)]
        outputs_out = sem("outputs_out")
        rows_back = [sem(f"rows_back{g}") for g in range(G)]
        first_scaled = sem("first_scaled")
        second_scaled = sem("second_scaled")
        x_joined = sem("x_joined")
        norm1_ready = sem("norm1_ready")
        norm2_ready = sem("norm2_ready")

        kernel_in = sem("kernel_in")
        fwd_in = sem("fwd_in")
        inv_in = sem("inv_in")
        rows_in = sem("rows_in")
        biases_in = sem("biases_in")
        xs_in0 = sem("xs_in0")
        xs_in1 = sem("xs_in1")
        k_t_done = sem("k_t_done")
        k_t_copied = sem("k_t_copied")
        khat_mm = sem("khat_mm")
        khat_copied = sem("khat_copied")
        khat_ready = sem("khat_ready")
        x_hat_done = sem("x_hat_done")
        fwd0_in = sem("fwd0_in")
        spectra_mm = sem("spectra_mm")
        spectra_copied = sem("spectra_copied")
        spectra_stored = [sem(f"spectra_stored{i}") for i in range(4)]
        spectra_in = [sem(f"spectra_in{m}") for m in range(ME)]
        products_done = sem("products_done")
        z_ready = sem("z_ready")
        wst1_in = [sem(f"wst1_in{i}") for i in range(STAGES)]
        w1_hi_done = sem("w1_hi_done")
        w1_lo_done = sem("w1_lo_done")
        y_done = sem("y_done")
        mid_stats = sem("mid_stats")
        root1_done = sem("root1_done")
        norm1_done = sem("norm1_done")
        scaled_done = sem("scaled_done")
        xb_done = sem("xb_done")
        x1_done = sem("x1_done")
        mid_stats2 = sem("mid_stats2")
        root2_done = sem("root2_done")
        xn1_done = sem("xn1_done")
        xt1_done = sem("xt1_done")
        xt1_hi_done = sem("xt1_hi_done")
        xt1_lo_done = sem("xt1_lo_done")
        logits1_done = sem("logits1_done")
        gates_out = sem("gates_out")
        gate_exp_done = sem("gate_exp_done")
        gate_soft = sem("gate_soft")
        gates1_done = sem("gates1_done")
        gates1_turned = sem("gates1_turned")
        gates1_copied = sem("gates1_copied")
        qkv_mm = sem("qkv_mm")
        qkv_hi_done = sem("qkv_hi_done")
        qkv_lo_done = sem("qkv_lo_done")
        s_done = sem("s_done")
        max_done = sem("max_done")
        exp1_done = sem("exp1_done")
        prob_done = [sem(f"prob_done{a}") for a in range(2)]
        inverse_done = sem("inverse_done")
        pt_done = sem("pt_done")
        pt_hi_done = sem("pt_hi_done")
        pt_lo_done = sem("pt_lo_done")
        pv_done = sem("pv_done")
        pv_copied = sem("pv_copied")
        up1_done = sem("up1_done")
        hid1_done = sem("hid1_done")
        hid1_lo_done = sem("hid1_lo_done")
        expert1_done = sem("expert1_done")
        part1_done = sem("part1_done")
        join1_done = sem("join1_done")
        gate1_in0 = sem("gate1_in0")
        gate1_in1 = sem("gate1_in1")
        gate1_in2 = sem("gate1_in2")
        gate1_in3 = sem("gate1_in3")
        final_done = sem("final_done")
        added_done = sem("added_done")
        stored = [sem(f"stored{n}") for n in range(2)]
        gate1_in = [gate1_in0, gate1_in1, gate1_in2, gate1_in3]
        xs_in = [xs_in0, xs_in1]

        block = ctx.enter_context(nc.Block())

        def all_chunks(engine, body):
            engine.wait_ge(slots_done, 4)
            n = engine.value_load(pairs[0:1, 0:1], min_val=MIN_PAIRS, max_val=MAX_PAIRS)
            body(0, 0, 0, 2)
            with engine.Fori(0, n) as i:
                body(i * 2 + 1, i, 1, 2)
                body(i * 2 + 2, i + 1, 0, 2)
            body(n * 2 + 1, n, 1, 1)
            body(n * 2 + 2, n + 1, 0, 0)
            return n * 2 + 2, n + 1

        is_first = lambda q: isinstance(q, int) and q == 0
        second_part = lambda g: xn1 if g < 2 else prod
        y_parts = ps[:, 4:6].rearrange("p a (t i c) -> p (a t) i c", t=2, i=2)
        k_bank = lambda c: 6 - 2 * (c % 2)
        width0 = lambda j: min(P, HID0 - j * P)

        pieces1 = [(wqkv, lambda a: a.rearrange("p (k e) -> p k e", k=3), QKV, 3 * P), (wg1, lambda a: a, GATE1, GW)]
        for e in range(E):
            pieces1.append((w1_1[e], lambda a: a, e * HID1, HID1))
            pieces1.append((w2_1[e].rearrange("(j f) d -> f j d", j=J1), lambda a: a.rearrange("p (j d) -> p j d", j=J1),
                            E * HID1 + e * HID1, HID1))

        def qkv_piece(m):
            if m < 4:
                return 0, m
            b, i = divmod(m - 4, 6)
            return (b, 4 + i) if i < 2 else (b + 1, i - 2)

        def qkv_after(n):
            m = 4 + 6 * (n // G) + n % G - 1
            return m if 1 <= n % G <= 6 and m < 6 * B else None

        def qkv_dst(m, q, k, v):
            b, i = qkv_piece(m)
            half = slice((i % 2) * C, (i % 2 + 1) * C)
            return q[:, b % 2, half] if i < 2 else k[:, half] if i < 4 else v[:, 4 * (i - 4):4 * (i - 3)]

        def qkv_src(m):
            bank = ps[:, (7, 4, 5, 2)[m] if m < 4 else 7]
            return bank if qkv_piece(m)[1] < 4 else bank.rearrange("p (t e) -> p t e", t=4)

        def turned_dst(pt, n, a):
            return pt[:, n // 2 % 2, 4 * a:4 * a + 4, (n % 2) * P:(n % 2 + 1) * P]

        def turned_src(a):
            return ps[:, 4 + a].rearrange("p (t j) -> p t j", t=4)

        @block.sync
        def _(sp):
            for g in range(G):
                sp.dma_start(xn[:, g, :].rearrange("p (b h) -> p b h", b=B),
                             x[:, g * P:(g + 1) * P, :].rearrange("b p h -> p b h")).then_inc(x_in[g], 16)
            sp.dma_start(small[:], state_params).then_inc(small_in, 16)
            for half in range(2):
                sp.dma_start(ks[half * N:(half + 1) * N, 0, :],
                             log_dt[half * HH:(half + 1) * HH].partition_broadcast(N)).then_inc(small_in, 16)
            sp.dma_start(consts[:], lag_row.partition_broadcast(P)).then_inc(small_in, 16)
            sp.dma_start(wg0_sb[:], wg0).then_inc(small_in, 16)
            sp.wait_ge(zeros_done, 1)
            blank = x_slots.rearrange("(p r) h -> p (r h)", p=P).rearrange("p (a w) -> p a w", w=W)
            blanks = [(a, min(a + 2, NC)) for a in range(0, NC, 2)]

            def clear(n):
                a, b_ = blanks[n]
                sp.dma_start(blank[:, a:b_], zeros[:].unsqueeze(1).broadcast_to((P, b_ - a, W))).then_inc(zeros_out, 16)

            for n, (src, view, col, cols) in enumerate(pieces1):
                if n >= STAGES:
                    sp.wait_ge(w1_lo_done, n - STAGES + 1)
                sp.dma_start(view(wst1[:, n % STAGES, 0:cols]), src).then_inc(wst1_in[n % STAGES], 16)
                if n % 3 == 2:
                    clear(n // 3)
                if n == len(pieces1) - 6:
                    sp.dma_start(fwd0, dft_fwd).then_inc(fwd0_in, 16)
            for n in range(len(pieces1) // 3, len(blanks)):
                clear(n)
            sp.dma_start(y_slots[SURE * W:].rearrange("(p r) h -> p (r h)", p=P).rearrange("p (a w) -> p a w", w=W),
                         zeros[:].unsqueeze(1).broadcast_to((P, NC - SURE, W))).then_inc(zeros_out, 16)
            sp.dma_start(bias1[:], gate_bias.partition_broadcast(P)).then_inc(biases_in, 16)
            sp.dma_start(b1_sb[:], b1).then_inc(biases_in, 16)
            sp.dma_start(b2_sb[:], b2).then_inc(biases_in, 16)
            def w_load(q, s):
                e = sp.value_load(expert_of[0:1, bass.ds(q, 1)], min_val=0, max_val=E - 1)
                sp.dma_start(wraw[:, s], w0[bass.ds(e, 1)].rearrange("a p w -> p (a w)")).then_inc(wraw_in[s], 16)

            def k_store(c):
                sp.wait_ge(k_copied, 2 * c + 2)
                for half in range(2):
                    heads = half * HH + c * CH
                    sp.dma_start(kernel_dram[heads:heads + CH].rearrange("j m n -> m j n"),
                                 k_out[:, c % 2, half]).then_inc(k_stored[c % 2], 16)

            k_store(0)
            sp.wait_ge(slots_done, 4)
            sp.wait_ge(w1_lo_done, len(pieces1))
            sp.wait_ge(zeros_out, 16 * (-(-NC // 2) + 1))
            for r in range(4):
                sp.wait_ge(spectra_stored[r], 16 * ME)
            for q in range(2):
                w_load(q, q)
            for c in range(1, KC - 1):
                k_store(c)
            rows_of = lambda a, q: a[bass.ds(q * W, W)].rearrange("(p t) h -> p t h", t=4)

            def x_load(q, s):
                sp.dma_start(xc[:, s], rows_of(x_slots, q)).then_inc(xc_in[s], 16)

            sp.wait_ge(scattered, 16 * 2 * T)
            for q in range(2):
                x_load(q, q)
                sp.sem_inc(y_stored[q], 16)
            k_store(KC - 1)

            def y_store(q, s):
                sp.wait_ge(y_copied, q + 1)
                sp.dma_start(rows_of(y_slots, q), yo[:, s]).then_inc(y_stored[s], 16)

            def chunk_loads(q, k, s, left):
                if left == 2:
                    sp.wait_ge(xct_done, q + 1)
                    x_load(q + 2, s)
                    sp.wait_ge(up_lo_done, q + 1)
                    sp.wait_ge(down_lo_done, q + 1)
                    w_load(q + 2, s)
                if left == 1:
                    for n in range(2):
                        sp.wait_ge(k_stored[n], 16 * KC)
                    sp.dma_start(k_nat, kernel_dram.rearrange("h m n -> h (m n)")).then_inc(kernel_in, 16)
                    sp.dma_start(fwd[:], dft_fwd).then_inc(fwd_in, 16)
                if not is_first(q):
                    y_store(q - 1, 1 - s)

            final_chunk, half = all_chunks(sp, chunk_loads)
            y_store(final_chunk, 0)

            sp.wait_ge(chunk_done, final_chunk + 1)
            sp.dma_start(vec_rows[:, 0], skip.partition_broadcast(P)).then_inc(rows_in, 16)
            sp.dma_start(vec_rows[:, 1], ln_w.partition_broadcast(P)).then_inc(rows_in, 16)
            sp.dma_start(vec_rows[:, 2], ln_b.partition_broadcast(P)).then_inc(rows_in, 16)
            for m in range(ME):
                sp.dma_start(z[:, m].rearrange("p c r w -> p (c r) w"),
                             x_hat_dram[m].rearrange("k p w -> p k w")).then_inc(spectra_in[m], 16)
            sp.wait_ge(y_stored[1], half * 16 + 16)
            sp.dma_start(inv[:], dft_inv).then_inc(inv_in, 16)
            sp.wait_ge(y_stored[0], half * 16 + 32)
            sp.sem_inc(outputs_out, 1)
            for g in range(G):
                if g >= 2:
                    sp.wait_ge(x_joined, g - 1)
                sp.dma_start(xs[:, g % 2].rearrange("p (b h) -> p b h", b=B),
                             x[:, g * P:(g + 1) * P, :].rearrange("b p h -> p b h")).then_inc(xs_in[g % 2], 16)
            sp.wait_ge(gates1_copied, 1)
            sp.dma_start(gates_dram.rearrange("(a t) e p -> (t e) a p", a=2), gates_t).then_inc(gates_out, 16)
            sp.wait_ge(gates_out, 16)
            sp.wait_ge(up1_done, 1)
            sp.wait_ge(pv_copied, B * G // 2)

            def gate1_load(g, e):
                src = gates_dram[bass.ds(g * B, B), e, :].partition_broadcast(P)
                sp.dma_start(gate_row1[:, e % 4, :].rearrange("p (b t) -> p b t", b=B), src).then_inc(gate1_in[e % 4], 16)

            for e in range(4):
                gate1_load(0, e)

            def gate1_loads(g, last):
                for e in range(E):
                    sp.wait_ge(part1_done, g * E + e + 1)
                    if e < 4:
                        gate1_load(g, e + 4)
                    elif not last:
                        gate1_load(g + 1, e - 4)
                    if last and e < G - 1:
                        store(e)

            def store(g):
                sp.wait_ge(added_done, g + 1)
                sp.dma_start(out[:, g * P:(g + 1) * P, :].rearrange("b p h -> p b h"),
                             final[:, g % 2].rearrange("p (b h) -> p b h", b=B)).then_inc(stored[g % 2], 16)

            with sp.Fori(0, G - 1) as g:
                gate1_loads(g, False)
            gate1_loads(G - 1, True)
            store(G - 1)
            for n in range(2):
                sp.wait_ge(stored[n], 16 * G // 2)

        @block.gpsimd
        def _(pool):
            nc.gpsimd.memset(zeros[:], 0.0).then_inc(zeros_done, 1)
            nc.gpsimd.memset(ident[:], 0.0).then_inc(pool_step, 1)
            nc.gpsimd.memset(before[:], 1.0).then_inc(pool_step, 1)
            nc.gpsimd.memset(ones[:], 1.0).then_inc(pool_step, 1)
            pool.wait_ge(pool_step, 3)
            nc.gpsimd.affine_select(out=ident[:], in_=ident[:], compare_op=ALU.not_equal, fill=1.0, base=0,
                                    pattern=[[-1, P]], channel_multiplier=1).then_inc(ident_done, 1)
            nc.gpsimd.affine_select(out=before[:], in_=before[:], compare_op=ALU.is_gt, fill=0.0, base=0,
                                    pattern=[[1, P]], channel_multiplier=-1).then_inc(ident_done, 1)
            for n, (_, _, col, cols) in enumerate(pieces1):
                pool.wait_ge(w1_hi_done, n + 1)
                nc.gpsimd.tensor_tensor(w_lo[:, col:col + cols], wst1[:, n % STAGES, 0:cols],
                                        w_hi[:, col:col + cols].bitcast(F32), ALU.subtract).then_inc(w1_lo_done, 1)

            of_slots = lambda k, t: bass.IndirectOffsetOnAxis(ap=slot[:, k, t:t + 1], axis=0)
            rows = lambda a, t: a[:, t // B, (t % B) * P:(t % B + 1) * P]
            pool.wait_ge(zeros_out, 16 * (-(-NC // 2) + 1))
            pool.wait_ge(slots_done, 4)
            for t in range(T):
                for k in range(2):
                    nc.gpsimd.indirect_dma_start(x_slots, of_slots(k, t), rows(xn, t), None).then_inc(scattered, 16)

            def hidden_low(q, j):
                pool.wait_ge(hid_done, q * J0 + j + 1)
                f = width0(j)
                nc.gpsimd.tensor_tensor(hid_lo[0:f, j], hid[0:f, j], hid_hi[0:f, j].bitcast(F32),
                                        ALU.subtract).then_inc(hid_lo_done, 1)

            def up_low(q, s):
                pool.wait_ge(up_hi_done, q + 1)
                nc.gpsimd.tensor_tensor(wc[:, s, 1, 0:WA], wraw[:, s, 0:WA], wc[:, s, 0, 0:WA].bitcast(F32),
                                        ALU.subtract).then_inc(up_lo_done, 1)

            def chunk_low(q, k, s, left):
                hidden_low(q, 0)
                if left:
                    up_low(q + 1, 1 - s)
                hidden_low(q, 1)
                hidden_low(q, 2)

            up_low(0, 0)
            all_chunks(pool, chunk_low)

            pool.wait_ge(outputs_out, 1)
            for t in range(T):
                nc.gpsimd.indirect_dma_start(rows(acc, t), None, y_slots, of_slots(0, t)).then_inc(rows_back[t // B], 16)
            pool.wait_ge(rows_in, 48)
            row = lambda i: vec_rows[:, i].unsqueeze(1).broadcast_to((P, B, P))
            for_batch = lambda a: a.rearrange("p (b h) -> p b h", b=B)
            def join_x(g):
                pool.wait_ge(xs_in[g % 2], 16 * (g // 2 + 1))
                nc.gpsimd.tensor_tensor(for_batch(xs[:, g % 2]), for_batch(xs[:, g % 2]), row(2), ALU.add).then_inc(xb_done, 1)
                pool.wait_ge(first_scaled, g + 1)
                pool.wait_ge(xb_done, g + 1)
                nc.gpsimd.tensor_tensor(acc[:, g], acc[:, g], xs[:, g % 2], ALU.add).then_inc(x_joined, 1)

            def second_outputs(g):
                pool.wait_ge(first_scaled, g + 1)
                for t in range(g * B, (g + 1) * B):
                    nc.gpsimd.indirect_dma_start(rows(second_part(g), t), None, y_slots, of_slots(1, t)).then_inc(rows_back[g], 16)

            pool.wait_ge(khat_mm, M)
            for g in range(2):
                second_outputs(g)
            for g in range(4):
                join_x(g)
            pool.wait_ge(z_ready, M)
            for g in range(G):
                pool.wait_ge(norm1_done, g + 1)
                nc.gpsimd.tensor_tensor(for_batch(xn[:, g]), for_batch(xn[:, g]), row(1), ALU.mult).then_inc(scaled_done, 1)
                if g + 2 < G:
                    second_outputs(g + 2)
                if g + 4 < G:
                    join_x(g + 4)

            for n in range(B * G):
                pool.wait_ge(inverse_done, n + 1)
                nc.gpsimd.tensor_tensor(prob[:, n % 2, C:], prob[:, n % 2, C:], sm[:, n % 2, 3:4].broadcast_to((P, L - C)),
                                        ALU.mult).then_inc(prob_done[1], 1)

        @block.scalar
        def _(act_e):
            copy = lambda dst, src: nc.scalar.activation(dst, src, ACT.Copy)
            w_next = [0]

            def weights(count):
                for n in range(w_next[0], min(w_next[0] + count, len(pieces1))):
                    _, _, col, cols = pieces1[n]
                    act_e.wait_ge(wst1_in[n % STAGES], 16 * (n // STAGES + 1))
                    copy(w_hi[:, col:col + cols], wst1[:, n % STAGES, 0:cols]).then_inc(w1_hi_done, 1)
                    w_next[0] = n + 1

            def root0(half):
                t = slice(half * T // 2, (half + 1) * T // 2)
                act_e.wait_ge(stats_done, half + 1)
                nc.scalar.activation(rstd[:, t], mv[:, t, 1], ACT.Sqrt, bias=eps[:]).then_inc(root_done, 1)

            root0(0)
            for g in range(G):
                act_e.wait_ge(xt_done, g + 1)
                copy(xt[:, g % 2], ps[:, g % 2]).then_inc(xt_copied, 1)
                if g == 1:
                    root0(1)
                weights(1 if g < 2 else 2)
            act_e.wait_ge(decay_done, 1)
            nc.scalar.activation(ks[:, 5], ks[:, 4], ACT.Tanh, scale=0.5).then_inc(trig_done, 1)
            nc.scalar.activation(ks[:, 6], ks[:, 4], ACT.Exp).then_inc(trig_done, 1)
            act_e.wait_ge(top2_done, 1)
            nc.scalar.activation(p2, m2, ACT.Exp).then_inc(top2_exp_done, 1)
            act_e.wait_ge(phase_done, 1)
            nc.scalar.activation(ks[:, 7], ks[:, 12], ACT.Sin, scale=TWO_PI).then_inc(trig_done, 1)
            nc.scalar.activation(ks[:, 8], ks[:, 12], ACT.Sin, scale=TWO_PI / 2).then_inc(trig_done, 1)
            weights(len(pieces1))

            def k_copy(c):
                for half in range(2):
                    act_e.wait_ge(k_mm_done, 2 * c + half + 1)
                    if c >= 2 and half == 0:
                        act_e.wait_ge(k_stored[c % 2], 32 * (c // 2))
                    copy(k_out[:, c % 2, half], ps[0:LO, k_bank(c) + half].rearrange("p (a b) -> p a b", a=CH)).then_inc(k_copied, 1)

            def spectra_copy(m):
                for k in range(4):
                    n = 4 * m + k
                    act_e.wait_ge(spectra_mm, n + 1)
                    if m:
                        act_e.wait_ge(spectra_stored[k], 16 * m)
                    copy(wst1[:, k], ps[:, k]).then_inc(spectra_copied, 1)
                    act_e.wait_ge(spectra_copied, n + 1)
                    act_e.dma_start(x_hat_dram[m, k], wst1[:, k]).then_inc(spectra_stored[k], 16)

            act_e.wait_ge(w1_lo_done, len(pieces1))
            spectra_copy(0)
            for c in range(KC):
                s = c % 2
                act_e.wait_ge(decay_done, c + 2)
                nc.scalar.activation(kc[:, s, 3], kc[:, s, 3], ACT.Exp).then_inc(exp_done, 1)
                act_e.wait_ge(phase_done, c + 2)
                nc.scalar.activation(kc[:, s, 4], kc[:, s, 0], ACT.Sin, scale=TWO_PI).then_inc(sin_done, 1)
                if c >= 2:
                    act_e.wait_ge(k_mm_done, 2 * c - 2)
                nc.scalar.activation(kc[:, s, 5], kc[:, s, 0], ACT.Sin, scale=TWO_PI / 2).then_inc(sin_done, 1)
                act_e.wait_ge(sin_done, 3 * c + 2)
                nc.scalar.activation(kc[:, s, 5], kc[:, s, 5], ACT.Square).then_inc(sin_done, 1)
                if c + 1 < ME:
                    spectra_copy(c + 1)
                if c >= 1:
                    k_copy(c - 1)

            def up_high(q, k, s):
                act_e.wait_ge(wraw_in[s], (k + 1) * 16)
                copy(wc[:, s, 0, 0:WA], wraw[:, s, 0:WA]).then_inc(up_hi_done, 1)

            def down_high(q, s):
                if not (isinstance(q, int) and q < 2):
                    act_e.wait_ge(chunk_done, q - 1)
                copy(wc[:, s, 0, WA:WC], wraw[:, s, WA:WC]).then_inc(down_hi_done, 1)

            def input_high(q, s):
                act_e.wait_ge(xct_done, q + 1)
                copy(xct_hi[:, s], ps[:, 6]).then_inc(xct_hi_done, 1)

            def output_half(q, k, s):
                act_e.wait_ge(chunk_done, q + 1)
                act_e.wait_ge(y_stored[s], (k + 1) * 16)
                copy(yo[:, s], y_parts[:, :, 1]).then_inc(y_half_copied, 1)

            def chunk_act(q, k, s, left):
                for j in range(J0):
                    f, r = width0(j), (s + j) % 2
                    act_e.wait_ge(up_done, q * J0 + j + 1)
                    nc.scalar.activation(act[0:f, r], ps[0:f, r], ACT.Silu).then_inc(act_done, 1)
                    if j == 1 and not is_first(q):
                        output_half(q - 1, k - (1 - s), 1 - s)
                    if not left:
                        continue
                    if j == 0:
                        up_high(q + 1, k + s, 1 - s)
                    elif j == 1:
                        input_high(q + 1, 1 - s)
                    else:
                        down_high(q + 1, 1 - s)

            act_e.wait_ge(tables_done, 2 * KC)
            act_e.wait_ge(w1_lo_done, len(pieces1))
            up_high(0, 0, 0)
            down_high(0, 0)
            k_copy(KC - 1)
            input_high(0, 0)
            final_chunk, half = all_chunks(act_e, chunk_act)
            output_half(final_chunk, half, 0)

            act_e.wait_ge(k_t_done, 1)
            for a in range(2):
                copy(k_t[:, 4 * a:4 * a + 4], ps[:, a].rearrange("p (t h) -> p t h", t=4)).then_inc(k_t_copied, 1)
            for m in range(M):
                act_e.wait_ge(khat_mm, m + 1)
                copy(khat[:, m].rearrange("p (c r) h -> p r c h", c=2),
                     ps[:, 4 + m].rearrange("p (r c h) -> p r c h", r=2, c=2)).then_inc(khat_copied, 1)

            def times_gates(y, k, g):
                for b in range(B):
                    c = slice(b * P, (b + 1) * P)
                    last = nc.scalar.activation(y[:, g, c], y[:, g, c], ACT.Copy, scale=gate2[:, k, g * B + b:g * B + b + 1])
                return last

            def second_times_gates(g):
                act_e.wait_ge(rows_back[g], 2 * 16 * B)
                times_gates(second_part(g), 1, g).then_inc(second_scaled, 1)

            def root(i, g, signal, stats_ready):
                act_e.wait_ge(stats_ready, g + 1)
                nc.scalar.activation(mid[:, g % 2, i, 0], mid_mv[:, g % 2, i, :, 1], ACT.Sqrt, bias=eps[:]).then_inc(signal, 1)

            def normalised(dst, src, i, g, ready, signal):
                act_e.wait_ge(ready, g + 1)
                for b in range(B):
                    c = slice(b * P, (b + 1) * P)
                    last = nc.scalar.activation(dst[:, c], src[:, c], ACT.Identity, bias=mid[:, g % 2, i, 2, b:b + 1],
                                                scale=mid[:, g % 2, i, 0, b:b + 1])
                last.then_inc(signal, 1)

            def high_part(g):
                act_e.wait_ge(xt1_done, g + 1)
                copy(xt1_hi[:, g], ps[:, 4 + g % 2]).then_inc(xt1_hi_done, 1)

            for g in range(G):
                act_e.wait_ge(rows_back[g], 16 * B)
                times_gates(acc, 0, g).then_inc(first_scaled, 1)
            for g in range(2):
                second_times_gates(g)
            for i in range(G + 2):
                if i < G:
                    root(0, i, root1_done, mid_stats)
                if 1 <= i <= G:
                    root(1, i - 1, root2_done, mid_stats2)
                if i >= 2:
                    high_part(i - 2)
                if i < G:
                    normalised(xn[:, i], ps[:, i % 4], 0, i, norm1_ready, norm1_done)
                if 1 <= i <= G:
                    normalised(xn1[:, (i - 1) % 2], xn[:, i - 1], 1, i - 1, norm2_ready, xn1_done)
                if 2 <= i + 1 < G:
                    second_times_gates(i + 1)

            def qkv_high(m):
                act_e.wait_ge(qkv_mm, m + 1)
                copy(qkv_dst(m, q_hi, k_hi, v_hi), qkv_src(m)).then_inc(qkv_hi_done, 1)

            def turned_high(n):
                for a in range(2):
                    act_e.wait_ge(pt_done, 2 * n + a + 1)
                    copy(turned_dst(pt_hi, n, a), turned_src(a)).then_inc(pt_hi_done, 1)

            def softmax_exp(n):
                act_e.wait_ge(max_done, n + 1)
                nc.scalar.activation(prob[:, n % 2], ps[:, 2 * (n % 2):2 * (n % 2) + 2].rearrange("p a w -> p (a w)"), ACT.Exp,
                                     bias=sm[:, n % 2, 1:2], scale=SCALE, accum_out=sm[:, n % 2, 2:3]).then_inc(exp1_done, 1)

            def attended(k):
                act_e.wait_ge(pv_done, k + 1)
                b, t = divmod(2 * k, G)
                copy(acc[:, t:t + 2, b * P:(b + 1) * P], ps[:, 6, 0:2 * P].rearrange("p (t j) -> p t j", t=2)).then_inc(pv_copied, 1)

            for m in range(4):
                qkv_high(m)
            softmax_exp(0)
            softmax_exp(1)
            for n in range(B * G):
                if n == 1:
                    act_e.wait_ge(gate_soft, 1)
                    nc.scalar.activation(gl[:, :, 0:E], gl[:, :, 0:E], ACT.Exp).then_inc(gate_exp_done, 1)
                    nc.scalar.activation(gl[:, :, E:E + 1], gl[:, :, E:E + 1], ACT.Tanh, scale=0.5).then_inc(gate_exp_done, 1)
                turned_high(n)
                if n == 4:
                    act_e.wait_ge(gates1_turned, 1)
                    copy(gates_t, ps[:, 7, 0:2 * P].rearrange("p (a t) -> p a t", a=2)).then_inc(gates1_copied, 1)
                if n % 2 == 0 and n >= 4:
                    attended(n // 2 - 2)
                if qkv_after(n) is not None:
                    qkv_high(qkv_after(n))
                if n + 2 < B * G:
                    softmax_exp(n + 2)
            for k in range(2):
                attended(B * G // 2 - 2 + k)

            def hidden1(g):
                for u in range(UN1):
                    act_e.wait_ge(up1_done, g * UN1 + u + 1)
                    nc.scalar.activation(hid1[:, u % 4], ps[:, u % 4], ACT.Gelu_apprx_tanh, bias=b1_sb[:, u:u + 1])
                    nc.scalar.activation(hid1_hi[:, u % 4], ps[:, u % 4], ACT.Gelu_apprx_tanh,
                                         bias=b1_sb[:, u:u + 1]).then_inc(hid1_done, 1)

            with act_e.Fori(0, G) as g:
                hidden1(g)

        @block.vector
        def _(dve):
            step = Tally(dve_step)
            need = lambda v: dve.wait_ge(dve_step, v)
            tt, ts, stt = nc.vector.tensor_tensor, nc.vector.tensor_scalar, nc.vector.scalar_tensor_tensor
            mul, add, sub = ALU.mult, ALU.add, ALU.subtract
            K = lambda i: ks[:, i]
            a_im, c_re, c_im = small[:, 1], small[:, 2], small[:, 3]
            step.mark(nc.vector.memset(eps[:], LN_EPS))

            def inverse_root(r, var, t):
                v = step.mark(nc.vector.reciprocal(r, r))
                need(v)
                v = step.mark(tt(t, r, r, mul))
                need(v)
                v = step.mark(stt(t, var, LN_EPS, t, add, mul))
                need(v)
                v = step.mark(ts(t, t, -0.5, 1.5, mul, add))
                need(v)
                v = step.mark(tt(r, r, t, mul))
                need(v)

            def moments0(g, signal=False):
                dve.wait_ge(x_in[g], 16)
                for b in range(B):
                    st = (g % 2) * B + b
                    v = step.mark(nc.vector.bn_stats(stats[:, st], xn[:, g, b * P:(b + 1) * P]))
                need(v)
                for b in range(B):
                    last = nc.vector.bn_aggr(mv[:, g * B + b], stats[:, (g % 2) * B + b])
                if signal:
                    last.then_inc(stats_done, 1)
                else:
                    step.mark(last)

            def normalise0(half):
                t = slice(half * T // 2, (half + 1) * T // 2)
                dve.wait_ge(root_done, half + 1)
                inverse_root(rstd[:, t], mv[:, t, 1], newton[:, t])
                for g in range(half * G // 2, (half + 1) * G // 2):
                    for b in range(B):
                        t = g * B + b
                        v = nc.vector.tensor_scalar(xn[:, g, b * P:(b + 1) * P], xn[:, g, b * P:(b + 1) * P],
                                                    mv[:, t, 0:1], rstd[:, t:t + 1], sub, mul)
                    v.then_inc(xn_ready, 1)

            for g in range(5):
                moments0(g, signal=(g == 3))
            normalise0(0)
            for g in range(5, G):
                moments0(g, signal=(g == G - 1))
            normalise0(1)

            dve.wait_ge(small_in, 80)
            step.mark(nc.vector.tensor_copy(ks[:, 1], ks[:, 0]))
            v = step.mark(nc.vector.tensor_copy(ks[:, 2], small[:, 0]))
            pair = lambda i: ks[:, i:i + 2]
            X, NN, R, PP = pair(1), pair(5), pair(7), pair(9)
            need(v)
            v = step.mark(ts(X, X, 88.0, -87.0, ALU.min, ALU.max))
            need(v)
            v = step.mark(ts(NN, X, 1.0 / math.log(2.0), None, mul))
            need(v)
            v = step.mark(ts(NN, NN, MAGIC, MAGIC, add, sub))
            need(v)
            v = step.mark(stt(R, NN, -LN2_HI, X, mul, add))
            need(v)
            v = step.mark(stt(R, NN, -LN2_LO, R, mul, add))
            need(v)
            v = step.mark(ts(PP, R, 1.0 / math.factorial(7), None, mul))
            for k in range(6, 0, -1):
                need(v)
                v = step.mark(stt(PP, PP, 1.0 / math.factorial(k), R, add, mul))
            power = exp2[:].rearrange("p (a h) -> p a h", a=2)
            v = step.mark(ts(power, NN, 127.0, 2.0 ** 23, add, mul))
            need(v)
            v = step.mark(stt(X, PP, 1.0, power.bitcast(F32), add, mul))
            need(v)
            s_th = step.mark(tt(K(9), K(1), a_im, mul))
            step.mark(ts(K(3), K(2), -1.0, None, mul))
            nc.vector.scalar_tensor_tensor(K(4), K(2), -1.0, K(1), mul, mul).then_inc(decay_done, 1)
            need(s_th)
            v = step.mark(nc.vector.tensor_copy(th_hi[:], K(9)))
            need(v)
            step.mark(tt(K(10), K(9), th_hi[:].bitcast(F32), sub))
            v = step.mark(ts(K(11), th_hi[:].bitcast(F32), INV_2PI_HI, None, mul))
            need(v)
            v = step.mark(ts(K(12), K(11), MAGIC, MAGIC, add, sub))
            need(v)
            step.mark(tt(K(11), K(11), K(12), sub))
            v = step.mark(ts(K(13), K(10), INV_2PI_HI, None, mul))
            need(v)
            v = step.mark(stt(K(13), K(9), INV_2PI_LO, K(13), mul, add))
            need(v)
            v = step.mark(tt(K(14), K(11), K(13), add))
            need(v)
            v = step.mark(ts(K(15), K(14), MAGIC_13, MAGIC_13, add, sub))
            need(v)
            v = step.mark(tt(K(11), K(11), K(15), sub))
            need(v)
            v = step.mark(tt(K(16), K(11), K(13), add))
            step.mark(ts(K(12), K(14), MAGIC, MAGIC, add, sub))
            need(step.n)
            nc.vector.tensor_tensor(K(12), K(14), K(12), sub).then_inc(phase_done, 1)
            wide = lambda a: a.unsqueeze(2).broadcast_to((P, T, E))
            revb = rev.unsqueeze(1).broadcast_to((P, T, E))
            dve.wait_ge(logits_done, G)
            v = step.mark(nc.vector.tensor_copy(lg, ps[:, 2, 0:T * E].rearrange("p (t e) -> p t e", e=E)))
            need(v)
            for m, p, oh, low in ((m1, p1, oh1, False), (m2, p2, oh2, True)):
                v = step.mark(nc.vector.reduce_max(m, lg, AX.X))
                need(v)
                v = step.mark(tt(eq, lg, wide(m), ALU.is_equal))
                need(v)
                v = step.mark(tt(k2, eq, revb, mul))
                need(v)
                v = step.mark(nc.vector.reduce_max(p, k2, AX.X))
                need(v)
                v = step.mark(tt(oh, k2, wide(p), ALU.is_equal))
                need(v)
                if not low:
                    v = step.mark(stt(lg, oh, -3.0e38, lg, mul, add))
                    need(v)
            tt(m2, m2, m1, sub).then_inc(top2_done, 1)
            tt(member, oh1, oh2, add).then_inc(member_done, 1)
            dve.wait_ge(top2_exp_done, 1)
            v = step.mark(ts(p1, p2, 1.0, None, add))
            need(v)
            v = step.mark(nc.vector.reciprocal(p1, p1))
            need(v)
            tt(p2, p2, p1, mul).then_inc(gate2_done, 1)
            step.mark(nc.vector.tensor_copy(gate2[:, 0], p1))
            dve.wait_ge(gate2_done, 1)
            step.mark(nc.vector.tensor_copy(gate2[:, 1], p2))

            dve.wait_ge(counted, 1)
            before_in_tile = ps[:, 3, 0:T * E].rearrange("p (t e) -> p t e", e=E)
            in_tile = ps[:, 3, T * E:2 * T * E].rearrange("p (t e) -> p t e", e=E)
            v = step.mark(nc.vector.tensor_copy(count_a, in_tile))
            step.mark(nc.vector.tensor_copy(rank, before_in_tile))
            src, dst, d = count_a, count_b, 1
            while d < T:
                need(step.n)
                step.mark(nc.vector.tensor_copy(dst[:, 0:d], src[:, 0:d]))
                step.mark(tt(dst[:, d:], src[:, d:], src[:, :T - d], add))
                src, dst, d = dst, src, 2 * d
            need(step.n)
            v = step.mark(tt(dst, src, in_tile, sub))
            R_ = lambda i: route[:, i]
            step.mark(ts(R_(0), src[:, T - 1], 1.0 / W, (W - 1) / 2.0 / W, mul, add))
            need(step.n)
            step.mark(tt(rank, rank, dst, add))
            v = step.mark(ts(R_(0), R_(0), MAGIC, MAGIC, add, sub))
            need(v)
            a, b_, d = 0, 1, 1
            while d < E:
                need(step.n)
                step.mark(nc.vector.tensor_copy(R_(b_)[:, 0:d], R_(a)[:, 0:d]))
                step.mark(tt(R_(b_)[:, d:], R_(a)[:, d:], R_(a)[:, :E - d], add))
                a, b_, d = b_, b_ + 1, 2 * d
            need(step.n)
            v = step.mark(tt(R_(5), R_(a), R_(0), sub))
            need(v)
            v = step.mark(ts(R_(5), R_(5), float(W), None, mul))
            need(v)
            v = step.mark(tt(rank, rank, R_(5).unsqueeze(1).broadcast_to((P, T, E)), add))
            need(v)
            step.mark(tt(oh1, oh1, rank, mul))
            v = step.mark(tt(oh2, oh2, rank, mul))
            need(v)
            step.mark(nc.vector.reduce_sum(slot_f[:, 0], oh1, AX.X))
            v = step.mark(nc.vector.reduce_sum(slot_f[:, 1], oh2, AX.X))
            v3 = step.mark(ts(R_(6)[:, 0:1], R_(a)[:, E - 1:E], 0.5, -1.25, mul, add))
            need(v3)
            v3 = step.mark(ts(R_(6)[:, 0:1], R_(6)[:, 0:1], MAGIC, MAGIC, add, sub))
            need(v3)
            done = eq.rearrange("p t e -> p (t e)")[:, 0:NC * E].rearrange("p (q e) -> p q e", e=E)
            v2 = step.mark(tt(done, lagv[:, 0:NC].unsqueeze(2).broadcast_to((P, NC, E)),
                              R_(a).unsqueeze(1).broadcast_to((P, NC, E)), ALU.is_ge))
            need(v2)
            nc.vector.tensor_copy(pairs[:], R_(6)[:, 0:1]).then_inc(slots_done, 1)
            nc.vector.tensor_copy(slot[:, 0], slot_f[:, 0]).then_inc(slots_done, 1)
            nc.vector.tensor_copy(slot[:, 1], slot_f[:, 1]).then_inc(slots_done, 1)
            v = step.mark(nc.vector.reduce_sum(expert_f[:], done, AX.X))
            need(v)
            ts(expert_of[:], expert_f[:], float(E - 1), None, ALU.min).then_inc(slots_done, 1)

            step.mark(tt(K(17), K(3), K(3), mul))
            v = step.mark(tt(K(18), a_im, a_im, mul))
            need(v)
            v = step.mark(tt(K(17), K(17), K(18), add))
            need(v)
            v = step.mark(nc.vector.reciprocal(K(17), K(17)))
            need(v)
            v = step.mark(ts(K(17), K(17), 2.0 / C, None, mul))
            dve.wait_ge(trig_done, 4)
            step.mark(tt(K(8), K(8), K(8), mul))
            step.mark(tt(K(7), K(7), K(6), mul))
            v = step.mark(stt(K(5), K(6), 1.0, K(5), add, mul))
            need(v)
            v = step.mark(tt(K(8), K(8), K(6), mul))
            need(v)
            v = step.mark(stt(K(8), K(8), -2.0, K(5), mul, add))
            need(v)
            step.mark(tt(K(18), K(8), K(3), mul))
            step.mark(tt(K(19), K(7), a_im, mul))
            step.mark(tt(K(20), K(7), K(3), mul))
            v = step.mark(tt(K(21), K(8), a_im, mul))
            need(v)
            step.mark(tt(K(18), K(18), K(19), add))
            v = step.mark(tt(K(20), K(20), K(21), sub))
            need(v)
            step.mark(tt(K(18), K(18), K(17), mul))
            v = step.mark(tt(K(20), K(20), K(17), mul))
            need(v)
            step.mark(tt(K(19), c_re, K(18), mul))
            step.mark(tt(K(21), c_im, K(20), mul))
            step.mark(tt(K(22), c_re, K(20), mul))
            v = step.mark(tt(K(23), c_im, K(18), mul))
            need(v)
            step.mark(tt(K(19), K(19), K(21), sub))
            v = step.mark(tt(K(22), K(22), K(23), add))
            need(v)
            v = step.mark(ts(K(21), K(19), -1.0, None, mul))
            FH, FL, AR, CTR, CTI, NCTR = K(15), K(16), K(4), K(19), K(22), K(21)

            lag = lagv.unsqueeze(1).broadcast_to((P, CH, LAGS))
            lo, hi = slice(0, LO), slice(LO, LAGS)

            def angles(c):
                k = lambda i: kc[:, c % 2, i]
                col = lambda a: a[:, c * CH:(c + 1) * CH].unsqueeze(2).broadcast_to((P, CH, LAGS))
                v1 = step.mark(tt(k(0), col(FH), lag, mul))
                v2 = step.mark(tt(k(2), col(FL), lag, mul))
                tt(k(3), col(AR), lag, mul).then_inc(decay_done, 1)
                need(v1)
                v1 = step.mark(ts(k(1), k(0), MAGIC, MAGIC, add, sub))
                need(v1)
                v1 = step.mark(tt(k(0), k(0), k(1), sub))
                need(v1)
                v1 = step.mark(tt(k(0), k(0), k(2), add))
                need(v1)
                v1 = step.mark(ts(k(1), k(0), MAGIC, MAGIC, add, sub))
                need(v1)
                tt(k(0), k(0), k(1), sub).then_inc(phase_done, 1)

            def powers(c):
                k = lambda i: kc[:, c % 2, i]
                g_ = lambda i: kg[:, c % 2, i]
                col = lambda a: a[:, c * CH:(c + 1) * CH].unsqueeze(2).broadcast_to((P, CH, LO))
                dve.wait_ge(sin_done, 3 * c + 3)
                v1 = step.mark(ts(k(1), k(5), -2.0, 1.0, mul, add))
                dve.wait_ge(exp_done, c + 1)
                if c >= 2:
                    dve.wait_ge(k_mm_done, 2 * c - 2)
                step.mark(tt(k(6), k(3), k(4), mul))
                need(v1)
                v2 = step.mark(tt(k(5), k(3), k(1), mul))
                need(v2)
                step.mark(tt(g_(0), col(CTR), k(5)[:, :, hi], mul))
                step.mark(tt(g_(2), col(CTI), k(6)[:, :, hi], mul))
                step.mark(tt(g_(1), col(NCTR), k(6)[:, :, hi], mul))
                v4 = step.mark(tt(g_(3), col(CTI), k(5)[:, :, hi], mul))
                need(v4)
                tt(g_(0), g_(0), g_(2), sub).then_inc(tables_done, 1)
                tt(g_(1), g_(1), g_(3), sub).then_inc(tables_done, 1)

            angles(0)
            for c in range(KC):
                if c + 1 < KC:
                    angles(c + 1)
                powers(c)

            def input_low(q, s):
                dve.wait_ge(xct_hi_done, q + 1)
                tt(xct_lo[:, s], ps[:, 6], xct_hi[:, s].bitcast(F32), sub).then_inc(xct_lo_done, 1)

            def down_low(q, s):
                dve.wait_ge(down_hi_done, q + 1)
                tt(wc[:, s, 1, WA:WC], wraw[:, s, WA:WC], wc[:, s, 0, WA:WC].bitcast(F32), sub).then_inc(down_lo_done, 1)

            def output(q, s):
                dve.wait_ge(y_half_copied, q + 1)
                tt(yo[:, s], yo[:, s], y_parts[:, :, 0], add).then_inc(y_copied, 1)

            def chunk_hidden(q, k, s, left):
                for j in range(J0):
                    f, r = width0(j), (s + j) % 2
                    dve.wait_ge(act_done, q * J0 + j + 1)
                    tt(hid[0:f, j], act[0:f, r], ps[0:f, 2 + r], mul)
                    tt(hid_hi[0:f, j], act[0:f, r], ps[0:f, 2 + r], mul).then_inc(hid_done, 1)
                    if j == 1:
                        if not is_first(q):
                            output(q - 1, 1 - s)
                        if left:
                            input_low(q + 1, 1 - s)
                    if j == 2 and left:
                        down_low(q + 1, 1 - s)

            down_low(0, 0)
            dve.wait_ge(scattered, 16 * 2 * T)
            dve.wait_ge(k_copied, 2 * KC)
            input_low(0, 0)
            final_chunk, _ = all_chunks(dve, chunk_hidden)
            output(final_chunk, 0)

            dve.wait_ge(outputs_out, 1)
            wide3 = lambda a: a.rearrange("p (b h) -> p b h", b=B)
            T_ = lambda i: prod[:, i]
            dve.wait_ge(rows_in, 48)
            v = step.mark(ts(vec_rows[:, 0], vec_rows[:, 0], 1.0, 1.0 / C, add, mul))
            need(v)
            for m in range(M):
                X = (lambda c, ri: ps[:, 4 + 2 * c + ri]) if m == ME else (lambda c, ri: z[:, m, c, ri])
                Z = lambda c, ri: z[:, m, c, ri]
                K_ = lambda kind: khat[:, m, kind].unsqueeze(1).broadcast_to((P, B, P))
                o_re, o_im = (sub, add) if m < M // 2 else (add, sub)
                dve.wait_ge(khat_copied, m + 1)
                v = step.mark(tt(khat[:, m, 0], khat[:, m, 0], vec_rows[:, 0], add))
                need(v)
                tt(khat[:, m, 2], khat[:, m, 2], khat[:, m, 1], o_re).then_inc(khat_ready, 1)
                tt(khat[:, m, 3], khat[:, m, 3], khat[:, m, 0], o_im).then_inc(khat_ready, 1)
                dve.wait_ge(khat_ready, 2 * m + 2)
                dve.wait_ge(x_hat_done, 1) if m == ME else dve.wait_ge(spectra_in[m], 16)
                dve.wait_ge(z_ready, m) if m else dve.wait_ge(k_t_done, 1)
                for n, (ri, kind) in enumerate(((0, 0), (1, 1), (0, 1), (1, 0), (0, 2), (1, 3), (0, 3), (1, 2))):
                    v = step.mark(tt(wide3(T_(n)), wide3(X(0, ri)), K_(kind), mul))
                need(v)
                step.mark(tt(Z(0, 0), T_(0), T_(1), sub))
                step.mark(tt(Z(0, 1), T_(2), T_(3), add))
                step.mark(tt(T_(4), T_(4), T_(5), sub))
                v = step.mark(tt(T_(6), T_(6), T_(7), add))
                need(v)
                for n, (ri, kind) in enumerate(((0, 0), (1, 1), (0, 1), (1, 0))):
                    last = tt(wide3(T_(n)), wide3(X(1, ri)), K_(kind), mul)
                last.then_inc(products_done, 1)
                dve.wait_ge(products_done, m + 1)
                step.mark(tt(T_(0), T_(0), T_(1), sub))
                v = step.mark(tt(T_(2), T_(2), T_(3), add))
                need(v)
                tt(Z(1, 0), T_(4), T_(0), add)
                tt(Z(1, 1), T_(6), T_(2), add).then_inc(z_ready, 1)

            def moments(src, i, g, signal):
                for b in range(B):
                    v = step.mark(nc.vector.bn_stats(stats[:, i * B + b], src[:, b * P:(b + 1) * P]))
                need(v)
                for b in range(B):
                    last = nc.vector.bn_aggr(mid_mv[:, g % 2, i, b], stats[:, i * B + b])
                last.then_inc(signal, 1)

            def norm_factors(i, g, root_done_, signal):
                m, mv_ = mid[:, g % 2, i], mid_mv[:, g % 2, i]
                dve.wait_ge(root_done_, g + 1)
                inverse_root(m[:, 0], mv_[:, :, 1], m[:, 1])
                stt(m[:, 2], mv_[:, :, 0], -1.0, m[:, 0], mul, mul).then_inc(signal, 1)

            def residual(g):
                dve.wait_ge(y_done, g + 1)
                moments(ps[:, g % 4], 0, g, mid_stats)

            def layer0_sum(g):
                dve.wait_ge(second_scaled, g + 1)
                dve.wait_ge(x_joined, g + 1)
                v = step.mark(tt(acc[:, g], acc[:, g], second_part(g)[:, g], add))
                dve.wait_ge(scaled_done, g + 1)
                need(v)
                tt(xn[:, g], xn[:, g], acc[:, g], add).then_inc(x1_done, 1)
                dve.wait_ge(x1_done, g + 1)
                moments(xn[:, g], 1, g, mid_stats2)

            def low1(g):
                dve.wait_ge(xt1_hi_done, g + 1)
                tt(xt1_lo[:, g], ps[:, 4 + g % 2], xt1_hi[:, g].bitcast(F32), sub).then_inc(xt1_lo_done, 1)

            for i in range(G + 2):
                if i < G:
                    residual(i)
                if 1 <= i <= G:
                    layer0_sum(i - 1)
                if i < G:
                    norm_factors(0, i, root1_done, norm1_ready)
                if 1 <= i <= G:
                    norm_factors(1, i - 1, root2_done, norm2_ready)
                if i >= 2:
                    low1(i - 2)

            def qkv_low(m):
                dve.wait_ge(qkv_hi_done, m + 1)
                tt(qkv_dst(m, q_lo, k_lo, v_lo), qkv_src(m), qkv_dst(m, q_hi, k_hi, v_hi).bitcast(F32), sub).then_inc(qkv_lo_done, 1)

            def row_max(n):
                s = n % 2
                dve.wait_ge(s_done, n + 1)
                v = step.mark(nc.vector.reduce_max(sm[:, s, 0:1], ps[:, 2 * s:2 * s + 2].rearrange("p a w -> p (a w)"), AX.X))
                need(v)
                ts(sm[:, s, 1:2], sm[:, s, 0:1], -SCALE, None, mul).then_inc(max_done, 1)

            def inverse_sum(n):
                s = n % 2
                dve.wait_ge(exp1_done, n + 1)
                nc.vector.reciprocal(sm[:, s, 3:4], sm[:, s, 2:3]).then_inc(inverse_done, 1)
                dve.wait_ge(inverse_done, n + 1)
                ts(prob[:, s, 0:C], prob[:, s, 0:C], sm[:, s, 3:4], None, mul).then_inc(prob_done[0], 1)

            def turned_low(n):
                for a in range(2):
                    dve.wait_ge(pt_hi_done, 2 * n + a + 1)
                    tt(turned_dst(pt_lo, n, a), turned_src(a), turned_dst(pt_hi, n, a).bitcast(F32), sub).then_inc(pt_lo_done, 1)

            gw, thr = gl[:, :, 0:E], gl[:, :, E:E + 1]
            per_token = lambda i: gs[:, i].unsqueeze(2).broadcast_to((P, T, E))

            def gate_logits():
                dve.wait_ge(biases_in, 48)
                dve.wait_ge(logits1_done, G)
                v = step.mark(tt(gl[:], ps[:, 6, 0:T * GW].rearrange("p (t e) -> p t e", e=GW),
                                 bias1[:].unsqueeze(1).broadcast_to((P, T, GW)), add))
                need(v)
                v = step.mark(nc.vector.reduce_max(gs[:, 0], gw, AX.X))
                need(v)
                tt(gw, gw, per_token(0), sub).then_inc(gate_soft, 1)

            def gate_weights():
                dve.wait_ge(gate_exp_done, 2)
                step.mark(nc.vector.reduce_sum(gs[:, 0], gw, AX.X))
                v = step.mark(ts(thr, thr, THRESHOLD / 2, THRESHOLD / 2, mul, add))
                need(v)
                v = step.mark(nc.vector.reciprocal(gs[:, 0], gs[:, 0]))
                need(v)
                v = step.mark(tt(gw, gw, per_token(0), mul))
                need(v)
                v = step.mark(tt(gw, gw, thr.broadcast_to((P, T, E)), sub))
                need(v)
                v = step.mark(ts(gw, gw, 0.0, None, ALU.max))
                need(v)
                v = step.mark(nc.vector.reduce_sum(gs[:, 0], gw, AX.X))
                need(v)
                v = step.mark(ts(gs[:, 1], gs[:, 0], 0.0, None, ALU.is_equal))
                need(v)
                v = step.mark(tt(gs[:, 0], gs[:, 0], gs[:, 1], add))
                need(v)
                v = step.mark(nc.vector.reciprocal(gs[:, 0], gs[:, 0]))
                need(v)
                tt(gates[:], gw, per_token(0), mul).then_inc(gates1_done, 1)

            for m in range(4):
                qkv_low(m)
            row_max(0)
            row_max(1)
            inverse_sum(0)
            for n in range(B * G):
                if n == 0:
                    gate_logits()
                if n == 3:
                    gate_weights()
                if n + 2 < B * G:
                    row_max(n + 2)
                if n + 1 < B * G:
                    inverse_sum(n + 1)
                turned_low(n)
                if qkv_after(n) is not None:
                    qkv_low(qkv_after(n))

            def weigh1(g, e):
                dve.wait_ge(gate1_in[e % 4], 16 * (2 * g + e // 4 + 1))
                dve.wait_ge(expert1_done, g * E + e + 1)
                stt(part1[:, e % 2], ps[:, 4 + e % 2], b2_sb[:, e:e + 1], gate_row1[:, e % 4], add, mul).then_inc(part1_done, 1)

            def join1(g, e):
                a = acc[:, bass.ds(g, 1), :].rearrange("p a w -> p (a w)")
                dve.wait_ge(part1_done, g * E + e + 1)
                if e:
                    dve.wait_ge(join1_done, g * E + e)
                tt(a, a, part1[:, e % 2], add).then_inc(join1_done, 1)

            def add_final(g):
                if g >= 2:
                    dve.wait_ge(stored[g % 2], 16 * (g // 2))
                dve.wait_ge(final_done, g + 1)
                tt(final[:, g % 2], ps[:, 6 + g % 2], xn[:, g], add).then_inc(added_done, 1)

            def hidden1(g, first=False, last=False):
                for u in range(UN1):
                    e, j = divmod(u, J1)
                    dve.wait_ge(hid1_done, g * UN1 + u + 1)
                    tt(hid1_lo[:, u % 4], hid1[:, u % 4], hid1_hi[:, u % 4].bitcast(F32), sub).then_inc(hid1_lo_done, 1)
                    if not (first and e == 0):
                        to, ex = (g, e - 1) if e else (g - 1, E - 1)
                        if j == 2:
                            weigh1(to, ex)
                        if j == 3:
                            join1(to, ex)
                    if last and j == 1 and e >= 1:
                        add_final(e - 1)

            dve.wait_ge(pv_copied, B * G // 2)
            hidden1(0, first=True)
            with dve.Fori(1, G - 1) as g:
                hidden1(g)
            hidden1(G - 1, last=True)
            weigh1(G - 1, E - 1)
            join1(G - 1, E - 1)
            add_final(G - 1)

        @block.tensor
        def _(pe):
            mm = nc.tensor.matmul

            def three(dst, a_hi, a_lo, b_hi, b_lo, first=True, last=True):
                mm(dst, a_lo, b_hi, start=first, stop=False)
                mm(dst, a_hi, b_lo, start=False, stop=False)
                return mm(dst, a_hi, b_hi, start=False, stop=last)

            pe.wait_ge(ident_done, 1)
            pe.wait_ge(small_in, 80)

            def logits(g):
                pe.wait_ge(xt_copied, g + 1)
                for b in range(B):
                    o = ps[:, 2, (g * B + b) * E:(g * B + b + 1) * E]
                    last = mm(o, xt[:, g % 2, b * P:(b + 1) * P], wg0_sb[:], start=True, stop=True)
                last.then_inc(logits_done, 1)

            for g in range(G):
                pe.wait_ge(xn_ready, g + 1)
                for b in range(B):
                    last = nc.tensor.transpose(ps[:, g % 2, b * P:(b + 1) * P], xn[:, g, b * P:(b + 1) * P], ident[:])
                last.then_inc(xt_done, 1)
                if g >= 1:
                    logits(g - 1)
            logits(G - 1)
            pe.wait_ge(member_done, 1)
            pe.wait_ge(ident_done, 2)
            chosen = member.rearrange("p t e -> p (t e)")
            mm(ps[:, 3, 0:T * E], before[:], chosen, start=True, stop=True)
            mm(ps[:, 3, T * E:2 * T * E], ones[:], chosen, start=True, stop=True).then_inc(counted, 1)

            def spectra(m):
                for k in range(4):
                    c, part_ = divmod(k, 2)
                    if m:
                        pe.wait_ge(spectra_copied, 4 * (m - 1) + k + 1)
                    elif k == 3:
                        pe.wait_ge(slots_done, 1)
                    for t in range(CT):
                        last = mm(ps[:, k], fwd0[:, t, part_, m * P:(m + 1) * P], xn[:, c * CT + t],
                                  start=(t == 0), stop=(t == CT - 1))
                    last.then_inc(spectra_mm, 1)

            pe.wait_ge(fwd0_in, 16)
            for m in range(ME):
                spectra(m)
            for c in range(KC):
                pe.wait_ge(tables_done, 2 * c + 2)
                if c >= 2:
                    pe.wait_ge(k_copied, 2 * c - 2)
                for half in range(2):
                    states = slice(half * N, (half + 1) * N)
                    for h in range(CH):
                        o = ps[0:LO, k_bank(c) + half, h * LO:(h + 1) * LO]
                        mm(o, kg[states, c % 2, 0, h, :], kc[states, c % 2, 5, h, 0:LO], start=True, stop=False)
                        last = mm(o, kg[states, c % 2, 1, h, :], kc[states, c % 2, 6, h, 0:LO], start=False, stop=True)
                    last.then_inc(k_mm_done, 1)

            def turn_inputs(q, k, s):
                pe.wait_ge(xc_in[s], (k + 1) * 16)
                for t in range(4):
                    last = nc.tensor.transpose(ps[:, 6, t * P:(t + 1) * P], xc[:, s, t], ident[:])
                last.then_inc(xct_done, 1)

            def up(s, j):
                f, r = width0(j), (s + j) % 2
                for bank, col in ((r, 0), (2 + r, HID0)):
                    w = slice(col + j * P, col + j * P + f)
                    last = three(ps[0:f, bank], wc[:, s, 0, w], wc[:, s, 1, w], xct_hi[:, s], xct_lo[:, s])
                last.then_inc(up_done, 1)

            def down(q, s, j):
                f = width0(j)
                pe.wait_ge(hid_lo_done, q * J0 + j + 1)
                if j == 0:
                    pe.wait_ge(down_lo_done, q + 1)
                    if is_first(q):
                        pe.wait_ge(k_copied, 2 * KC)
                    else:
                        pe.wait_ge(y_copied, q)
                w = wc[0:f, s, :, WA + j * P:WA + (j + 1) * P]
                for t in range(4):
                    o = ps[:, 4 + t // 2, (t % 2) * 2 * P:(t % 2 + 1) * 2 * P].rearrange("p (i c) -> p i c", i=2)
                    mm(o, hid_lo[0:f, j, t * P:(t + 1) * P], w, start=(j == 0 and t % 2 == 0), stop=False)
                    last = mm(o, hid_hi[0:f, j, t * P:(t + 1) * P], w, start=False, stop=(j == J0 - 1 and t % 2 == 1))
                if j == J0 - 1:
                    last.then_inc(chunk_done, 1)

            def chunk_products(q, k, s, left):
                for j in range(J0):
                    if j == 0 and left:
                        turn_inputs(q + 1, k + s, 1 - s)
                    if j == 0 or left:
                        pe.wait_ge(hid_done, q * J0 + j + 1)
                    if j == 0:
                        up(s, 2)
                    elif left:
                        if j == 1:
                            pe.wait_ge(xct_lo_done, q + 2)
                            pe.wait_ge(up_lo_done, q + 2)
                        up(1 - s, j - 1)
                    down(q, s, j)

            pe.wait_ge(k_copied, 2 * (KC - 1))
            turn_inputs(0, 0, 0)
            pe.wait_ge(xct_lo_done, 1)
            pe.wait_ge(up_lo_done, 1)
            up(0, 0)
            up(0, 1)
            final_chunk, _ = all_chunks(pe, chunk_products)

            pe.wait_ge(kernel_in, 16)
            for t in range(G):
                last = nc.tensor.transpose(ps[:, t // 4, (t % 4) * P:(t % 4 + 1) * P], k_nat[:, t * P:(t + 1) * P], ident[:])
            last.then_inc(k_t_done, 1)
            pe.wait_ge(k_t_copied, 2)
            pe.wait_ge(fwd_in, 16)
            pe.wait_ge(y_copied, final_chunk + 1)
            halves = k_t.rearrange("p (c t) h -> p t c h", c=2)
            for m in range(M):
                for part_ in range(2):
                    for t in range(CT):
                        last = mm(ps[:, 4 + m, part_ * 2 * P:(part_ + 1) * 2 * P], fwd[:, t, part_, m * P:(m + 1) * P],
                                  halves[:, t], start=(t == 0), stop=(t == CT - 1))
                last.then_inc(khat_mm, 1)

            pe.wait_ge(khat_copied, M)
            for k in range(4):
                c, part_ = divmod(k, 2)
                for t in range(CT):
                    last = mm(ps[:, 4 + k], fwd[:, t, part_, ME * P:M * P], xn[:, c * CT + t],
                              start=(t == 0), stop=(t == CT - 1))
            last.then_inc(x_hat_done, 1)

            def logits1(g):
                pe.wait_ge(xt1_lo_done, g + 1)
                for b in range(B):
                    c = slice(b * P, (b + 1) * P)
                    o = ps[:, 6, (g * B + b) * GW:(g * B + b + 1) * GW]
                    w = slice(GATE1, GATE1 + GW)
                    last = three(o, xt1_hi[:, g, c], xt1_lo[:, g, c], w_hi[:, w], w_lo[:, w])
                last.then_inc(logits1_done, 1)

            def turn1(g):
                pe.wait_ge(xn1_done, g + 1)
                for b in range(B):
                    last = nc.tensor.transpose(ps[:, 4 + g % 2, b * P:(b + 1) * P], xn1[:, g % 2, b * P:(b + 1) * P], ident[:])
                last.then_inc(xt1_done, 1)

            def positions(g, tiles=range(M)):
                c, t = divmod(g, CT)
                if g >= 4:
                    pe.wait_ge(norm1_done, g - 3)
                for m in tiles:
                    for part_ in range(2):
                        last = mm(ps[:, g % 4], inv[:, m, part_, t * P:(t + 1) * P], z[:, m, c, part_],
                                  start=(m == 0 and part_ == 0), stop=(m == M - 1 and part_ == 1))
                if M - 1 in tiles:
                    last.then_inc(y_done, 1)

            pe.wait_ge(inv_in, 16)
            for m in range(M):
                pe.wait_ge(z_ready, m + 1)
                for g in range(4):
                    positions(g, range(m, m + 1))
            for i in range(G + 3):
                if 2 <= i < G + 2:
                    turn1(i - 2)
                if 4 <= i + 2 < G:
                    positions(i + 2)
                if i >= 3:
                    logits1(i - 3)

            def qkv(m):
                b, i = qkv_piece(m)
                if m >= 4:
                    pe.wait_ge(qkv_lo_done, m)
                src = qkv_src(m)
                cols = slice(b * P, (b + 1) * P)
                if i < 4:
                    w = slice(QKV + (i // 2) * P, QKV + (i // 2 + 1) * P)
                    gr = slice(4 * (i % 2), 4 * (i % 2) + 4)
                    last = three(src.rearrange("p (t j) -> p t j", t=4), w_hi[:, w], w_lo[:, w],
                                 xt1_hi[:, gr, cols], xt1_lo[:, gr, cols])
                else:
                    w = slice(QKV + 2 * P, QKV + 3 * P)
                    for t in range(4):
                        gr = 4 * (i - 4) + t
                        last = three(src[:, t], xt1_hi[:, gr, cols], xt1_lo[:, gr, cols], w_hi[:, w], w_lo[:, w])
                last.then_inc(qkv_mm, 1)

            def scores(n):
                b, jt = divmod(n, G)
                pe.wait_ge(qkv_lo_done, 4 + 6 * b if jt >= 4 or b == 0 else 3 + 6 * b)
                if n >= 2:
                    pe.wait_ge(exp1_done, n - 1)
                j = slice(jt * P, (jt + 1) * P)
                for a in range(2):
                    i = slice(a * C, (a + 1) * C)
                    last = three(ps[:, 2 * (n % 2) + a], k_hi[:, j], k_lo[:, j], q_hi[:, b % 2, i], q_lo[:, b % 2, i])
                last.then_inc(s_done, 1)

            def turn_probabilities(n):
                for a in range(2):
                    pe.wait_ge(prob_done[a], n + 1)
                    if n >= 1:
                        pe.wait_ge(pt_lo_done, 2 * n - 1 + a)
                    for t in range(4):
                        last = nc.tensor.transpose(ps[:, 4 + a, t * P:(t + 1) * P],
                                                   prob[:, n % 2, (4 * a + t) * P:(4 * a + t + 1) * P], ident[:])
                    last.then_inc(pt_done, 1)

            def attend(k, half):
                pe.wait_ge(pt_lo_done, 4 * k + 4)
                pe.wait_ge(qkv_lo_done, 4 + 6 * (2 * k // G) + 1 + half)
                if half == 0:
                    pe.wait_ge(pv_copied, k) if k else pe.wait_ge(gate_soft, 1)
                for t in range(4 * half, 4 * half + 4):
                    last = three(ps[:, 6, 0:2 * P], v_hi[:, t], v_lo[:, t], pt_hi[:, k % 2, t], pt_lo[:, k % 2, t],
                                 first=(t == 0), last=(t == G - 1))
                if half:
                    last.then_inc(pv_done, 1)

            for m in range(4):
                qkv(m)
            scores(0)
            scores(1)
            for n in range(B * G):
                if n + 2 < B * G:
                    scores(n + 2)
                turn_probabilities(n)
                if n == 4:
                    pe.wait_ge(gates1_done, 1)
                    pe.wait_ge(qkv_lo_done, 7)
                    flat = gates[:].rearrange("p t e -> p (t e)")
                    for a in range(2):
                        last = nc.tensor.transpose(ps[:, 7, a * P:(a + 1) * P], flat[:, a * P:(a + 1) * P], ident[:])
                    last.then_inc(gates1_turned, 1)
                    pe.wait_ge(gates1_copied, 1)
                if n % G == 1 and n >= G:
                    attend(n // 2 - 1, n % 2)
                if qkv_after(n) is not None:
                    qkv(qkv_after(n))
                if n >= 2 and n % G != 1:
                    attend(n // 2 - 1, n % 2)
            attend(B * G // 2 - 1, 0)
            attend(B * G // 2 - 1, 1)

            def up1(g, u):
                xh, xl = (t[:, bass.ds(g, 1), :].rearrange("p a w -> p (a w)") for t in (xt1_hi, xt1_lo))
                w = slice(u * P, (u + 1) * P)
                three(ps[:, u % 4], w_hi[:, w], w_lo[:, w], xh, xl).then_inc(up1_done, 1)

            def down1(g, u):
                e, j = divmod(u, J1)
                pe.wait_ge(hid1_lo_done, g * UN1 + u + 1)
                w = slice(E * HID1 + u * P, E * HID1 + (u + 1) * P)
                last = three(ps[:, 4 + e % 2], w_hi[:, w], w_lo[:, w], hid1_hi[:, u % 4], hid1_lo[:, u % 4],
                             first=(j == 0), last=(j == J1 - 1))
                if j == J1 - 1:
                    last.then_inc(expert1_done, 1)

            def turn_out(g):
                if g >= 2:
                    pe.wait_ge(added_done, g - 1)
                for b in range(B):
                    last = nc.tensor.transpose(ps[:, 6 + g % 2, b * P:(b + 1) * P], acc[:, g, b * P:(b + 1) * P], ident[:])
                last.then_inc(final_done, 1)

            def experts1(g, last):
                for u in range(UN1):
                    if u + 3 < UN1 or not last:
                        up1(g + (u + 3) // UN1, (u + 3) % UN1)
                    down1(g, u)
                    if last and u % J1 == 0 and u // J1 >= 1:
                        pe.wait_ge(join1_done, (u // J1) * E)
                        turn_out(u // J1 - 1)

            pe.wait_ge(w1_lo_done, len(pieces1))
            pe.wait_ge(exp1_done, B * G)
            pe.wait_ge(pv_copied, B * G // 2)
            for u in range(3):
                up1(0, u)
            with pe.Fori(0, G - 1) as g:
                experts1(g, False)
            experts1(G - 1, True)
            pe.wait_ge(join1_done, G * E)
            turn_out(G - 1)


def kernel(**inputs):
    from concourse import bacc
    from concourse.bass_utils import run_bass_kernel_spmd

    nc = bacc.Bacc("TRN2", target_bir_lowering=False, num_devices=1)
    arrays = layout({k: np.asarray(v) for k, v in inputs.items()})
    aps = {n: nc.dram_tensor(n, a.shape, F32, kind="ExternalInput").ap() for n, a in arrays.items()}
    out = nc.dram_tensor("out", (B, L, H), F32, kind="ExternalOutput").ap()
    program(nc, out=out, **aps)
    return run_bass_kernel_spmd(nc, [arrays], core_ids=[0]).results[0]["out"]


def layout(a):
    def by_state(p):
        return p.reshape(2, HH, N).transpose(0, 2, 1).reshape(P, HH)

    freq = np.concatenate([np.arange(0, C, 2), np.arange(1, C, 2)]) + 0.5
    angle = 2 * np.pi * np.outer(np.arange(C), freq) / (2 * C)
    dft = np.stack([np.cos(angle), -np.sin(angle)]).astype(np.float32)
    fwd = dft.reshape(2, CT, P, C).transpose(2, 1, 0, 3)
    inv = dft.transpose(0, 2, 1).reshape(2, M, P, C).transpose(2, 1, 0, 3)
    d = dict(
        x=a["L0_attn_x"],
        state_params=np.stack([by_state(a["L0_attn_" + n]) for n in ("log_A_real", "A_imag", "C_re", "C_im")], 1),
        log_dt=a["L0_attn_log_dt"], skip=a["L0_attn_D"], ln_w=a["L0_attn_ln_w"], ln_b=a["L0_attn_ln_b"],
        wg0=a["L0_ffn_Wg"].T,
        w0=np.concatenate([
            a["L0_ffn_W1"].transpose(0, 2, 1), a["L0_ffn_W2"].transpose(0, 2, 1),
            np.pad(a["L0_ffn_W3"].transpose(0, 2, 1), ((0, 0), (0, J0 * P - HID0), (0, 0)))
            .reshape(E, J0, P, P).transpose(0, 2, 1, 3).reshape(E, P, J0 * P)], 2),
        lag_row=np.concatenate([np.arange(LO), LO * np.arange(LO), E - np.arange(E)]).astype(np.float32),
        dft_fwd=fwd, dft_inv=inv,
        wqkv=np.stack([a["L1_attn_W_query"], a["L1_attn_W_key"], a["L1_attn_W_value"]], 1),
        wg1=np.pad(np.concatenate([a["L1_ffn_Wg"], a["L1_ffn_Wt"]], 1), ((0, 0), (0, GW - E - 1))),
        gate_bias=np.pad(np.concatenate([a["L1_ffn_bg"], a["L1_ffn_bt"]]), (0, GW - E - 1)),
        w1_1=a["L1_ffn_W1"],
        b1=a["L1_ffn_b1"].reshape(E * J1, P).T,
        w2_1=a["L1_ffn_W2"],
        b2=a["L1_ffn_b2"].T,
    )
    return {n: np.ascontiguousarray(v) for n, v in d.items()}
```
